# Optimizing a Trainium2 kernel written in Bass

```python
import numpy as np
import jax
import jax.numpy as jnp

def _softmax(x, axis=-1):
    return jax.nn.softmax(x, axis=axis)

def _gelu(x):
    return jax.nn.gelu(x, approximate=True)

def _silu(x):
    return jax.nn.silu(x)

def _sigmoid(x):
    return jax.nn.sigmoid(x)

def _layernorm(x, axis=-1, eps=1e-05):
    m = jnp.mean(x, axis=axis, keepdims=True)
    v = jnp.var(x, axis=axis, keepdims=True)
    return (x - m) / jnp.sqrt(v + eps)

def _scatter_add(tgt, idx, src, axis=0):
    return tgt.at[idx].add(src)

def _segment_sum(src, seg, n):
    return jax.ops.segment_sum(src, seg, n)
kernel_name = 'mk_adj_preln_d4_adj_r2_a3d23a'

def setup_inputs(seed: int=0):
    np.random.seed(seed)
    _w = jnp.asarray

    def _rec_inputs():
        import jax
        import jax.numpy as jnp
        _gk = jax.random.key(seed)
        x = -0.0005963 + 1.001 * jax.random.normal(jax.random.fold_in(_gk, 1), (1354, 256), jnp.float32)
        _w = (1.0 + jnp.arange(1354, dtype=jnp.float32)) ** (-0.5)
        _w = _w / _w.mean()
        _pij = jnp.clip(0.0014771 * _w[:, None] * _w[None, :], 0.0, 1.0)
        _a = jax.random.uniform(jax.random.fold_in(_gk, 2), (1354, 1354)) < _pij
        _af = _a.astype(jnp.float32)
        adj = _af
        return (x, adj)
    x, adj = _rec_inputs()

    def _L0_gnn_setup():
        import jax, jax.numpy as jnp
        import numpy as np
        N = 3072
        D_IN = 256
        D_OUT = 256
        DENSITY = 0.005
        key = jax.random.key(seed)
        ks = jax.random.split(key, 12)
        x = jax.random.normal(ks[0], (N, D_IN), dtype=jnp.float32)
        adj_a = (jax.random.uniform(ks[1], (N, N)) < DENSITY).astype(jnp.float32)
        adj_b = (jax.random.uniform(ks[2], (N, N)) < DENSITY).astype(jnp.float32)
        W_sa = jax.random.normal(ks[3], (D_IN, D_OUT), dtype=jnp.float32) * (1.414 / np.sqrt(D_IN + D_OUT))
        a_sa = jax.random.normal(ks[4], (1, 2 * D_OUT), dtype=jnp.float32) * (1.414 / np.sqrt(1 + 2 * D_OUT))
        stdv = 1.0 / np.sqrt(D_OUT)
        W_gcnb = jax.random.uniform(ks[5], (D_IN, D_OUT), minval=-stdv, maxval=stdv, dtype=jnp.float32)
        b_gcnb = jax.random.uniform(ks[6], (D_OUT,), minval=-stdv, maxval=stdv, dtype=jnp.float32)
        s = 1.0 / np.sqrt(2 * D_IN)
        Wa = jax.random.uniform(ks[7], (1, 2 * D_IN), minval=-s, maxval=s, dtype=jnp.float32)
        ba = jax.random.uniform(ks[8], (1,), minval=-s, maxval=s, dtype=jnp.float32)
        Wb = jax.random.uniform(ks[9], (1, 2 * D_IN), minval=-s, maxval=s, dtype=jnp.float32)
        bb = jax.random.uniform(ks[10], (1,), minval=-s, maxval=s, dtype=jnp.float32)
        return {'x': x, 'adj_a': adj_a, 'adj_b': adj_b, 'W_sa': W_sa, 'a_sa': a_sa, 'W_gcnb': W_gcnb, 'b_gcnb': b_gcnb, 'Wa': Wa, 'ba': ba, 'Wb': Wb, 'bb': bb}
    _L0_gnn_all = _L0_gnn_setup()
    _L0_gnn_in = {k: v for k, v in _L0_gnn_all.items() if k in ('W_sa', 'a_sa', 'W_gcnb', 'b_gcnb', 'Wa', 'ba', 'Wb', 'bb')}
    del _L0_gnn_all

    def _L1_gnn_setup():
        import jax, jax.numpy as jnp
        import numpy as np
        N, F, H = (1536, 256, 4)
        D = F // H
        ALPHA = 0.5
        EPS = 1e-06

        def _batchnorm(x, gamma, beta):
            m = jnp.mean(x, axis=0)
            v = jnp.var(x, axis=0)
            return (x - m) * jax.lax.rsqrt(v + EPS) * gamma + beta

        def _masked_softmax(scores, mask):
            s = jnp.where(mask, scores, -jnp.inf)
            att = jax.nn.softmax(s, axis=-1)
            return jnp.where(mask, att, 0.0)

        def _mlp_block(x, Wm, bm, g, b):
            h = jax.nn.elu(x @ Wm.T + bm) + x
            return _batchnorm(h, g, b)
        key = jax.random.key(seed)
        ks = jax.random.split(key, 12)
        X = jax.random.normal(ks[0], (N, F), dtype=jnp.float32)
        eye = jnp.eye(N, dtype=jnp.float32)
        local = (jax.random.uniform(ks[1], (N, N)) < 32.0 / N).astype(jnp.float32)
        local = jnp.clip(local + eye, 0.0, 1.0)
        longr = (jax.random.uniform(ks[2], (N, N)) < 16.0 / N).astype(jnp.float32)
        longr = jnp.clip(longr + eye, 0.0, 1.0)
        W = jax.random.normal(ks[3], (H, D, D), dtype=jnp.float32) * 0.1
        V = jax.random.normal(ks[4], (H, 2, D, 1), dtype=jnp.float32) * 0.1
        return {'X': X, 'local_pattern': local, 'long_range_pattern': longr, 'W': W, 'V': V, 'enc_bn_gamma': jnp.ones((F,), jnp.float32), 'enc_bn_beta': jnp.zeros((F,), jnp.float32), 'enc_mlp_W': jax.random.normal(ks[5], (F, F), dtype=jnp.float32) * 0.02, 'enc_mlp_b': jnp.zeros((F,), jnp.float32), 'enc_mlp_bn_gamma': jnp.ones((F,), jnp.float32), 'enc_mlp_bn_beta': jnp.zeros((F,), jnp.float32), 'dec_mlp_W': jax.random.normal(ks[6], (F, F), dtype=jnp.float32) * 0.02, 'dec_mlp_b': jnp.zeros((F,), jnp.float32), 'dec_mlp_bn_gamma': jnp.ones((F,), jnp.float32), 'dec_mlp_bn_beta': jnp.zeros((F,), jnp.float32)}
    _L1_gnn_all = _L1_gnn_setup()
    _L1_gnn_in = {k: v for k, v in _L1_gnn_all.items() if k in ('W', 'V', 'enc_bn_gamma', 'enc_bn_beta', 'enc_mlp_W', 'enc_mlp_b', 'enc_mlp_bn_gamma', 'enc_mlp_bn_beta', 'dec_mlp_W', 'dec_mlp_b', 'dec_mlp_bn_gamma', 'dec_mlp_bn_beta')}
    del _L1_gnn_all

    def _L2_gnn_setup():
        import jax, jax.numpy as jnp
        import numpy as np
        N = 8192
        D_IN = 256
        D_OUT = 256
        AVG_DEG = 32.0
        key = jax.random.key(seed)
        k1, k2, k3, k4 = jax.random.split(key, 4)
        p = AVG_DEG / N
        adjacency = (jax.random.uniform(k1, (N, N)) < p).astype(jnp.float32)
        adjacency = jnp.maximum(adjacency, adjacency.T)
        node_degree = jnp.sum(adjacency, axis=1, keepdims=True) + 1.0
        x = jax.random.normal(k2, (N, D_IN), dtype=jnp.float32)
        W = jax.random.normal(k3, (D_IN, D_OUT), dtype=jnp.float32) * (1.0 / np.sqrt(D_IN))
        b = jax.random.normal(k4, (D_OUT,), dtype=jnp.float32) * 0.01
        return {'x': x, 'adjacency': adjacency, 'node_degree': node_degree, 'W': W, 'b': b}
    _L2_gnn_all = _L2_gnn_setup()
    _L2_gnn_in = {k: v for k, v in _L2_gnn_all.items() if k in ('W', 'b')}
    del _L2_gnn_all

    def _L3_gnn_setup():
        import jax, jax.numpy as jnp
        import numpy as np
        N = 4096
        DIN = 256
        DOUT = 256
        TAU = 1.0
        EPS = 1e-08
        NORM_EPS = 1e-08
        key = jax.random.key(seed)
        k1, k2, k3 = jax.random.split(key, 3)
        x = jax.random.normal(k1, (N, DIN), dtype=jnp.float32)
        adj = jax.random.uniform(k2, (N, N), dtype=jnp.float32)
        limit = float(np.sqrt(6.0 / (DIN + DOUT)))
        weight = jax.random.uniform(k3, (DIN, DOUT), dtype=jnp.float32, minval=-limit, maxval=limit)
        bias = jnp.zeros((DOUT,), dtype=jnp.float32)
        return {'x': x, 'adj': adj, 'weight': weight, 'bias': bias}
    _L3_gnn_all = _L3_gnn_setup()
    _L3_gnn_in = {k: v for k, v in _L3_gnn_all.items() if k in ('weight', 'bias')}
    del _L3_gnn_all
    return {'x': x, 'adj': adj, 'L0_gnn_W_sa': _L0_gnn_in['W_sa'], 'L0_gnn_a_sa': _L0_gnn_in['a_sa'], 'L0_gnn_W_gcnb': _L0_gnn_in['W_gcnb'], 'L0_gnn_b_gcnb': _L0_gnn_in['b_gcnb'], 'L0_gnn_Wa': _L0_gnn_in['Wa'], 'L0_gnn_ba': _L0_gnn_in['ba'], 'L0_gnn_Wb': _L0_gnn_in['Wb'], 'L0_gnn_bb': _L0_gnn_in['bb'], 'L1_gnn_W': _L1_gnn_in['W'], 'L1_gnn_V': _L1_gnn_in['V'], 'L1_gnn_enc_bn_gamma': _L1_gnn_in['enc_bn_gamma'], 'L1_gnn_enc_bn_beta': _L1_gnn_in['enc_bn_beta'], 'L1_gnn_enc_mlp_W': _L1_gnn_in['enc_mlp_W'], 'L1_gnn_enc_mlp_b': _L1_gnn_in['enc_mlp_b'], 'L1_gnn_enc_mlp_bn_gamma': _L1_gnn_in['enc_mlp_bn_gamma'], 'L1_gnn_enc_mlp_bn_beta': _L1_gnn_in['enc_mlp_bn_beta'], 'L1_gnn_dec_mlp_W': _L1_gnn_in['dec_mlp_W'], 'L1_gnn_dec_mlp_b': _L1_gnn_in['dec_mlp_b'], 'L1_gnn_dec_mlp_bn_gamma': _L1_gnn_in['dec_mlp_bn_gamma'], 'L1_gnn_dec_mlp_bn_beta': _L1_gnn_in['dec_mlp_bn_beta'], 'L2_gnn_W': _L2_gnn_in['W'], 'L2_gnn_b': _L2_gnn_in['b'], 'L3_gnn_weight': _L3_gnn_in['weight'], 'L3_gnn_bias': _L3_gnn_in['bias']}

def reference(x, adj, L0_gnn_W_sa, L0_gnn_a_sa, L0_gnn_W_gcnb, L0_gnn_b_gcnb, L0_gnn_Wa, L0_gnn_ba, L0_gnn_Wb, L0_gnn_bb, L1_gnn_W, L1_gnn_V, L1_gnn_enc_bn_gamma, L1_gnn_enc_bn_beta, L1_gnn_enc_mlp_W, L1_gnn_enc_mlp_b, L1_gnn_enc_mlp_bn_gamma, L1_gnn_enc_mlp_bn_beta, L1_gnn_dec_mlp_W, L1_gnn_dec_mlp_b, L1_gnn_dec_mlp_bn_gamma, L1_gnn_dec_mlp_bn_beta, L2_gnn_W, L2_gnn_b, L3_gnn_weight, L3_gnn_bias):
    import jax
    import jax.numpy as jnp

    def _L0_gnn_ref(x, adj_a, adj_b, W_sa, a_sa, W_gcnb, b_gcnb, Wa, ba, Wb, bb):
        import jax, jax.numpy as jnp
        import numpy as np
        N = 3072
        D_IN = 256
        D_OUT = 256
        DENSITY = 0.005
        type_sum_a = adj_a @ x
        type_sum_b = adj_b @ x
        attn_a = jax.nn.sigmoid(jnp.concatenate([type_sum_a, x], axis=1) @ Wa.T + ba)
        attn_b = jax.nn.sigmoid(jnp.concatenate([type_sum_b, x], axis=1) @ Wb.T + bb)
        h = x @ W_sa
        Hd = h.shape[1]
        s_left = h @ a_sa[0, :Hd]
        s_right = h @ a_sa[0, Hd:]
        scores = s_left[:, None] + s_right[None, :]
        e = jnp.where(adj_a != 0, jnp.exp(-jax.nn.leaky_relu(scores, 0.01)), 0.0)
        attn = e / (jnp.sum(e, axis=1, keepdims=True) + 1e-05)
        x_a = attn @ h
        x_b = adj_b @ (x @ W_gcnb) + b_gcnb
        return jax.nn.sigmoid(attn_a * x_a + attn_b * x_b)

    def _L1_gnn_ref(X, local_pattern, long_range_pattern, W, V, enc_bn_gamma, enc_bn_beta, enc_mlp_W, enc_mlp_b, enc_mlp_bn_gamma, enc_mlp_bn_beta, dec_mlp_W, dec_mlp_b, dec_mlp_bn_gamma, dec_mlp_bn_beta):
        import jax, jax.numpy as jnp
        import numpy as np
        N, F, H = (1536, 256, 4)
        D = F // H
        ALPHA = 0.5
        EPS = 1e-06

        def _batchnorm(x, gamma, beta):
            m = jnp.mean(x, axis=0)
            v = jnp.var(x, axis=0)
            return (x - m) * jax.lax.rsqrt(v + EPS) * gamma + beta

        def _masked_softmax(scores, mask):
            s = jnp.where(mask, scores, -jnp.inf)
            att = jax.nn.softmax(s, axis=-1)
            return jnp.where(mask, att, 0.0)

        def _mlp_block(x, Wm, bm, g, b):
            h = jax.nn.elu(x @ Wm.T + bm) + x
            return _batchnorm(h, g, b)
        n = X.shape[0]
        Xh = X.reshape(n, H, D).transpose(1, 0, 2)
        Xw = jnp.einsum('hnd,hde->hne', Xh, W)
        f1 = jnp.einsum('hnd,hd->hn', Xw, V[:, 0, :, 0])
        f2 = jnp.einsum('hnd,hd->hn', Xw, V[:, 1, :, 0])
        sig = jax.nn.sigmoid(f1[:, :, None] + f2[:, None, :])
        lmask = (local_pattern != 0)[None]
        gmask = (long_range_pattern != 0)[None]
        local_att = _masked_softmax(local_pattern[None] * sig, lmask)
        long_att = _masked_softmax(long_range_pattern[None] * sig, gmask)
        att = ALPHA * long_att + (1.0 - ALPHA) * local_att
        Xa = jnp.einsum('hij,hjd->hid', att, Xw)
        Xc = Xa.transpose(1, 0, 2).reshape(n, F)
        Xn = _batchnorm(Xc, enc_bn_gamma, enc_bn_beta)
        emb = _mlp_block(Xn, enc_mlp_W, enc_mlp_b, enc_mlp_bn_gamma, enc_mlp_bn_beta)
        Yh = emb.reshape(n, H, D).transpose(1, 0, 2)
        Y = jnp.einsum('hij,hjd->hid', att, Yh)
        Y = jnp.einsum('hnd,hed->hne', Y, W)
        Yc = Y.transpose(1, 0, 2).reshape(n, F)
        Yc = jax.nn.elu(Yc)
        out = _mlp_block(Yc, dec_mlp_W, dec_mlp_b, dec_mlp_bn_gamma, dec_mlp_bn_beta)
        return out

    def _L2_gnn_ref(x, adjacency, node_degree, W, b):
        import jax, jax.numpy as jnp
        import numpy as np
        N = 8192
        D_IN = 256
        D_OUT = 256
        AVG_DEG = 32.0
        n = adjacency.shape[0]
        a_hat = adjacency + jnp.eye(n, dtype=adjacency.dtype)
        dinv = jax.lax.rsqrt(node_degree)
        a_norm = dinv * a_hat * dinv
        pooled = a_norm @ x + x
        return jax.nn.relu(pooled @ W + b)

    def _L3_gnn_ref(x, adj, weight, bias):
        import jax, jax.numpy as jnp
        import numpy as np
        N = 4096
        DIN = 256
        DOUT = 256
        TAU = 1.0
        EPS = 1e-08
        NORM_EPS = 1e-08
        h = x @ weight
        norm = jnp.linalg.norm(h, axis=1, keepdims=True)
        h_norm = h / jnp.maximum(norm, NORM_EPS)
        sim = h_norm @ h_norm.T
        attn_logits = sim / TAU + jnp.log(adj + EPS)
        attn = jax.nn.softmax(attn_logits, axis=1)
        out = attn @ h + bias
        return out
    deg = jnp.maximum((adj != 0).astype(jnp.float32).sum(-1), 1.0)
    h = jnp.maximum(_layernorm(x, axis=-1), 0.0)
    x = x + _L0_gnn_ref(h, adj, adj, L0_gnn_W_sa, L0_gnn_a_sa, L0_gnn_W_gcnb, L0_gnn_b_gcnb, L0_gnn_Wa, L0_gnn_ba, L0_gnn_Wb, L0_gnn_bb)
    h = jnp.maximum(_layernorm(x, axis=-1), 0.0)
    x = x + _L1_gnn_ref(h, adj, adj, L1_gnn_W, L1_gnn_V, L1_gnn_enc_bn_gamma, L1_gnn_enc_bn_beta, L1_gnn_enc_mlp_W, L1_gnn_enc_mlp_b, L1_gnn_enc_mlp_bn_gamma, L1_gnn_enc_mlp_bn_beta, L1_gnn_dec_mlp_W, L1_gnn_dec_mlp_b, L1_gnn_dec_mlp_bn_gamma, L1_gnn_dec_mlp_bn_beta)
    h = jnp.maximum(_layernorm(x, axis=-1), 0.0)
    x = x + _L2_gnn_ref(h, adj, deg[..., None], L2_gnn_W, L2_gnn_b)
    h = jnp.maximum(_layernorm(x, axis=-1), 0.0)
    x = x + _L3_gnn_ref(h, adj, L3_gnn_weight, L3_gnn_bias)
    return x

_drawn_inputs = setup_inputs


def setup_inputs(seed=0):
    import zlib

    import numpy as np

    out = dict(_drawn_inputs(seed))
    spreads = {'L1_gnn_enc_bn_gamma': (1.0, 0.2),
     'L1_gnn_enc_bn_beta': (0.0, 2.0),
     'L1_gnn_enc_mlp_b': (0.0, 0.8),
     'L1_gnn_enc_mlp_bn_gamma': (1.0, 0.2),
     'L1_gnn_enc_mlp_bn_beta': (0.0, 0.1),
     'L1_gnn_dec_mlp_b': (0.0, 0.8),
     'L1_gnn_dec_mlp_bn_gamma': (1.0, 0.2),
     'L1_gnn_dec_mlp_bn_beta': (0.0, 0.1),
     'L3_gnn_bias': (0.0, 0.1)}
    factors = {'L0_gnn_a_sa': 32.68, 'L0_gnn_b_gcnb': 8.0, 'L0_gnn_Wa': 4.963, 'L2_gnn_b': 8.0}
    for name, (base, spread) in spreads.items():
        noise = np.random.default_rng([zlib.crc32(name.encode()), seed]).standard_normal(out[name].shape)
        drawn = base * np.exp(spread * noise) if base else spread * noise
        out[name] = jnp.asarray(drawn.astype(out[name].dtype))
    for name, factor in factors.items():
        out[name] = (out[name] * factor).astype(out[name].dtype)
    return out
```

```python
from contextlib import ExitStack

import concourse.bass as bass
from concourse import mybir

F32 = mybir.dt.float32
F16 = mybir.dt.float16
ALU = mybir.AluOpType
ACT = mybir.ActivationFunctionType
AX_X = mybir.AxisListType.X
ds = bass.ds

P = 128
LN_EPS = 1e-5
BN_EPS = 1e-6
L0_EPS = 1e-5
ADJ_EPS = 1e-8
NORM_EPS = 1e-8


def gnn_stack(nc, x_in, adj_t, weights, blocks, cols, rows, out):
    N = out.shape[0]
    D = out.shape[1]
    T = -(-N // P)
    NP = T * P
    W = adj_t.shape[1]
    NC = 3
    C = W // NC
    LAST = N - (T - 1) * P
    F = D // P
    H = 4
    DH = D // H
    RING = 4
    assert F == 2 and C * NC == W and C <= 512 and W >= N
    (W_SA, W_SA_T, W_GCNB, MLP_E, MLP_D, W_L2, W_L3) = range(7)
    (W_BD, W_BD_T) = range(2)
    (E_G, E_B, EM_B, EM_G, EM_BB, DM_B, DM_G, DM_BB) = range(8)
    R_GCNB, R_L2B, R_L3B, R_BA = 0, D, 2 * D, 3 * D
    NR = 3 * D + 2

    with ExitStack() as ctx:
        def sb(name, width, dt=F32):
            return ctx.enter_context(nc.sbuf_tensor("sb_" + name, [P, width], dt))

        def sem(name):
            return ctx.enter_context(nc.semaphore(name))

        at = sb("adj_t", T * W, F16)
        x = sb("x", T * D)
        h = sb("h", T * D)
        h_hi = sb("h_hi", T * D, F16)
        h_lo = sb("h_lo", T * D, F16)
        ht = sb("ht", F * NP)
        ga = sb("ga", F * NP)
        gb = sb("gb", F * NP)
        rinv = sb("rinv", F * W)
        frow = sb("frow", H * W)
        tt = sb("tt", 3 * W)
        ring = sb("ring", RING * W)
        s_acc = sb("s_acc", NP)
        d_acc = sb("d_acc", NP)
        vs = sb("vs", 2 * 2 * P * F)
        wt = sb("wt", 7 * F * D)
        wbd = sb("wbd", 2 * F * P)
        colv = sb("colv", F * 8)
        rowv = sb("rowv", NR)
        smallw = sb("smallw", F * (2 + 2 + 8 + 3))
        gw = smallw[:, 0:F * 2]
        a2 = smallw[:, F * 2:F * 4]
        vb = smallw[:, F * 4:F * 12]
        r3 = smallw[:, F * 12:F * 15]
        c0 = sb("c0", F * 2)
        cb = sb("cb", H * P)
        c1 = sb("c1", F * 8)
        f2 = sb("f2", H * T)
        ident = sb("ident", P)
        ones = sb("ones", P)
        stats = sb("stats", T * 6)
        lnt = sb("lnt", 6 * T)
        rstd = sb("rstd", T)
        nmr = sb("nmr", T)
        mhalf = sb("mhalf", T)
        one = sb("one", 4)
        epsv = sb("epsv", T)
        nodev = sb("nodev", 16 * T)
        bnst = sb("bnst", F * NC * 6)
        bnag = sb("bnag", F * 2)
        bnv = sb("bnv", F * 4)
        e_t = sb("e_t", 2 * D)
        e_q = sb("e_q", 2 * D)
        ps = ctx.enter_context(nc.psum_tensor("ps", [P, 8, 512], F32))

        gab, gates, attn, rs, ca, dinv, dmax, dinv1, srt, sr99, n2, nsum = (
            nodev[:, 0:2 * T], nodev[:, 2 * T:4 * T], nodev[:, 4 * T:6 * T], nodev[:, 6 * T:7 * T],
            nodev[:, 7 * T:8 * T], nodev[:, 8 * T:9 * T], nodev[:, 9 * T:10 * T], nodev[:, 10 * T:11 * T],
            nodev[:, 11 * T:12 * T], nodev[:, 12 * T:13 * T], nodev[:, 13 * T:14 * T], nodev[:, 14 * T:15 * T])

        psf = ps[:, :, :].rearrange("p b n -> p (b n)")
        TR = -(-T // 2)
        NCONST = 8

        def fm(a, width=NP):
            return a[:, :].rearrange("p (f n) -> p f n", f=F)

        def chunks(a, f=0, width=NP):
            return a[:, f * width:f * width + W].rearrange("p (c n) -> p c n", c=NC)

        adj_ld = [sem(f"adj_loaded{s}") for s in range(RING)]
        adj_cast = sem("adj_cast")
        x_loaded = sem("x_loaded")
        w_loaded = sem("w_loaded")
        w0_loaded = sem("w0_loaded")
        consts = sem("consts_ready")
        stats_done = sem("stats_done")
        x_done = sem("x_done")
        lnvar = sem("ln_var")
        lnpow = sem("ln_pow")
        h_done = sem("h_done")
        h16_done = sem("h16_done")
        tr_done = sem("transposed")
        tr_copied = sem("transposes_copied")
        dve_own = sem("dve_own")
        act_own = sem("act_own")
        pool_own = sem("pool_own")
        c0_mm, c0_copied, r3_mm, r3_copied, srow_mm, srow_copied = (
            sem("c0_mm"), sem("c0_copied"), sem("r3_mm"), sem("r3_copied"), sem("srow_mm"), sem("srow_copied"))
        cb_ready = sem("cb_ready")
        agg_done, agg_copied = sem("aggregated"), sem("aggregate_copied")
        tile_arg, tile_tanh, tile_exp, tile_masked, tile_used, tile_summed = (
            sem("tile_arg"), sem("tile_tanh"), sem("tile_exp"), sem("tile_masked"), sem("tile_used"), sem("tile_summed"))
        vs_ready = sem("values_ready")
        gate_mm, gate_sum, gate_tanh, gate_attn, dinv_ready = (
            sem("gate_mm"), sem("gate_sum"), sem("gate_tanh"), sem("gate_attn"), sem("dinv_ready"))
        np_mm, np_scaled, np_mixed, np_act, np_done = (
            sem("node_product"), sem("node_scaled"), sem("node_mixed"), sem("node_act"), sem("node_done"))
        f_mm, f_even_copied, f_odd_copied = sem("f_mm"), sem("f_even_copied"), sem("f_odd_copied")
        head_copied = sem("head_copied")
        norm_ready, proj_mm, bn_var, bn_pow, bn_cols, aff_done, mlp_mm, mlp_min, mlp_act, mlp_sum = (
            sem("normalised"), sem("proj_mm"), sem("bn_var"), sem("bn_pow"), sem("bn_cols"), sem("affine_done"),
            sem("mlp_mm"), sem("mlp_min"), sem("mlp_act"), sem("mlp_sum"))
        sim_mm, sim_exp, nrm_done, nrm_pow, hn_done, hn_copied = (
            sem("sim_mm"), sem("sim_exp"), sem("norm_done"), sem("norm_pow"), sem("hn_done"), sem("hn_copied"))
        out_stored = sem("out_stored")
        f2_mm, f2_copied, c1_mm, dec_ready, hn_mm, hi_done, sq_done, bias_done, s3_mm = (
            sem("f2_mm"), sem("f2_copied"), sem("c1_mm"), sem("dec_ready"), sem("hn_mm"), sem("hi_done"),
            sem("sq_done"), sem("bias_done"), sem("s3_mm"))
        NW0, NWR = 7, 8

        N0, NE, ND, N3 = T, H * T, H * T, T
        B0, BE, BD, B3 = 0, N0, N0 + NE, N0 + NE + ND

        block = ctx.enter_context(nc.Block())

        @block.sync
        def _(sp):
            sp.dma_start(x[:, :].rearrange("p (t d) -> p t d", t=T),
                         x_in.rearrange("(t p) d -> p t d", p=P)).then_inc(x_loaded, 16)

            def load_w(dst, src, s):
                sp.dma_start(dst.rearrange("p (f n) -> p f n", f=F),
                             src.rearrange("(f p) n -> p f n", p=P)).then_inc(s, 16)

            load_w(a2, cols["a2"], w0_loaded)
            load_w(gw, cols["gw"], w0_loaded)
            sp.dma_start(r3.rearrange("p (f n) -> p f n", f=F)[:, :, 0:2],
                         cols["wr"].rearrange("(f p) n -> p f n", p=P)).then_inc(w0_loaded, 16)
            for i in (W_SA, W_SA_T, W_GCNB):
                load_w(wt[:, i * F * D:(i + 1) * F * D], weights[i], w0_loaded)
            sp.dma_start(rowv[:, :], rows.partition_broadcast(P)).then_inc(w0_loaded, 16)
            for j in range(RING):
                sp.dma_start(ring[:, j * W:(j + 1) * W], adj_t[j * P:(j + 1) * P, :]).then_inc(adj_ld[j], 16)
            for j in range(RING, T):
                sp.wait_ge(adj_cast, j - RING + 1)
                sp.dma_start(ring[:, (j % RING) * W:(j % RING + 1) * W],
                             adj_t[j * P:(j + 1) * P, :]).then_inc(adj_ld[j % RING], 16)
            for i in (MLP_E, MLP_D, W_L2, W_L3):
                load_w(wt[:, i * F * D:(i + 1) * F * D], weights[i], w_loaded)
            for i in range(2):
                load_w(wbd[:, i * F * P:(i + 1) * F * P], blocks[i], w_loaded)
            load_w(vb, cols["vb"], w_loaded)
            load_w(colv[:, :], cols["colv"], w_loaded)
            sp.wait_ge(np_done, 3 * T)
            sp.dma_start(out[0:(T - 1) * P, :].rearrange("(t p) d -> p t d", p=P),
                         x[:, 0:(T - 1) * D].rearrange("p (t d) -> p t d", d=D)).then_inc(out_stored, 16)
            sp.dma_start(out[(T - 1) * P:N, :], x[0:LAST, (T - 1) * D:T * D]).then_inc(out_stored, 16)
            sp.wait_ge(out_stored, 32)


        @block.gpsimd
        def _(pool):
            own = [0]

            def link(ins):
                own[0] += 1
                ins.then_inc(pool_own, 1)
                pool.wait_ge(pool_own, own[0])

            link(pool.memset(ident[:, :], 0.0))
            link(pool.memset(epsv[:, :], ADJ_EPS))
            pool.affine_select(out=ident[:, :], in_=ident[:, :], compare_op=ALU.not_equal, fill=1.0, base=0,
                               pattern=[[-1, P]], channel_multiplier=1).then_inc(consts, 1)
            pool.affine_select(out=epsv[:, T - 1:T], in_=epsv[:, T - 1:T], compare_op=ALU.is_ge, fill=0.0,
                               base=LAST - 1, pattern=[[0, 1]], channel_multiplier=-1).then_inc(consts, 1)
            pool.memset(ones[:, :], 1.0).then_inc(consts, 1)
            pool.memset(mhalf[:, :], -0.5).then_inc(consts, 1)
            pool.memset(s_acc[:, :], 0.0).then_inc(consts, 1)
            pool.memset(d_acc[:, :], 0.0).then_inc(consts, 1)
            for a in (ga, gb):
                pool.memset(fm(a)[:, :, W:NP], 0.0).then_inc(consts, 1)
            pool.wait_ge(consts, NCONST)

            def norm_power(layer):
                pool.wait_ge(lnvar, layer + 1)
                link(pool.tensor_tensor(rstd[:, :], lnt[:, 4 * T:5 * T], mhalf[:, :], ALU.pow))
                pool.tensor_tensor(nmr[:, :], lnt[:, 5 * T:6 * T], rstd[:, :], ALU.mult).then_inc(lnpow, 1)

            def batch_power(k):
                pool.wait_ge(bn_var, k + 1)
                pool.tensor_tensor(bnv[:, 0:F], bnv[:, 0:F], mhalf[:, 0:F], ALU.pow).then_inc(bn_pow, 1)

            def node_values(j, base):
                pool.wait_ge(tile_used, base + j - 1)
                pool.tensor_copy(vs[:, ds((j % 2) * D, D)], h[:, ds(j * D, D)]).then_inc(vs_ready, 1)

            def sum_weights(j, base, before):
                pool.wait_ge(tile_masked, base + j + 1)
                pool.wait_ge(tile_summed, before + j)
                pool.tensor_tensor(s_acc[:, 0:W], s_acc[:, 0:W], ring[:, ds(((base + j) % RING) * W, W)],
                                   ALU.add).then_inc(tile_summed, 1)

            norm_power(0)
            with pool.Fori(0, T) as j:
                pool.wait_ge(adj_cast, j + 1)
                pool.tensor_tensor(d_acc[:, 0:W], d_acc[:, 0:W], at[:, ds(j * W, W)],
                                   ALU.add).then_inc(tile_summed, 1)
                pool.wait_ge(tile_summed, j + 1)
            pool.wait_ge(h_done, T)
            for j in range(2):
                pool.tensor_copy(vs[:, j * D:(j + 1) * D], h[:, j * D:(j + 1) * D]).then_inc(vs_ready, 1)
                sum_weights(j, B0, T)
            with pool.Fori(2, T) as j:
                node_values(j, B0)
                sum_weights(j, B0, T)
            pool.wait_ge(gate_mm, 1)
            pool.memset(s_acc[:, 0:W], 0.0).then_inc(tile_summed, 1)

            norm_power(1)
            pool.wait_ge(tile_used, B0 + N0)
            link(pool.memset(vs[:, :], 1.0))
            pool.wait_ge(h_done, 2 * T)
            for hd in range(H):
                with pool.Fori(0, T) as j:
                    pool.wait_ge(tile_used, BE + hd * T + j - 1)
                    pool.tensor_copy(vs[:, ds(((hd * T + j) % 2) * P + (hd % 2) * (2 * P + DH), DH)],
                                     h[:, ds(j * D + hd * DH, DH)]).then_inc(vs_ready, 1)
            batch_power(0)
            batch_power(1)
            pool.wait_ge(tr_copied, 3 * TR)
            pool.wait_ge(tile_used, BE + NE)
            for pr in range(2):
                with pool.Fori(0, T) as j:
                    pool.wait_ge(tile_used, BD + 2 * (pr * T + j - 1))
                    pool.tensor_copy(vs[:, ds(((pr * T + j) % 2) * P, P)],
                                     h[:, ds(j * D + pr * P, P)]).then_inc(vs_ready, 1)
            batch_power(2)
            norm_power(2)
            norm_power(3)
            pool.wait_ge(nrm_done, 1)
            pool.tensor_tensor(nsum, n2, mhalf[:, :], ALU.pow).then_inc(nrm_pow, 1)
            pool.wait_ge(hn_copied, T)
            pool.wait_ge(tile_used, B3)
            with pool.Fori(0, T) as j:
                node_values(j, B3)
                sum_weights(j, B3, 2 * T + 1)

        @block.scalar
        def _(act):
            act.preload_act_table(ACT.Exp)
            act.wait_ge(consts, NCONST)

            def norm_apply(layer):
                act.wait_ge(lnpow, layer + 1)
                with act.Fori(0, T) as t:
                    act.activation(h[:, ds(t * D, D)], x[:, ds(t * D, D)], ACT.Relu, bias=nmr[:, ds(t, 1)],
                                   scale=rstd[:, ds(t, 1)]).then_inc(h_done, 1)

            def copy_aggregate(done, count, dst):
                act.wait_ge(done, count)
                act.activation(chunks(dst), ps[:, 0:NC, 0:C], ACT.Copy).then_inc(agg_copied, 1)

            norm_apply(0)
            act.wait_ge(srow_mm, 1)
            act.activation(chunks(frow, 0, W), ps[:, 2:2 + NC, 0:C], ACT.Copy).then_inc(srow_copied, 1)
            act.wait_ge(r3_copied, 4)

            def score_exp(j):
                act.wait_ge(tile_arg, j + 1)
                act.wait_ge(r3_copied, 4)
                act.activation(ring[:, ds((j % RING) * W, W)], tt[:, ds((j % 2) * W, W)], ACT.Exp,
                               bias=srt[:, ds(j, 1)], scale=-1.0).then_inc(tile_exp, 1)

            with act.Fori(0, RING) as j:
                score_exp(j)
            copy_aggregate(agg_done, 1, ga)
            with act.Fori(RING, T) as j:
                act.wait_ge(tile_used, j - RING + 1)
                act.wait_ge(tile_summed, T + j - RING + 1)
                score_exp(j)
            copy_aggregate(tile_used, B0 + T, gb)
            act.wait_ge(gate_sum, 1)
            act.activation(gates, gates, ACT.Tanh, scale=0.5).then_inc(gate_tanh, 1)
            act.wait_ge(gate_attn, 1)

            def l0_scale(t):
                act.wait_ge(np_mm, t + 1)
                act.wait_ge(gate_attn, 1)
                act.activation(e_q[:, ds((t % 2) * D, D)], psf[:, ds((t % 2) * 1024, D)], ACT.Copy,
                               scale=attn[:, ds(t + T, 1)]).then_inc(np_scaled, 1)

            def l0_tanh(t):
                act.wait_ge(np_mixed, t + 1)
                act.wait_ge(gate_attn, 1)
                act.activation(e_t[:, ds((t % 2) * D, D)], e_t[:, ds((t % 2) * D, D)], ACT.Tanh,
                               scale=0.5).then_inc(np_act, 1)

            l0_scale(0)
            with act.Fori(0, T - 1) as t:
                l0_scale(t + 1)
                l0_tanh(t)
            l0_tanh(T - 1)

            norm_apply(1)
            for hd in (0, 2):
                act.wait_ge(f_mm, hd + 1)
                act.activation(chunks(frow, hd, W), ps[:, 2:2 + NC, 0:C], ACT.Copy).then_inc(f_even_copied, 1)
                if hd == 0:
                    act.wait_ge(f2_copied, 1)

            def tile_pass(base, number, head_of, node_of):
                def tanh(m):
                    act.activation(tt[:, ds((m % 3) * W, W)], frow[:, ds(head_of(m) * W, W)], ACT.Tanh,
                                   bias=f2[:, ds(head_of(m) * T + node_of(m), 1)],
                                   scale=0.5).then_inc(tile_tanh, 1)

                def exp(m):
                    act.wait_ge(tile_tanh, base - BE + m + 1)
                    act.wait_ge(tile_used, base + m - RING + 1)
                    act.wait_ge(f_even_copied, 2)
                    act.activation(ring[:, ds(((base + m) % RING) * W, W)], tt[:, ds((m % 3) * W, W)], ACT.Exp,
                                   scale=0.5).then_inc(tile_exp, 1)

                tanh(0)
                with act.Fori(0, number - 1) as m:
                    act.wait_ge(tile_exp, base + m - 1)
                    act.wait_ge(f_even_copied, 2)
                    tanh(m + 1)
                    exp(m)
                exp(number - 1)

            act.wait_ge(f_even_copied, 2)
            act.wait_ge(f_odd_copied, 2)
            tile_pass(BE, NE, lambda m: m // T, lambda m: m % T)

            def batch_affine(k, dst, src, width):
                act.wait_ge(bn_cols, k + 1)
                act.activation(chunks(dst), src, ACT.Identity, bias=bnv[:, 2 * F:2 * F + 1],
                               scale=bnv[:, F:F + 1]).then_inc(aff_done, 1)

            def elu_parts(k, bias):
                act.wait_ge(mlp_mm, k + 1)
                for f in range(F):
                    act.wait_ge(mlp_min, F * k + f + 1)
                    act.activation(chunks(ring, f, W), ps[:, f * NC:(f + 1) * NC, 0:C], ACT.Relu,
                                   bias=bias(f)).then_inc(mlp_act, 1)
                    act.activation(tt[:, f * W:(f + 1) * W], tt[:, f * W:(f + 1) * W], ACT.Exp).then_inc(mlp_act, 1)

            def col(i, f):
                return colv[:, f * 8 + i:f * 8 + i + 1]

            batch_affine(0, gb, ps[:, 0:NC, 0:C], NP)
            elu_parts(0, lambda f: col(EM_B, f))
            batch_affine(1, ht, chunks(ga), NP)
            for r in range(TR):
                act.wait_ge(tr_done, 2 * TR + r + 1)
                k = min(2, T - 2 * r) * D
                act.activation(h[:, 2 * r * D:2 * r * D + k], ps[:, 6 + r % 2, 0:k], ACT.Copy).then_inc(tr_copied, 1)
            tile_pass(BD, ND, lambda m: 2 * (m // (2 * T)) + m % 2, lambda m: (m % (2 * T)) // 2)
            elu_parts(1, lambda f: 0.0)
            elu_parts(2, lambda f: col(DM_B, f))
            batch_affine(2, ht, chunks(ga), NP)

            norm_apply(2)
            copy_aggregate(agg_done, 2, ga)
            with act.Fori(0, T) as t:
                act.wait_ge(np_mm, T + t + 1)
                act.wait_ge(np_mixed, T + t - 1)
                act.wait_ge(dinv_ready, 1)
                act.activation(e_q[:, ds((t % 2) * D, D)], psf[:, ds((t % 2) * 1024, D)], ACT.Copy,
                               scale=dinv1[:, ds(t, 1)]).then_inc(np_scaled, 1)

            norm_apply(3)
            with act.Fori(0, T) as t:
                act.wait_ge(hn_mm, t + 1)
                act.wait_ge(tr_copied, 6 * TR)
                act.activation(h[:, ds(t * D, D)], psf[:, ds((t % 2) * 512, D)], ACT.Copy).then_inc(hn_copied, 1)
            for r in range(TR):
                act.wait_ge(tr_done, 6 * TR + r + 1)
                k = min(2, T - 2 * r)
                act.activation(fm(h_hi)[:, :, 2 * r * P:(2 * r + k) * P],
                               ps[:, 6 + r % 2, 0:F * 2 * P].rearrange("p (f n) -> p f n", f=F)[:, :, 0:k * P],
                               ACT.Copy).then_inc(hi_done, 1)
            with act.Fori(0, T) as j:
                act.wait_ge(tile_used, B3 + j - RING + 1)
                act.wait_ge(tile_summed, 2 * T + 1 + j - RING + 1)
                for c in range(NC):
                    act.wait_ge(sim_mm, NC * j + c + 1)
                    act.wait_ge(hi_done, TR)
                    act.activation(ring[:, ds(((B3 + j) % RING) * W + c * C, C)],
                                   psf[:, ds((6 + (j + c) % 2) * 512, C)], ACT.Exp).then_inc(sim_exp, 1)
            copy_aggregate(tile_used, B3 + T, ga)

        @block.vector
        def _(dve):
            own = [0]

            def link(ins):
                own[0] += 1
                ins.then_inc(dve_own, 1)
                dve.wait_ge(dve_own, own[0])

            def note(ins):
                own[0] += 1
                ins.then_inc(dve_own, 1)

            def norm_stats(layer):
                with dve.Fori(0, T) as t:
                    dve.bn_stats(stats[:, ds(t * 6, 6)], x[:, ds(t * D, D)]).then_inc(stats_done, 1)
                dve.wait_ge(stats_done, T * (layer + 1))
                s = stats[:, :].rearrange("p (t k) -> p k t", k=6)
                total, diff, m2, d2, var, nmean = (lnt[:, k * T:(k + 1) * T] for k in range(6))
                note(dve.tensor_tensor(total, s[:, 1], s[:, 4], ALU.add))
                note(dve.tensor_tensor(diff, s[:, 1], s[:, 4], ALU.subtract))
                link(dve.tensor_tensor(m2, s[:, 2], s[:, 5], ALU.add))
                note(dve.tensor_tensor(d2, diff, diff, ALU.mult))
                note(dve.tensor_scalar(nmean, total, -0.5, None, ALU.mult))
                link(dve.tensor_scalar(m2, m2, 1.0 / D, LN_EPS, ALU.mult, ALU.add))
                dve.scalar_tensor_tensor(var, d2, 0.25, m2, ALU.mult, ALU.add).then_inc(lnvar, 1)

            def copy_transposes(batch, dst):
                for r in range(TR):
                    dve.wait_ge(tr_done, batch * TR + r + 1)
                    k = min(2, T - 2 * r) * P
                    dve.tensor_copy(fm(dst)[:, :, 2 * r * P:2 * r * P + k],
                                    ps[:, 6 + r % 2, 0:F * 2 * P].rearrange("p (f n) -> p f n", f=F)[:, :, 0:k])\
                       .then_inc(tr_copied, 1)

            def copy_aggregate(done, count, dst):
                dve.wait_ge(done, count)
                dve.tensor_copy(chunks(dst, 1), ps[:, NC:2 * NC, 0:C]).then_inc(agg_copied, 1)

            dve.wait_ge(x_loaded, 16)
            norm_stats(0)
            for j in range(T):
                dve.wait_ge(adj_ld[j % RING], 16 * (j // RING + 1))
                dve.tensor_copy(at[:, j * W:(j + 1) * W], ring[:, (j % RING) * W:(j % RING + 1) * W])\
                   .then_inc(adj_cast, 1)
                if j == 1:
                    dve.wait_ge(h_done, T)
                    dve.tensor_copy(h_hi[:, :], h[:, :]).then_inc(h16_done, 1)
                    dve.wait_ge(h16_done, 1)
                    dve.tensor_tensor(h_lo[:, :], h[:, :], h_hi[:, :], ALU.subtract).then_inc(h16_done, 1)
                if j == 2:
                    copy_transposes(0, ht)
            dve.wait_ge(c0_mm, 1)
            link(dve.tensor_copy(c0[:, :], ps[:, 0, 0:F * 2]))
            r3v = r3.rearrange("p (f n) -> p f n", f=F)
            c0v = c0[:, :].rearrange("p (f n) -> p f n", f=F)
            dve.wait_ge(w0_loaded, 16 * NW0)
            dve.tensor_copy(r3v[:, :, 2:3], c0v[:, :, 1:2]).then_inc(c0_copied, 1)
            dve.wait_ge(consts, NCONST)
            for f in range(F):
                dve.tensor_scalar(cb[:, f * P:(f + 1) * P], ones[:, :], c0[:, f * 2:f * 2 + 1], None, ALU.mult)\
                   .then_inc(cb_ready, 1)
            dve.wait_ge(r3_mm, 1)
            pr3 = ps[:, 1, 0:3 * T].rearrange("p (t k) -> p k t", k=3)
            dve.tensor_scalar(srt, pr3[:, 2], -0.01, None, ALU.mult).then_inc(r3_copied, 1)
            dve.tensor_scalar(sr99, pr3[:, 2], 0.99, None, ALU.mult).then_inc(r3_copied, 1)
            for k in range(2):
                dve.tensor_scalar(gab[:, k * T:(k + 1) * T], pr3[:, k], rowv[:, R_BA + k:R_BA + k + 1], None,
                                  ALU.add).then_inc(r3_copied, 1)
            dve.wait_ge(srow_mm, 1)
            dve.wait_ge(srow_copied, 1)
            dve.tensor_scalar(chunks(frow, 1, W), ps[:, 2:2 + NC, 0:C], 0.01, None, ALU.mult)\
               .then_inc(srow_copied, 1)
            dve.wait_ge(srow_copied, 2)
            dve.wait_ge(r3_copied, 4)

            def score_arg(j):
                dve.scalar_tensor_tensor(tt[:, ds((j % 2) * W, W)], frow[:, 0:W], sr99[:, ds(j, 1)],
                                         frow[:, W:2 * W], ALU.add, ALU.max).then_inc(tile_arg, 1)

            def mask(n, j):
                dve.wait_ge(tile_exp, n + 1)
                w = ring[:, ds((n % RING) * W, W)]
                dve.tensor_tensor(w, w, at[:, ds(j * W, W)], ALU.mult).then_inc(tile_masked, 1)

            score_arg(0)
            with dve.Fori(1, RING + 1) as j:
                score_arg(j)
                mask(j - 1, j - 1)
            copy_aggregate(agg_done, 1, ga)
            with dve.Fori(RING + 1, T) as j:
                score_arg(j)
                mask(j - 1, j - 1)
            mask(T - 1, T - 1)
            link(dve.tensor_scalar(x[:, :], x[:, :], 0.5, None, ALU.add))
            dve.wait_ge(gate_mm, 1)
            pg = ps[:, 6, 0:2 * T].rearrange("p (t k) -> p k t", k=2)
            dve.tensor_tensor(gates.rearrange("p (k t) -> p k t", k=2), pg,
                              gab.rearrange("p (k t) -> p k t", k=2), ALU.add).then_inc(gate_sum, 1)
            link(dve.tensor_scalar(dmax, ps[:, 6, 3 * T:4 * T], 1.0, None, ALU.max))
            link(dve.reciprocal(dinv, dmax))
            dve.tensor_scalar(dinv1, dinv, 1.0, None, ALU.add).then_inc(dinv_ready, 1)
            link(dve.tensor_scalar(rs, ps[:, 6, 2 * T:3 * T], L0_EPS, None, ALU.add))
            link(dve.reciprocal(rs, rs))
            dve.wait_ge(gate_tanh, 1)
            link(dve.tensor_scalar(attn, gates, 0.5, 0.5, ALU.mult, ALU.add))
            dve.tensor_tensor(ca, attn[:, 0:T], rs, ALU.mult).then_inc(gate_attn, 1)
            copy_aggregate(tile_used, B0 + T, gb)
            dve.wait_ge(gate_attn, 1)

            def l0_mix(t):
                dve.wait_ge(np_scaled, t + 1)
                dve.scalar_tensor_tensor(e_t[:, ds((t % 2) * D, D)], psf[:, ds((t % 2) * 1024 + 512, D)],
                                         ca[:, ds(t, 1)], e_q[:, ds((t % 2) * D, D)], ALU.mult, ALU.add)\
                   .then_inc(np_mixed, 1)

            def l0_add(t):
                dve.wait_ge(np_act, t + 1)
                dve.scalar_tensor_tensor(x[:, ds(t * D, D)], e_t[:, ds((t % 2) * D, D)], 0.5,
                                         x[:, ds(t * D, D)], ALU.mult, ALU.add).then_inc(np_done, 1)

            l0_mix(0)
            l0_mix(1)
            l0_add(0)
            with dve.Fori(1, T - 1) as t:
                dve.wait_ge(np_done, t)
                l0_mix(t + 1)
                l0_add(t)
            l0_add(T - 1)

            dve.wait_ge(np_done, T)
            norm_stats(1)
            dve.wait_ge(c1_mm, 1)
            link(dve.tensor_copy(c1[:, :], ps[:, 0, 0:F * 8]))
            for hd in range(H):
                dve.tensor_scalar(cb[:, hd * P:(hd + 1) * P], ones[:, :],
                                  c1[:, (hd // 2) * 8 + 2 * hd:(hd // 2) * 8 + 2 * hd + 1], None, ALU.mult)\
                   .then_inc(cb_ready, 1)
            copy_transposes(1, ht)
            dve.wait_ge(f2_mm, 1)
            dve.tensor_scalar(f2[:, :].rearrange("p (h t) -> p h t", h=H),
                              ps[:, 1, 0:8 * T].rearrange("p (t h s) -> p s h t", t=T, h=H)[:, 1],
                              0.5, None, ALU.mult).then_inc(f2_copied, 1)
            for hd in (1, 3):
                dve.wait_ge(f_mm, hd + 1)
                dve.tensor_copy(chunks(frow, hd, W), ps[:, 5:5 + NC, 0:C]).then_inc(f_odd_copied, 1)

            def enc_masks(hd, a, b):
                with dve.Fori(a, b) as j:
                    mask(BE + hd * T + j, j)

            def copy_head(hd):
                b, pr = hd % 2, hd // 2
                mine, other = b * DH, (1 - b) * DH
                banks = ps[:, b * NC:(b + 1) * NC, 0:C]
                dve.wait_ge(tile_used, BE + (hd + 1) * T)
                dve.tensor_copy(chunks(ga, pr)[mine:mine + DH], banks[mine:mine + DH]).then_inc(head_copied, 1)
                dve.tensor_scalar(chunks(rinv, pr, W)[mine:mine + DH], banks[other:other + DH], 0.25, None,
                                  ALU.max).then_inc(head_copied, 1)

            def invert(pr, c):
                a = pr * W + c * C
                dve.wait_ge(head_copied, 4 * (pr + 1))
                link(dve.reciprocal(rinv[:, a:a + C], rinv[:, a:a + C]))
                g = ga[:, pr * NP + c * C:pr * NP + (c + 1) * C]
                dve.tensor_tensor(g, g, rinv[:, a:a + C], ALU.mult).then_inc(norm_ready, 1)

            for hd in range(H):
                enc_masks(hd, 0, 3)
                if hd:
                    copy_head(hd - 1)
                for c in range(NC):
                    if hd == 2:
                        invert(0, c)
                    enc_masks(hd, 3 + 2 * c, 5 + 2 * c)
                enc_masks(hd, 9, T)
            copy_head(H - 1)
            for c in range(NC):
                invert(1, c)

            def batch_stats(k, src, gamma, beta):
                for f in range(F):
                    for c in range(NC):
                        last = dve.bn_stats(bnst[:, (f * NC + c) * 6:(f * NC + c + 1) * 6],
                                            src(f, c, min(C, N - c * C)))
                        (link if (f, c) == (F - 1, NC - 1) else note)(last)
                for f in range(F):
                    (link if f == F - 1 else note)(
                        dve.bn_aggr(bnag[:, f * 2:(f + 1) * 2], bnst[:, f * NC * 6:(f + 1) * NC * 6]))
                ag = bnag[:, :].rearrange("p (f k) -> p k f", k=2)
                dve.tensor_scalar(bnv[:, 0:F], ag[:, 1], BN_EPS, None, ALU.add).then_inc(bn_var, 1)
                dve.wait_ge(bn_pow, k + 1)
                cv = colv[:, :].rearrange("p (f k) -> p k f", k=8)
                dve.wait_ge(w_loaded, 16 * NWR)
                link(dve.tensor_tensor(bnv[:, F:2 * F], bnv[:, 0:F], cv[:, gamma], ALU.mult))
                link(dve.tensor_tensor(bnv[:, 2 * F:3 * F], ag[:, 0], bnv[:, F:2 * F], ALU.mult))
                dve.tensor_tensor(bnv[:, 2 * F:3 * F], cv[:, beta], bnv[:, 2 * F:3 * F],
                                  ALU.subtract).then_inc(bn_cols, 1)
                dve.wait_ge(bn_cols, k + 1)

            def batch_affine(dst, src):
                dve.tensor_scalar(chunks(dst, 1), src, bnv[:, F + 1:F + 2], bnv[:, 2 * F + 1:2 * F + 2],
                                  ALU.mult, ALU.add).then_inc(aff_done, 1)

            def elu(k, bias, residual, dst, done):
                dve.wait_ge(mlp_mm, k + 1)
                for f in range(F):
                    dve.tensor_scalar(chunks(tt, f, W), ps[:, f * NC:(f + 1) * NC, 0:C], bias(f), 0.0,
                                      ALU.add, ALU.min).then_inc(mlp_min, 1)
                for f in range(F):
                    dve.wait_ge(mlp_act, 2 * (F * k + f) + 2)
                    q = dve.scalar_tensor_tensor(dst[:, f * NP:f * NP + W], tt[:, f * W:(f + 1) * W], -1.0,
                                                 ring[:, f * W:(f + 1) * W], ALU.add, ALU.add)
                    if residual is not None:
                        link(q)
                        q = dve.tensor_tensor(dst[:, f * NP:f * NP + W], dst[:, f * NP:f * NP + W],
                                              residual[:, f * NP:f * NP + W], ALU.add)
                    q.then_inc(done, 1)

            def col(i, f):
                return colv[:, f * 8 + i:f * 8 + i + 1]

            dve.wait_ge(proj_mm, 1)
            batch_stats(0, lambda f, c, n: ps[:, f * NC + c, 0:n], E_G, E_B)
            batch_affine(gb, ps[:, NC:2 * NC, 0:C])
            dve.wait_ge(aff_done, 2)
            elu(0, lambda f: col(EM_B, f), gb, ga, mlp_sum)
            dve.wait_ge(mlp_sum, F)
            batch_stats(1, lambda f, c, n: ga[:, f * NP + c * C:f * NP + c * C + n], EM_G, EM_BB)
            batch_affine(ht, chunks(ga, 1))
            for pr in range(2):
                with dve.Fori(0, 2 * T) as m:
                    mask(BD + pr * 2 * T + m, m // 2)
                if pr:
                    for q in range(2):
                        dve.wait_ge(tile_used, BD + 2 * T * (q + 1))
                        dve.tensor_tensor(chunks(ga, q), ps[:, q * NC:(q + 1) * NC, 0:C], chunks(rinv, q, W),
                                          ALU.mult).then_inc(norm_ready, 1)
            elu(1, lambda f: 0.0, None, gb, dec_ready)
            dve.wait_ge(dec_ready, F)
            elu(2, lambda f: col(DM_B, f), gb, ga, mlp_sum)
            dve.wait_ge(mlp_sum, 2 * F)
            batch_stats(2, lambda f, c, n: ga[:, f * NP + c * C:f * NP + c * C + n], DM_G, DM_BB)
            batch_affine(ht, chunks(ga, 1))
            for r in range(TR):
                dve.wait_ge(tr_done, 3 * TR + r + 1)
                a, b = 2 * r * D, min(2 * r + 2, T) * D
                dve.tensor_tensor(x[:, a:b], x[:, a:b], ps[:, 6 + r % 2, 0:b - a], ALU.add).then_inc(tr_copied, 1)

            dve.wait_ge(tr_copied, 4 * TR)
            norm_stats(2)
            dve.wait_ge(h_done, 3 * T)
            dve.tensor_copy(h_hi[:, :], h[:, :]).then_inc(h16_done, 1)
            dve.wait_ge(h16_done, 3)
            dve.tensor_tensor(h_lo[:, :], h[:, :], h_hi[:, :], ALU.subtract).then_inc(h16_done, 1)
            copy_transposes(4, ht)
            copy_aggregate(agg_done, 2, ga)

            with dve.Fori(0, T) as t:
                o = e_t[:, ds((t % 2) * D, D)]
                dve.wait_ge(np_scaled, T + t + 1)
                dve.scalar_tensor_tensor(o, psf[:, ds((t % 2) * 1024 + 512, D)], dinv[:, ds(t, 1)],
                                         e_q[:, ds((t % 2) * D, D)], ALU.mult, ALU.add).then_inc(np_mixed, 1)
                dve.wait_ge(np_mixed, T + t + 1)
                dve.tensor_tensor(o, o, rowv[:, R_L2B:R_L2B + D], ALU.add).then_inc(np_act, 1)
                dve.wait_ge(np_act, T + t + 1)
                dve.scalar_tensor_tensor(x[:, ds(t * D, D)], o, 0.0, x[:, ds(t * D, D)], ALU.max, ALU.add)\
                   .then_inc(np_done, 1)

            dve.wait_ge(np_done, 2 * T)
            norm_stats(3)
            copy_transposes(5, ht)
            with dve.Fori(0, T) as t:
                dve.wait_ge(hn_copied, t + 1)
                dve.tensor_tensor(gb[:, ds(t * D, D)], h[:, ds(t * D, D)], h[:, ds(t * D, D)], ALU.mult)\
                   .then_inc(sq_done, 1)
            dve.wait_ge(sq_done, T)
            link(dve.tensor_reduce(n2, gb[:, 0:T * D].rearrange("p (t d) -> p t d", t=T), AX_X, ALU.add))
            dve.tensor_scalar(n2, n2, NORM_EPS * NORM_EPS, None, ALU.max).then_inc(nrm_done, 1)
            dve.wait_ge(nrm_pow, 1)
            with dve.Fori(0, T) as t:
                dve.tensor_scalar(ga[:, ds(t * D, D)], h[:, ds(t * D, D)], nsum[:, ds(t, 1)], None, ALU.mult)\
                   .then_inc(hn_done, 1)
            for r in range(TR):
                dve.wait_ge(hi_done, r + 1)
                k = min(2, T - 2 * r)
                hi = fm(h_hi)[:, :, 2 * r * P:(2 * r + k) * P]
                dve.tensor_tensor(fm(h_lo)[:, :, 2 * r * P:(2 * r + k) * P],
                                  ps[:, 6 + r % 2, 0:F * 2 * P].rearrange("p (f n) -> p f n", f=F)[:, :, 0:k * P],
                                  hi, ALU.subtract).then_inc(tr_copied, 1)
            with dve.Fori(0, T) as t:
                dve.tensor_tensor(x[:, ds(t * D, D)], x[:, ds(t * D, D)], rowv[:, R_L3B:R_L3B + D], ALU.add)\
                   .then_inc(bias_done, 1)
            with dve.Fori(0, T) as j:
                dve.wait_ge(sim_exp, NC * j + NC)
                w = ring[:, ds(((B3 + j) % RING) * W, W)]
                dve.scalar_tensor_tensor(w, at[:, ds(j * W, W)], epsv[:, ds(j, 1)], w, ALU.add, ALU.mult)\
                   .then_inc(tile_masked, 1)
            dve.wait_ge(s3_mm, 1)
            link(dve.tensor_scalar(rs, ps[:, 6, 0:T], 1e-30, None, ALU.max))
            link(dve.reciprocal(rs, rs))
            copy_aggregate(tile_used, B3 + T, ga)
            dve.wait_ge(bias_done, T)
            for t in range(T):
                dve.wait_ge(tr_done, 7 * TR + t // 2 + 1)
                a = (t % 2) * D
                last = dve.scalar_tensor_tensor(x[:, t * D:(t + 1) * D], ps[:, 6 + (t // 2) % 2, a:a + D],
                                                rs[:, t:t + 1], x[:, t * D:(t + 1) * D], ALU.mult, ALU.add)
                last.then_inc(np_done, 1)

        @block.tensor
        def _(pe):
            pe.wait_ge(consts, NCONST)

            def weight(i, f):
                return wt[:, (i * F + f) * D:(i * F + f + 1) * D]

            def to_feature_major(batch, src, ready, base, every=1):
                for r in range(TR):
                    pe.wait_ge(ready, base + min(2 * r + 2, T))
                    if r >= 2:
                        pe.wait_ge(tr_copied, batch * TR + r - 1)
                    for f in range(F):
                        for u in range(min(2, T - 2 * r)):
                            a = (2 * r + u) * D + f * P
                            last = pe.transpose(ps[:, 6 + r % 2, f * 2 * P + u * P:f * 2 * P + (u + 1) * P],
                                                src[:, a:a + P], ident[:, :])
                    last.then_inc(tr_done, 1)

            def to_node_major(batch, src):
                for r in range(TR):
                    if r >= 2:
                        if batch == 7:
                            pe.wait_ge(np_done, 2 * T + 2 * (r - 1))
                        else:
                            pe.wait_ge(tr_copied, batch * TR + r - 1)
                    for u in range(min(2, T - 2 * r)):
                        for f in range(F):
                            a = f * NP + (2 * r + u) * P
                            last = pe.transpose(ps[:, 6 + r % 2, u * D + f * P:u * D + (f + 1) * P],
                                                src[:, a:a + P], ident[:, :])
                    last.then_inc(tr_done, 1)

            def node_product(dst, src, t, rhs, n):
                for f in range(F):
                    last = pe.matmul(dst, src[:, f * NP + t * P:f * NP + (t + 1) * P], rhs(f)[:, 0:n],
                                     start=f == 0, stop=f == F - 1)
                return last

            def aggregate(k):
                def tile(j, start, stop):
                    for f in range(F):
                        for part in (h_hi, h_lo):
                            for c in range(NC):
                                last = pe.matmul(ps[:, f * NC + c, 0:C], part[:, ds(j * D + f * P, P)],
                                                 at[:, ds(j * W + c * C, C)], start=start and part is h_hi,
                                                 stop=stop and part is h_lo)
                    return last
                if k == 0:
                    pe.wait_ge(adj_cast, T)
                tile(0, True, False)
                with pe.Fori(1, T - 1) as j:
                    tile(j, False, False)
                tile(T - 1, False, True).then_inc(agg_done, 1)

            def weighted(base, vbase):
                def tile(j, slot, start, stop):
                    pe.wait_ge(vs_ready, vbase + j + 1)
                    pe.wait_ge(tile_masked, base + j + 1)
                    for f in range(F):
                        for c in range(NC):
                            last = pe.matmul(ps[:, f * NC + c, 0:C], vs[:, slot * D + f * P:slot * D + (f + 1) * P],
                                             ring[:, ds(((base + j) % RING) * W + c * C, C)], start=start, stop=stop)
                    last.then_inc(tile_used, 1)
                return tile

            pe.wait_ge(w0_loaded, 16 * NW0)
            for d in range(F):
                for f in range(F):
                    last = pe.matmul(ps[:, 0, d * 2:d * 2 + 2], weight(W_SA_T, f)[:, d * P:(d + 1) * P],
                                     a2[:, f * 2:f * 2 + 2], start=f == 0, stop=f == F - 1)
            last.then_inc(c0_mm, 1)
            to_feature_major(0, h, h_done, 0)
            pe.wait_ge(c0_copied, 1)
            pe.wait_ge(tr_copied, TR)
            for t in range(T):
                last = node_product(ps[:, 1, 3 * t:3 * t + 3], ht, t, lambda f: r3[:, f * 3:(f + 1) * 3], 3)
            last.then_inc(r3_mm, 1)
            pe.wait_ge(cb_ready, F)
            for c in range(NC):
                for f in range(F):
                    last = pe.matmul(ps[:, 2 + c, 0:C], cb[:, f * P:(f + 1) * P],
                                     ht[:, f * NP + c * C:f * NP + (c + 1) * C], start=f == 0, stop=f == F - 1)
            last.then_inc(srow_mm, 1)
            pe.wait_ge(h16_done, 2)
            pe.wait_ge(r3_copied, 4)
            pe.wait_ge(srow_copied, 2)
            aggregate(0)
            pe.wait_ge(agg_copied, 2)
            tile = weighted(B0, 0)
            tile(0, 0, True, False)
            with pe.Fori(1, T - 2, 2) as j:
                tile(j, 1, False, False)
                tile(j + 1, 0, False, False)
            tile(T - 2, 1, False, False)
            tile(T - 1, 0, False, True)
            for t in range(T):
                last = node_product(ps[:, 6, 2 * t:2 * t + 2], ga, t, lambda f: gw[:, f * 2:(f + 1) * 2], 2)
            pe.wait_ge(tile_summed, 2 * T)
            for k, acc in ((2, s_acc), (3, d_acc)):
                for t in range(T):
                    last = pe.matmul(ps[:, 6, k * T + t:k * T + t + 1], acc[:, t * P:(t + 1) * P], ones[:, 0:1],
                                     start=True, stop=True)
            last.then_inc(gate_mm, 1)
            pe.wait_ge(agg_copied, 4)
            for t in range(T):
                if t >= 2:
                    pe.wait_ge(np_mixed, t - 1)
                pb, pa = ps[:, 2 * (t % 2), 0:D], ps[:, 2 * (t % 2) + 1, 0:D]
                pe.matmul(pb, ones[0:1, :], rowv[0:1, R_GCNB:R_GCNB + D], start=True, stop=False)
                for f in range(F):
                    pe.matmul(pb, ga[:, f * NP + t * P:f * NP + (t + 1) * P], weight(W_GCNB, f), start=False,
                              stop=f == F - 1)
                node_product(pa, gb, t, lambda f: weight(W_SA, f), D).then_inc(np_mm, 1)

            pe.wait_ge(w_loaded, 16 * NWR)
            pe.wait_ge(np_mixed, T)
            for pr in range(F):
                last = pe.matmul(ps[:, 0, pr * 8:pr * 8 + 8], wbd[:, (W_BD_T * F + pr) * P:(W_BD_T * F + pr + 1) * P],
                                 vb[:, pr * 8:(pr + 1) * 8], start=True, stop=True)
            last.then_inc(c1_mm, 1)
            to_feature_major(1, h, h_done, T)
            pe.wait_ge(cb_ready, F + H)
            pe.wait_ge(tr_copied, 2 * TR)
            for hd in range(H):
                if hd >= 2:
                    pe.wait_ge((f_even_copied, f_odd_copied)[hd % 2], 1)
                pr, b0 = hd // 2, 2 + (hd % 2) * NC
                for c in range(NC):
                    last = pe.matmul(ps[:, b0 + c, 0:C], cb[:, hd * P:(hd + 1) * P],
                                     ht[:, pr * NP + c * C:pr * NP + (c + 1) * C], start=True, stop=True)
                last.then_inc(f_mm, 1)
                if hd == 0:
                    for t in range(T):
                        last = node_product(ps[:, 1, 8 * t:8 * t + 8], ht, t, lambda f: c1[:, f * 8:(f + 1) * 8], 8)
                    last.then_inc(f2_mm, 1)
            pe.wait_ge(f_even_copied, 2)
            pe.wait_ge(f_odd_copied, 2)
            pe.wait_ge(f2_copied, 1)

            for hd in range(H):
                b = hd % 2
                if hd >= 2:
                    pe.wait_ge(head_copied, 2 * (hd - 1))

                def enc_tile(j, par, start, stop):
                    n = hd * T + j
                    pe.wait_ge(vs_ready, T + n + 1)
                    pe.wait_ge(tile_masked, BE + n + 1)
                    for c in range(NC):
                        last = pe.matmul(ps[:, b * NC + c, 0:C], vs[:, (b * 2 + par) * P:(b * 2 + par + 1) * P],
                                         ring[:, ds(((BE + n) % RING) * W + c * C, C)], start=start, stop=stop)
                    return last.then_inc(tile_used, 1)

                s = (hd * T) % 2
                enc_tile(0, s, True, False)
                with pe.Fori(1, T - 2, 2) as j:
                    enc_tile(j, 1 - s, False, False)
                    enc_tile(j + 1, s, False, False)
                enc_tile(T - 2, 1 - s, False, False)
                enc_tile(T - 1, s, False, True)

            def project(which, ready, count, done):
                pe.wait_ge(ready, count)
                for pr in range(F):
                    for c in range(NC):
                        last = pe.matmul(ps[:, pr * NC + c, 0:C], wbd[:, (which * F + pr) * P:(which * F + pr + 1) * P],
                                         ga[:, pr * NP + c * C:pr * NP + (c + 1) * C], start=True, stop=True)
                last.then_inc(done, 1)

            def mlp(i):
                for fo in range(F):
                    for fi in range(F):
                        for c in range(NC):
                            last = pe.matmul(ps[:, fo * NC + c, 0:C], weight(i, fi)[:, fo * P:(fo + 1) * P],
                                             gb[:, fi * NP + c * C:fi * NP + (c + 1) * C], start=fi == 0,
                                             stop=fi == F - 1)
                last.then_inc(mlp_mm, 1)

            pe.wait_ge(head_copied, 2 * H)
            project(W_BD, norm_ready, 2 * NC, proj_mm)
            pe.wait_ge(aff_done, 2)
            mlp(MLP_E)
            pe.wait_ge(aff_done, 4)
            to_node_major(2, ht)

            for pr in range(2):
                def dec_tile(j, u, start, stop):
                    pe.wait_ge(vs_ready, T + NE + pr * T + j + 1)
                    for b in range(2):
                        n = BD + 2 * (pr * T + j) + b
                        slot = (BD + 2 * (pr * T + u) + b) % RING
                        par = (pr * T + u) % 2
                        pe.wait_ge(tile_masked, n + 1)
                        for c in range(NC):
                            last = pe.matmul(ps[b * DH:(b + 1) * DH, pr * NC + c, 0:C],
                                             vs[:, par * P + b * DH:par * P + (b + 1) * DH],
                                             ring[:, slot * W + c * C:slot * W + (c + 1) * C], start=start, stop=stop)
                    last.then_inc(tile_used, 2)

                dec_tile(0, 0, True, False)
                with pe.Fori(1, T - 2, 2) as j:
                    dec_tile(j, 1, False, False)
                    dec_tile(j + 1, 2, False, False)
                dec_tile(T - 2, T - 2, False, False)
                dec_tile(T - 1, T - 1, False, True)
            project(W_BD_T, norm_ready, 2 * NC + 2, mlp_mm)
            pe.wait_ge(dec_ready, F)
            mlp(MLP_D)
            pe.wait_ge(aff_done, 6)
            to_node_major(3, ht)

            to_feature_major(4, h, h_done, 2 * T)
            pe.wait_ge(h16_done, 4)
            aggregate(2)
            pe.wait_ge(agg_copied, 6)
            pe.wait_ge(tr_copied, 5 * TR)
            for t in range(T):
                if t >= 2:
                    pe.wait_ge(np_mixed, T + t - 1)
                node_product(ps[:, 2 * (t % 2), 0:D], ht, t, lambda f: weight(W_L2, f), D)
                node_product(ps[:, 2 * (t % 2) + 1, 0:D], ga, t, lambda f: weight(W_L2, f), D).then_inc(np_mm, 1)

            to_feature_major(5, h, h_done, 3 * T)
            pe.wait_ge(tr_copied, 6 * TR)
            for t in range(T):
                if t >= 2:
                    pe.wait_ge(hn_copied, t - 1)
                node_product(ps[:, t % 2, 0:D], ht, t, lambda f: weight(W_L3, f), D).then_inc(hn_mm, 1)
            to_feature_major(6, ga, hn_done, 0)
            pe.wait_ge(tr_copied, 7 * TR)

            def similarity(j):
                for c in range(NC):
                    if c < 2:
                        pe.wait_ge(sim_exp, NC * j + c - 1)
                    else:
                        pe.wait_ge(sim_exp, NC * j + 1)
                    pairs = [(a, b, f) for a, b in ((h_hi, h_hi), (h_hi, h_lo), (h_lo, h_hi)) for f in range(F)]
                    for k, (a, b, f) in enumerate(pairs):
                        if k == 0:
                            pe.wait_ge(tr_copied, 7 * TR)
                        last = pe.matmul(psf[:, ds((6 + (j + c) % 2) * 512, C)], a[:, ds(f * NP + j * P, P)],
                                         b[:, f * NP + c * C:f * NP + (c + 1) * C], start=k == 0,
                                         stop=k == len(pairs) - 1)
                    last.then_inc(sim_mm, 1)

            def similarity_first():
                for c in range(NC):
                    if c == 2:
                        pe.wait_ge(sim_exp, 1)
                    pairs = [(a, b, f) for a, b in ((h_hi, h_hi), (h_hi, h_lo), (h_lo, h_hi)) for f in range(F)]
                    for k, (a, b, f) in enumerate(pairs):
                        last = pe.matmul(ps[:, 6 + c % 2, 0:C], a[:, f * NP:f * NP + P],
                                         b[:, f * NP + c * C:f * NP + (c + 1) * C], start=k == 0,
                                         stop=k == len(pairs) - 1)
                    last.then_inc(sim_mm, 1)

            tile = weighted(B3, T + NE + 2 * T)
            similarity_first()
            similarity(1)
            tile(0, 0, True, False)
            with pe.Fori(1, T - 2, 2) as j:
                similarity(j + 1)
                tile(j, 1, False, False)
                similarity(j + 2)
                tile(j + 1, 0, False, False)
            similarity(T - 1)
            tile(T - 2, 1, False, False)
            tile(T - 1, 0, False, True)
            pe.wait_ge(tile_summed, 3 * T + 1)
            for t in range(T):
                last = pe.matmul(ps[:, 6, t:t + 1], s_acc[:, t * P:(t + 1) * P], ones[:, 0:1], start=True, stop=True)
            last.then_inc(s3_mm, 1)
            pe.wait_ge(agg_copied, 8)
            to_node_major(7, ga)


def kernel(**inputs):
    import numpy as np
    import concourse.bacc as bacc
    from concourse.bass_utils import run_bass_kernel_spmd

    a = {k: np.ascontiguousarray(v) for k, v in inputs.items()}
    n, d = a["x"].shape
    tiles = -(-n // P)
    width = -(-n // 3) * 3
    heads, dh = a["L1_gnn_W"].shape[:2]

    def zeros(*shape):
        return np.zeros(shape, np.float32)

    x = zeros(tiles * P, d)
    x[:n] = a["x"]
    adj_t = zeros(tiles * P, width)
    adj_t[:n, :n] = a["adj"].T
    bd, bdt, vb = zeros(d, P), zeros(d, P), zeros(d, 2 * heads)
    for i in range(heads):
        rows_, c = slice(i * dh, (i + 1) * dh), (i % 2) * dh
        bd[rows_, c:c + dh] = a["L1_gnn_W"][i]
        bdt[rows_, c:c + dh] = a["L1_gnn_W"][i].T
        vb[rows_, 2 * i] = a["L1_gnn_V"][i, 0, :, 0]
        vb[rows_, 2 * i + 1] = a["L1_gnn_V"][i, 1, :, 0]
    mats = [a["L0_gnn_W_sa"], a["L0_gnn_W_sa"].T, a["L0_gnn_W_gcnb"], a["L1_gnn_enc_mlp_W"].T,
            a["L1_gnn_dec_mlp_W"].T, a["L2_gnn_W"], a["L3_gnn_weight"]]
    wa, wb, asa = a["L0_gnn_Wa"][0], a["L0_gnn_Wb"][0], a["L0_gnn_a_sa"][0]
    names = ["enc_bn_gamma", "enc_bn_beta", "enc_mlp_b", "enc_mlp_bn_gamma", "enc_mlp_bn_beta",
             "dec_mlp_b", "dec_mlp_bn_gamma", "dec_mlp_bn_beta"]
    arrays = {
        "in_x": x, "in_adj_t": adj_t, "in_mats": np.ascontiguousarray(np.stack(mats)),
        "in_blocks": np.ascontiguousarray(np.stack([bd, bdt])),
        "in_a2": np.ascontiguousarray(np.stack([asa[:d], asa[d:]], 1)),
        "in_gw": np.ascontiguousarray(np.stack([wa[:d], wb[:d]], 1)),
        "in_wr": np.ascontiguousarray(np.stack([wa[d:], wb[d:]], 1)),
        "in_vb": vb,
        "in_colv": np.ascontiguousarray(np.stack([a["L1_gnn_" + k] for k in names], 1)),
        "in_rows": np.concatenate([a["L0_gnn_b_gcnb"], a["L2_gnn_b"], a["L3_gnn_bias"], a["L0_gnn_ba"],
                                   a["L0_gnn_bb"]])[None],
    }
    nc = bacc.Bacc("TRN2", target_bir_lowering=False, num_devices=1)
    ap = {k: nc.dram_tensor(k, v.shape, mybir.dt.from_np(v.dtype), kind="ExternalInput").ap()
          for k, v in arrays.items()}
    out = nc.dram_tensor("out_0", (n, d), F32, kind="ExternalOutput").ap()
    gnn_stack(nc, ap["in_x"], ap["in_adj_t"], ap["in_mats"], ap["in_blocks"],
              {k: ap["in_" + k] for k in ("a2", "gw", "wr", "vb", "colv")}, ap["in_rows"], out)
    return run_bass_kernel_spmd(nc, [arrays], core_ids=[0]).results[0]["out_0"]
```

```python
from contextlib import ExitStack

import concourse.bass as bass
from concourse import mybir

F32 = mybir.dt.float32
F16 = mybir.dt.float16
ALU = mybir.AluOpType
ACT = mybir.ActivationFunctionType
AX_X = mybir.AxisListType.X
ds = bass.ds

P = 128
LN_EPS = 1e-5
BN_EPS = 1e-6
L0_EPS = 1e-5
ADJ_EPS = 1e-8
NORM_EPS = 1e-8


def gnn_stack(nc, x_in, adj_t, weights, blocks, cols, rows, out):
    N = out.shape[0]
    D = out.shape[1]
    T = -(-N // P)
    NP = T * P
    W = adj_t.shape[1]
    NC = 3
    C = W // NC
    LAST = N - (T - 1) * P
    F = D // P
    H = 4
    DH = D // H
    RING = 4
    assert F == 2 and C * NC == W and C <= 512 and W >= N
    (W_SA, W_SA_T, MLP_E, MLP_D, W_L2, W_L3) = range(6)
    (W_BD, W_BD_T) = range(2)
    (E_G, E_B, EM_B, EM_G, EM_BB, DM_B, DM_G, DM_BB) = range(8)
    R_GCNB, R_L2B, R_L3B, R_BA = 0, D, 2 * D, 3 * D
    NR = 3 * D + 2

    with ExitStack() as ctx:
        def sb(name, width, dt=F32):
            return ctx.enter_context(nc.sbuf_tensor("sb_" + name, [P, width], dt))

        def sem(name):
            return ctx.enter_context(nc.semaphore(name))

        at = sb("adj_t", T * W, F16)
        x = sb("x", T * D)
        h = sb("h", T * D)
        shared = sb("shared", T * D + 2 * NP)
        h_hi = shared[:, 0:T * D // 2].bitcast(F16)
        h_lo = shared[:, T * D // 2:T * D].bitcast(F16)
        s_acc = shared[:, T * D:T * D + NP]
        d_acc = shared[:, T * D + NP:T * D + NP + NP // 2].bitcast(F16)
        back = shared[:, 0:RING * W]
        ht = sb("ht", F * NP)
        ga = sb("ga", F * NP)
        gb = sb("gb", F * NP)
        rinv = sb("rinv", F * NP)
        frow = sb("frow", H * W)
        tt = sb("tt", 3 * W)
        ring = sb("ring", RING * W)
        vs = sb("vs", 2 * 2 * P * F)
        wt = sb("wt", 6 * F * D)
        DG = D + 2
        wg = sb("wg", F * DG)
        wbd = sb("wbd", 2 * F * P)
        colv = sb("colv", F * 8)
        rowv = sb("rowv", NR)
        smallw = sb("smallw", F * (2 + 8 + 3))
        a2 = smallw[:, 0:F * 2]
        vb = smallw[:, F * 2:F * 10]
        r3 = smallw[:, F * 10:F * 13]
        c0 = sb("c0", F * 2)
        c1 = sb("c1", F * 8)
        f2 = sb("f2", H * T)
        ident = sb("ident", P)
        ones = sb("ones", P)
        ones16 = sb("ones16", 2, F16)
        rcol = sb("rcol", 2 * T)
        rbc = gb[:, 0:T * P]
        ncol = sb("ncol", 4 * F)
        stats = sb("stats", T * 6)
        lnt = sb("lnt", 6 * T)
        rstd = sb("rstd", T)
        nmr = sb("nmr", T)
        mhalf = sb("mhalf", T)
        epsv = sb("epsv", T)
        nodev = sb("nodev", 16 * T)
        bnst = sb("bnst", F * NC * 6)
        bnag = sb("bnag", F * 2)
        bnv = sb("bnv", F * 4)
        e_t = sb("e_t", 2 * D)
        cb = e_t
        e_q = sb("e_q", 2 * D)
        e_pair = (e_t, e_q)
        ps = ctx.enter_context(nc.psum_tensor("ps", [P, 8, 512], F32))

        gab, gates, attn, rs, ca, dinv, dmax, deg1, srt, sr99, n2, nsum, ndeg1 = (
            nodev[:, 0:2 * T], nodev[:, 2 * T:4 * T], nodev[:, 4 * T:6 * T], nodev[:, 6 * T:7 * T],
            nodev[:, 7 * T:8 * T], nodev[:, 8 * T:9 * T], nodev[:, 9 * T:10 * T], nodev[:, 10 * T:11 * T],
            nodev[:, 11 * T:12 * T], nodev[:, 12 * T:13 * T], nodev[:, 13 * T:14 * T], nodev[:, 14 * T:15 * T],
            nodev[:, 15 * T:16 * T])

        psf = ps[:, :, :].rearrange("p b n -> p (b n)")
        TR = -(-T // 2)
        NCONST = 8
        spill = nc.dram_tensor("spill", [2 * T * P, W], F32, kind="Internal").ap()

        def fm(a, width=NP):
            return a[:, :].rearrange("p (f n) -> p f n", f=F)

        def chunks(a, f=0, width=NP):
            return a[:, f * width:f * width + W].rearrange("p (c n) -> p c n", c=NC)

        adj_ld = [sem(f"adj_loaded{j}") for j in range(T)]
        cast_dve, cast_act = sem("adj_cast_by_vector"), sem("adj_cast_by_scalar")
        x_ld = [sem(f"x_loaded{k}") for k in range(3)]
        accs_zero = sem("accs_zero")
        diag_added, diag_removed = sem("diagonal_added"), sem("diagonal_removed")
        xb_mm, xb_added, xb_scaled, sums_mm = sem("xb_mm"), sem("xb_added"), sem("xb_scaled"), sem("sums_mm")
        w_loaded = sem("w_loaded")
        w0_loaded, wl0_loaded = sem("w0_loaded"), sem("w_l0_loaded")
        consts = sem("consts_ready")
        stats_done = sem("stats_done")
        x_done = sem("x_done")
        lnvar = sem("ln_var")
        lnpow = sem("ln_pow")
        h_done = sem("h_done")
        h16_hi = sem("h_high_part")
        h16_done = sem("h16_done")
        tr_done = sem("transposed")
        tr_copied = sem("transposes_copied")
        dve_own = sem("dve_own")
        act_own = sem("act_own")
        pool_own = sem("pool_own")
        c0_mm, c0_copied, r3_mm, r3_copied, srow_mm, srow_copied = (
            sem("c0_mm"), sem("c0_copied"), sem("r3_mm"), sem("r3_copied"), sem("srow_mm"), sem("srow_copied"))
        cb_ready = sem("cb_ready")
        agg_done, agg_copied = sem("aggregated"), sem("aggregate_copied")
        tile_arg, tile_tanh, tile_exp, tile_masked, tile_used, tile_summed = (
            sem("tile_arg"), sem("tile_tanh"), sem("tile_exp"), sem("tile_masked"), sem("tile_used"), sem("tile_summed"))
        vs_ready = sem("values_ready")
        gate_mm, gate_sum, gate_tanh, gate_attn, dinv_ready = (
            sem("gate_mm"), sem("gate_sum"), sem("gate_tanh"), sem("gate_attn"), sem("dinv_ready"))
        np_mm, np_mixed, np_act, np_done = (
            sem("node_product"), sem("node_mixed"), sem("node_act"), sem("node_done"))
        f_mm, f_even_copied, f_odd_copied = sem("f_mm"), sem("f_even_copied"), sem("f_odd_copied")
        head_copied = sem("head_copied")
        norm_ready, proj_mm, bn_var, bn_pow, bn_cols, aff_done, mlp_mm, mlp_min, mlp_act, mlp_sum = (
            sem("normalised"), sem("proj_mm"), sem("bn_var"), sem("bn_pow"), sem("bn_cols"), sem("affine_done"),
            sem("mlp_mm"), sem("mlp_min"), sem("mlp_act"), sem("mlp_sum"))
        sim_mm, sim_exp, nrm_done, nrm_pow, hn_done, hn_copied = (
            sem("sim_mm"), sem("sim_exp"), sem("norm_done"), sem("norm_pow"), sem("hn_done"), sem("hn_copied"))
        out_stored = sem("out_stored")
        f2_mm, f2_copied, c1_mm, dec_ready, hn_mm, hi_done, sq_done, bias_done, s3_mm = (
            sem("f2_mm"), sem("f2_copied"), sem("c1_mm"), sem("dec_ready"), sem("hn_mm"), sem("hi_done"),
            sem("sq_done"), sem("bias_done"), sem("s3_mm"))
        NW0, NWL0, NWR = 4, 2, 8
        X_CUTS = (0, 3, 6, T)
        CD = 4
        landing = ([ring[:, k * W:(k + 1) * W] for k in range(RING)] + [tt[:, k * W:(k + 1) * W] for k in range(3)]
                   + [a[:, f * NP:f * NP + W] for a in (rinv, gb, ga) for f in range(F)])[:T]
        xb = shared[:, 0:T * D]
        HALVES = ((0, 6), (6, T))
        saved, ring_saved, loaded = [sem("saved0"), sem("saved1")], sem("ring_saved"), [sem("loaded0"), sem("loaded1")]
        misc_mm, misc_read, frow_ready, rbc_ready, norm_dec = (
            sem("misc_mm"), sem("misc_read"), sem("frow_ready"), sem("rbc_ready"), sem("norm_dec"))
        num_copied, elu_relu, elu_exp, aff_act, aff_dve, ncol_ready = (
            sem("num_copied"), sem("elu_relu"), sem("elu_exp"), sem("aff_act"), sem("aff_dve"), sem("ncol_ready"))
        F2_PARTS = ((0, 0, 2), (0, 2, T), (1, 0, T))
        MISC = ([("f2", 0)] + [("frow", 0, c) for c in range(NC)] + [("f2", 1)]
                + [("frow", 1, c) for c in range(NC)] + [("f2", 2)]
                + [("frow", 2, c) for c in range(NC)] + [("frow", 3, c) for c in range(NC)]
                + [(k, pr, c) for pr in range(2) for k, n in (("sums", 2), ("spread", NC)) for c in range(n)])
        SR = DH + 1
        ST = 512 // SR

        N0, NE, ND, N3 = T, H * T, 2 * T, T
        B0, BE, BD, B3 = 0, N0, N0 + NE, N0 + NE + ND

        block = ctx.enter_context(nc.Block())

        @block.sync
        def _(sp):
            for k in range(3):
                a, b = X_CUTS[k], X_CUTS[k + 1]
                sp.dma_start(x[:, a * D:b * D].rearrange("p (t d) -> p t d", d=D),
                             x_in[a * P:b * P, :].rearrange("(t p) d -> p t d", p=P)).then_inc(x_ld[k], 16)

            def load_w(dst, src, s):
                sp.dma_start(dst.rearrange("p (f n) -> p f n", f=F),
                             src.rearrange("(f p) n -> p f n", p=P)).then_inc(s, 16)

            load_w(a2, cols["a2"], w0_loaded)
            load_w(wt[:, W_SA_T * F * D:(W_SA_T + 1) * F * D], weights[W_SA_T], w0_loaded)
            sp.dma_start(r3.rearrange("p (f n) -> p f n", f=F)[:, :, 0:2],
                         cols["wr"].rearrange("(f p) n -> p f n", p=P)).then_inc(w0_loaded, 16)
            for j in range(T):
                sp.dma_start(landing[j], adj_t[j * P:(j + 1) * P, :]).then_inc(adj_ld[j], 16)
                if j == 1:
                    sp.dma_start(rowv[:, :], rows.partition_broadcast(P)).then_inc(w0_loaded, 16)
            load_w(wg[:, :], cols["wg"], wl0_loaded)
            load_w(wt[:, W_SA * F * D:(W_SA + 1) * F * D], weights[W_SA], wl0_loaded)
            for i in (MLP_E, MLP_D, W_L2, W_L3):
                load_w(wt[:, i * F * D:(i + 1) * F * D], weights[i], w_loaded)
            for i in range(2):
                load_w(wbd[:, i * F * P:(i + 1) * F * P], blocks[i], w_loaded)
            load_w(vb, cols["vb"], w_loaded)
            load_w(colv[:, :], cols["colv"], w_loaded)
            sp.sem_inc(ring_saved, BE)
            k = 0
            for hd in range(H):
                if hd % 2:
                    with sp.Fori(0, T) as j:
                        sp.wait_ge(tile_masked, BE + hd * T + j + 1)
                        sp.sem_inc(ring_saved, 1)
                    continue
                for j in range(T):
                    slot = (BE + hd * T + j) % RING
                    sp.wait_ge(tile_masked, BE + hd * T + j + 1)
                    sp.dma_start(spill[k * P:(k + 1) * P, :], ring[:, slot * W:(slot + 1) * W])\
                      .then_inc(saved[k % 2], 16)
                    if j:
                        sp.wait_ge(saved[(k - 1) % 2], 16 * ((k - 1) // 2 + 1))
                        sp.sem_inc(ring_saved, 1)
                    k += 1
                sp.wait_ge(saved[(k - 1) % 2], 16 * ((k - 1) // 2 + 1))
                sp.sem_inc(ring_saved, 1)
            for k in range(2 * T):
                if k >= 2:
                    sp.wait_ge(loaded[k % 2], 16 * (k // 2))
                if k >= RING:
                    sp.wait_ge(tile_used, BD + k - RING + 1)
                slot = k % RING
                sp.dma_start(back[:, slot * W:(slot + 1) * W], spill[k * P:(k + 1) * P, :])\
                  .then_inc(loaded[k % 2], 16)
            for a, b in ((0, 4), (4, 8), (8, T - 1)):
                sp.wait_ge(np_done, 2 * TR + b)
                sp.dma_start(out[a * P:b * P, :].rearrange("(t p) d -> p t d", p=P),
                             x[:, a * D:b * D].rearrange("p (t d) -> p t d", d=D)).then_inc(out_stored, 16)
            sp.wait_ge(np_done, 2 * TR + T)
            sp.dma_start(out[(T - 1) * P:N, :], x[0:LAST, (T - 1) * D:T * D]).then_inc(out_stored, 16)
            sp.wait_ge(out_stored, 64)


        @block.gpsimd
        def _(pool):
            own = [0]

            def link(ins):
                own[0] += 1
                ins.then_inc(pool_own, 1)
                pool.wait_ge(pool_own, own[0])

            link(pool.memset(ident[:, :], 0.0))
            link(pool.memset(epsv[:, :], ADJ_EPS))
            pool.affine_select(out=ident[:, :], in_=ident[:, :], compare_op=ALU.not_equal, fill=1.0, base=0,
                               pattern=[[-1, P]], channel_multiplier=1).then_inc(consts, 1)
            pool.affine_select(out=epsv[:, T - 1:T], in_=epsv[:, T - 1:T], compare_op=ALU.is_ge, fill=0.0,
                               base=LAST - 1, pattern=[[0, 1]], channel_multiplier=-1).then_inc(consts, 1)
            pool.memset(ones[:, :], 1.0).then_inc(consts, 1)
            pool.memset(ones16[:, :], 1.0).then_inc(consts, 1)
            pool.memset(mhalf[:, :], -0.5).then_inc(consts, 1)
            for a, v in ((ga, 0.0), (gb, 0.0), (rinv, 1.0)):
                pool.memset(fm(a)[:, :, W:NP], v).then_inc(consts, 1)
            pool.wait_ge(consts, NCONST)

            def norm_power(layer):
                for k, (a, b) in enumerate(HALVES):
                    pool.wait_ge(lnvar, 2 * layer + k + 1)
                    link(pool.tensor_tensor(rstd[:, a:b], lnt[:, 4 * T + a:4 * T + b], mhalf[:, a:b], ALU.pow))
                    pool.tensor_tensor(nmr[:, a:b], lnt[:, 5 * T + a:5 * T + b], rstd[:, a:b], ALU.mult)\
                        .then_inc(lnpow, 1)

            def batch_power(k):
                for f in range(F):
                    pool.wait_ge(bn_var, F * k + f + 1)
                    pool.tensor_tensor(bnv[:, f:f + 1], bnv[:, f:f + 1], mhalf[:, 0:1], ALU.pow).then_inc(bn_pow, 1)

            def node_values(j, base):
                pool.wait_ge(tile_used, base + j - 1)
                pool.tensor_copy(vs[:, ds((j % 2) * D, D)], h[:, ds(j * D, D)]).then_inc(vs_ready, 1)

            def sum_weights(j, base, before):
                pool.wait_ge(tile_masked, base + j + 1)
                pool.wait_ge(tile_summed, before + j)
                pool.tensor_tensor(s_acc[:, 0:W], s_acc[:, 0:W], ring[:, ds(((base + j) % RING) * W, W)],
                                   ALU.add).then_inc(tile_summed, 1)

            norm_power(0)
            pool.memset(s_acc[:, :], 0.0).then_inc(accs_zero, 1)
            pool.memset(d_acc[:, :], 0.0).then_inc(accs_zero, 1)
            pool.wait_ge(accs_zero, 2)

            def sum_adjacency(j):
                pool.tensor_tensor(d_acc[:, 0:W], d_acc[:, 0:W], at[:, ds(j * W, W)],
                                   ALU.add).then_inc(tile_summed, 1)
                pool.wait_ge(tile_summed, j + 1)

            with pool.Fori(0, CD) as j:
                pool.wait_ge(cast_dve, j + 1)
                sum_adjacency(j)
            with pool.Fori(CD, T) as j:
                pool.wait_ge(cast_act, j - CD + 1)
                sum_adjacency(j)
            pool.wait_ge(h_done, T)
            for j in range(2):
                pool.tensor_copy(vs[:, j * D:(j + 1) * D], h[:, j * D:(j + 1) * D]).then_inc(vs_ready, 1)
                sum_weights(j, B0, T)
            with pool.Fori(2, T) as j:
                node_values(j, B0)
                sum_weights(j, B0, T)

            norm_power(1)
            pool.wait_ge(tile_used, B0 + N0)
            link(pool.memset(vs[:, :], 1.0))
            pool.wait_ge(h_done, 2 * T)
            for hd in range(H):
                with pool.Fori(0, T) as j:
                    pool.wait_ge(tile_used, BE + hd * T + j - 1)
                    pool.tensor_copy(vs[:, ds(((hd * T + j) % 2) * P + (hd % 2) * (2 * P + DH), DH)],
                                     h[:, ds(j * D + hd * DH, DH)]).then_inc(vs_ready, 1)
            batch_power(0)
            batch_power(1)
            pool.wait_ge(tr_copied, 3 * TR)
            pool.wait_ge(tile_used, BE + NE)
            for pr in range(2):
                with pool.Fori(0, T) as j:
                    pool.wait_ge(tile_used, BD + pr * T + j - 1)
                    pool.tensor_copy(vs[:, ds(((pr * T + j) % 2) * P, P)],
                                     h[:, ds(j * D + pr * P, P)]).then_inc(vs_ready, 1)
            batch_power(2)
            norm_power(2)
            pool.wait_ge(tile_used, BD + ND)
            pool.memset(s_acc[:, :], 0.0).then_inc(tile_summed, 1)
            norm_power(3)
            for k, (a, b) in enumerate(HALVES):
                pool.wait_ge(nrm_done, k + 1)
                pool.tensor_tensor(nsum[:, a:b], n2[:, a:b], mhalf[:, a:b], ALU.pow).then_inc(nrm_pow, 1)
            pool.wait_ge(hn_copied, T)
            pool.wait_ge(tile_used, B3)
            with pool.Fori(0, T) as j:
                node_values(j, B3)
                sum_weights(j, B3, 2 * T + 1)

        @block.scalar
        def _(act):
            act.preload_act_table(ACT.Exp)
            act.wait_ge(consts, NCONST)

            def norm_apply(layer, halves=(0, 1), split=False):
                for k in halves:
                    a, b = HALVES[k]
                    act.wait_ge(lnpow, 2 * layer + k + 1)
                    for t in range(a, b):
                        act.activation(h[:, t * D:(t + 1) * D], x[:, t * D:(t + 1) * D], ACT.Relu,
                                       bias=nmr[:, t:t + 1], scale=rstd[:, t:t + 1]).then_inc(h_done, 1)
                    if split:
                        act.wait_ge(h_done, T * layer + b)
                        act.activation(h_hi[:, a * D:b * D], h[:, a * D:b * D], ACT.Copy).then_inc(h16_hi, 1)

            def copy_aggregate(done, count, dst):
                act.wait_ge(done, count)
                act.activation(chunks(dst), ps[:, 0:NC, 0:C], ACT.Copy).then_inc(agg_copied, 1)

            norm_apply(0, split=True)
            for j in range(CD, T):
                if j == CD + 3:
                    act.wait_ge(srow_mm, 1)
                    act.activation(chunks(frow, 0, W), ps[:, 2:2 + NC, 0:C], ACT.Copy).then_inc(srow_copied, 1)
                act.wait_ge(adj_ld[j], 16)
                act.activation(at[:, j * W:(j + 1) * W], landing[j], ACT.Copy).then_inc(cast_act, 1)
            act.wait_ge(r3_copied, 4)

            def score_exp(j):
                act.wait_ge(tile_arg, j + 1)
                act.wait_ge(r3_copied, 4)
                act.activation(ring[:, ds((j % RING) * W, W)], tt[:, ds((j % 2) * W, W)], ACT.Exp,
                               bias=srt[:, ds(j, 1)], scale=-1.0).then_inc(tile_exp, 1)

            act.wait_ge(cast_dve, CD)
            with act.Fori(0, RING) as j:
                score_exp(j)
            copy_aggregate(agg_done, 1, ga)
            act.wait_ge(xb_added, 2 * T)
            act.activation(gates, gates, ACT.Tanh, scale=0.5).then_inc(gate_tanh, 1)
            with act.Fori(0, T) as t:
                act.wait_ge(gate_attn, 1)
                act.activation(xb[:, ds(t * D, D)], xb[:, ds(t * D, D)], ACT.Copy,
                               scale=attn[:, ds(t + T, 1)]).then_inc(xb_scaled, 1)
            with act.Fori(RING, T) as j:
                act.wait_ge(tile_used, j - RING + 1)
                act.wait_ge(tile_summed, T + j - RING + 1)
                score_exp(j)
            copy_aggregate(tile_used, B0 + T, gb)
            for r in range(TR):
                act.wait_ge(np_mixed, min(2 * r + 2, T))
                e = e_pair[r % 2][:, 0:min(2, T - 2 * r) * D]
                act.activation(e, e, ACT.Tanh, scale=0.5).then_inc(np_act, 1)
                if r == TR - 2:
                    norm_apply(1, (0,))
            norm_apply(1, (1,))


            def tanh(base, m, head_of, node_of):
                act.activation(tt[:, ds((m % 3) * W, W)], frow[:, ds(head_of(m) * W, W)], ACT.Tanh,
                               bias=f2[:, ds(head_of(m) * T + node_of(m), 1)], scale=0.5).then_inc(tile_tanh, 1)

            def exp(base, m):
                act.wait_ge(tile_tanh, base - BE + m + 1)
                act.wait_ge(tile_used, base + m - RING + 1)
                act.wait_ge(ring_saved, BE + NE if base == BD else base + m - RING + 1)
                act.wait_ge(f2_copied, 1)
                act.activation(ring[:, ds(((base + m) % RING) * W, W)], tt[:, ds((m % 3) * W, W)], ACT.Exp,
                               scale=0.5).then_inc(tile_exp, 1)

            def tiles(base, a, b, head_of, node_of, f2_parts):
                with act.Fori(a, b) as m:
                    act.wait_ge(tile_exp, base + m - 1)
                    if base == BE:
                        act.wait_ge(frow_ready, NC * ((m + 1) // T) + NC)
                    act.wait_ge(f2_copied, f2_parts)
                    tanh(base, m + 1, head_of, node_of)
                    exp(base, m)

            def batch_affine(k, dst, src):
                act.wait_ge(bn_cols, F * k + 1)
                act.activation(chunks(dst), src, ACT.Identity, bias=bnv[:, 2 * F:2 * F + 1],
                               scale=bnv[:, F:F + 1]).then_inc(aff_act, 1)

            def elu_exp_part(n, f, nbias, ready, count):
                e = frow[:, 2 * f * W:(2 * f + 1) * W]
                act.wait_ge(ready, count)
                act.activation(e.rearrange("p (c n) -> p c n", c=NC), ps[:, f * NC:(f + 1) * NC, 0:C], ACT.Relu,
                               bias=nbias, scale=-1.0).then_inc(elu_relu, 1)
                act.wait_ge(elu_relu, n + 1)
                act.activation(e, e, ACT.Exp, scale=-1.0).then_inc(elu_exp, 1)

            by_head = (lambda m: m // T, lambda m: m % T)
            act.wait_ge(frow_ready, NC)
            act.wait_ge(f2_copied, 1)
            tanh(BE, 0, *by_head)
            tiles(BE, 0, 1, *by_head, 1)
            tiles(BE, 1, 2 * T - 1, *by_head, 2)
            tiles(BE, 2 * T - 1, NE - 1, *by_head, 3)
            exp(BE, NE - 1)
            act.wait_ge(tile_used, BE + NE)
            act.activation(chunks(ga, 1)[DH:P], ps[DH:P, NC:2 * NC, 0:C], ACT.Copy).then_inc(num_copied, 1)
            odd_heads = (lambda m: 2 * (m // T) + 1, lambda m: m % T)
            tanh(BD, 0, *odd_heads)
            tiles(BD, 0, RING, *odd_heads, 3)
            batch_affine(0, gb, ps[:, 0:NC, 0:C])
            act.wait_ge(ncol_ready, 1)
            for f in range(F):
                elu_exp_part(f, f, ncol[:, f:f + 1], mlp_mm, f + 1)
            batch_affine(1, ht, chunks(ga))
            for r in range(TR):
                act.wait_ge(tr_done, 2 * TR + r + 1)
                k = min(2, T - 2 * r) * D
                act.activation(h[:, 2 * r * D:2 * r * D + k], ps[:, 6 + r % 2, 0:k], ACT.Copy).then_inc(tr_copied, 1)
            SPLIT = T + 6
            tiles(BD, RING, SPLIT, *odd_heads, 3)
            elu_exp_part(F, 0, 0.0, proj_mm, F + 1)
            tiles(BD, SPLIT, ND - 1, *odd_heads, 3)
            exp(BD, ND - 1)
            elu_exp_part(F + 1, 1, 0.0, proj_mm, F + 2)
            for f in range(F):
                elu_exp_part(2 * F + f, f, ncol[:, 2 * F + f:2 * F + f + 1], mlp_mm, F + f + 1)
            batch_affine(2, ht, chunks(ga))

            norm_apply(2, split=True)
            copy_aggregate(agg_done, 2, ga)
            norm_apply(3)
            with act.Fori(0, T) as t:
                act.wait_ge(hn_mm, t + 1)
                act.wait_ge(tr_copied, 5 * TR)
                act.activation(h[:, ds(t * D, D)], psf[:, ds((t % 2) * 512, D)], ACT.Copy).then_inc(hn_copied, 1)
            for r in range(TR):
                act.wait_ge(tr_done, 5 * TR + r + 1)
                k = min(2, T - 2 * r)
                act.activation(fm(h_hi)[:, :, 2 * r * P:(2 * r + k) * P],
                               ps[:, 6 + r % 2, 0:F * 2 * P].rearrange("p (f n) -> p f n", f=F)[:, :, 0:k * P],
                               ACT.Copy).then_inc(hi_done, 1)
            with act.Fori(0, T) as j:
                act.wait_ge(tile_used, B3 + j - RING + 1)
                act.wait_ge(tile_summed, 2 * T + 1 + j - RING + 1)
                for c in range(NC):
                    act.wait_ge(sim_mm, NC * j + c + 1)
                    act.wait_ge(hi_done, TR)
                    act.activation(ring[:, ds(((B3 + j) % RING) * W + c * C, C)],
                                   psf[:, ds((6 + (j + c) % 2) * 512, C)], ACT.Exp).then_inc(sim_exp, 1)
            copy_aggregate(tile_used, B3 + T, ga)

        @block.vector
        def _(dve):
            own = [0]

            def link(ins):
                own[0] += 1
                ins.then_inc(dve_own, 1)
                dve.wait_ge(dve_own, own[0])

            def note(ins):
                own[0] += 1
                ins.then_inc(dve_own, 1)

            def row_stats(t):
                dve.bn_stats(stats[:, ds(t * 6, 6)], x[:, ds(t * D, D)]).then_inc(stats_done, 1)

            def norm_half(layer, half):
                a, b = HALVES[half]
                dve.wait_ge(stats_done, T * layer + b)
                s = stats[:, :].rearrange("p (t k) -> p k t", k=6)[:, :, a:b]
                total, diff, m2, d2, var, nmean = (lnt[:, k * T + a:k * T + b] for k in range(6))
                note(dve.tensor_tensor(total, s[:, 1], s[:, 4], ALU.add))
                note(dve.tensor_tensor(diff, s[:, 1], s[:, 4], ALU.subtract))
                link(dve.tensor_tensor(m2, s[:, 2], s[:, 5], ALU.add))
                note(dve.tensor_tensor(d2, diff, diff, ALU.mult))
                note(dve.tensor_scalar(nmean, total, -0.5, None, ALU.mult))
                link(dve.tensor_scalar(m2, m2, 1.0 / D, LN_EPS, ALU.mult, ALU.add))
                dve.scalar_tensor_tensor(var, d2, 0.25, m2, ALU.mult, ALU.add).then_inc(lnvar, 1)

            def round_stats(layer, r):
                for t in range(2 * r, min(2 * r + 2, T)):
                    row_stats(t)
                    for half, (a, b) in enumerate(HALVES):
                        if t == b - 1:
                            norm_half(layer, half)

            def copy_transposes(batch, dst):
                for r in range(TR):
                    dve.wait_ge(tr_done, batch * TR + r + 1)
                    k = min(2, T - 2 * r) * P
                    dve.tensor_copy(fm(dst)[:, :, 2 * r * P:2 * r * P + k],
                                    ps[:, 6 + r % 2, 0:F * 2 * P].rearrange("p (f n) -> p f n", f=F)[:, :, 0:k])\
                       .then_inc(tr_copied, 1)

            def copy_aggregate(done, count, dst):
                dve.wait_ge(done, count)
                dve.tensor_copy(chunks(dst, 1), ps[:, NC:2 * NC, 0:C]).then_inc(agg_copied, 1)

            def on_diagonal(values, done, tiles=range(T)):
                for j in tiles:
                    d = at[:, j * W + j * P:j * W + min((j + 1) * P, W)]
                    dve.scalar_tensor_tensor(d, ident[:, 0:d.shape[1]], values[:, j:j + 1], d, ALU.mult,
                                             ALU.add).then_inc(done, 1)

            for k in range(3):
                dve.wait_ge(x_ld[k], 16)
                for t in range(X_CUTS[k], X_CUTS[k + 1]):
                    row_stats(t)
                if k:
                    norm_half(0, k - 1)

            def cast(j):
                dve.wait_ge(adj_ld[j], 16)
                dve.tensor_copy(at[:, j * W:(j + 1) * W], landing[j]).then_inc(cast_dve, 1)

            def low_parts(layer):
                for k, (a, b) in enumerate(HALVES):
                    dve.wait_ge(h16_hi, 2 * layer + k + 1)
                    dve.tensor_tensor(h_lo[:, a * D:b * D], h[:, a * D:b * D], h_hi[:, a * D:b * D],
                                      ALU.subtract).then_inc(h16_done, 1)

            cast(0)
            dve.wait_ge(c0_mm, 1)
            link(dve.tensor_copy(c0[:, :], ps[:, 0, 0:F * 2]))
            r3v = r3.rearrange("p (f n) -> p f n", f=F)
            c0v = c0[:, :].rearrange("p (f n) -> p f n", f=F)
            dve.wait_ge(w0_loaded, 16 * NW0)
            dve.tensor_copy(r3v[:, :, 2:3], c0v[:, :, 1:2]).then_inc(c0_copied, 1)
            dve.wait_ge(consts, NCONST)
            for f in range(F):
                dve.tensor_scalar(cb[:, f * P:(f + 1) * P], ones[:, :], c0[:, f * 2:f * 2 + 1], None, ALU.mult)\
                   .then_inc(cb_ready, 1)
            cast(1)
            copy_transposes(0, ht)
            cast(2)
            low_parts(0)
            cast(3)
            dve.wait_ge(srow_mm, 1)
            dve.wait_ge(srow_copied, 1)
            dve.tensor_scalar(chunks(frow, 1, W), ps[:, 2:2 + NC, 0:C], 0.01, None, ALU.mult)\
               .then_inc(srow_copied, 1)
            dve.wait_ge(r3_mm, 1)
            pr3 = ps[:, 7, 0:3 * T].rearrange("p (t k) -> p k t", k=3)
            dve.tensor_scalar(srt, pr3[:, 2], -0.01, None, ALU.mult).then_inc(r3_copied, 1)
            dve.tensor_scalar(sr99, pr3[:, 2], 0.99, None, ALU.mult).then_inc(r3_copied, 1)
            for k in range(2):
                dve.tensor_scalar(gab[:, k * T:(k + 1) * T], pr3[:, k], rowv[:, R_BA + k:R_BA + k + 1], None,
                                  ALU.add).then_inc(r3_copied, 1)
            dve.wait_ge(srow_copied, 2)
            dve.wait_ge(r3_copied, 4)

            def score_arg(j):
                dve.scalar_tensor_tensor(tt[:, ds((j % 2) * W, W)], frow[:, 0:W], sr99[:, ds(j, 1)],
                                         frow[:, W:2 * W], ALU.add, ALU.max).then_inc(tile_arg, 1)

            def mask(n, j):
                dve.wait_ge(tile_exp, n + 1)
                w = ring[:, ds((n % RING) * W, W)]
                dve.tensor_tensor(w, w, at[:, ds(j * W, W)], ALU.mult).then_inc(tile_masked, 1)

            dve.wait_ge(cast_act, min(3, T - CD))
            score_arg(0)
            with dve.Fori(1, RING + 1) as j:
                score_arg(j)
                mask(j - 1, j - 1)
            copy_aggregate(agg_done, 1, ga)
            for t in range(T):
                dve.wait_ge(xb_mm, t + 1)
                dve.tensor_tensor(xb[:, t * D:(t + 1) * D], ps[:, 6 + t % 2, 0:D], rowv[:, R_GCNB:R_GCNB + D],
                                  ALU.add).then_inc(xb_added, 1)
                dve.tensor_tensor(gates.rearrange("p (k t) -> p t k", k=2)[:, t], ps[:, 6 + t % 2, D:DG],
                                  gab.rearrange("p (k t) -> p t k", k=2)[:, t], ALU.add).then_inc(xb_added, 1)
            dve.wait_ge(gate_tanh, 1)
            dve.tensor_scalar(attn, gates, 0.5, 0.5, ALU.mult, ALU.add).then_inc(gate_attn, 1)
            with dve.Fori(RING + 1, T) as j:
                score_arg(j)
                mask(j - 1, j - 1)
            mask(T - 1, T - 1)
            link(dve.tensor_scalar(x[:, :], x[:, :], 0.5, None, ALU.add))
            copy_aggregate(tile_used, B0 + T, gb)
            dve.wait_ge(sums_mm, 1)
            link(dve.tensor_scalar(rs, ps[:, 6, 2 * T:3 * T], L0_EPS, None, ALU.add))
            link(dve.reciprocal(rs, rs))
            link(dve.tensor_tensor(ca, attn[:, 0:T], rs, ALU.mult))
            dve.wait_ge(xb_scaled, T)

            def l0_mix(r):
                dve.wait_ge(np_mm, r + 1)
                for u in range(min(2, T - 2 * r)):
                    t = 2 * r + u
                    dve.scalar_tensor_tensor(e_pair[r % 2][:, u * D:(u + 1) * D], ps[:, r % 4, u * D:(u + 1) * D],
                                             ca[:, t:t + 1], xb[:, t * D:(t + 1) * D], ALU.mult, ALU.add)\
                       .then_inc(np_mixed, 1)

            def degrees():
                link(dve.tensor_scalar(dmax, ps[:, 6, 3 * T:4 * T], 1.0, None, ALU.max))
                link(dve.reciprocal(dinv, dmax))
                note(dve.tensor_scalar(deg1, dmax, 1.0, None, ALU.add))
                link(dve.tensor_scalar(ndeg1, dmax, -1.0, -1.0, ALU.mult, ALU.add))
                dve.sem_inc(dinv_ready, 1)

            l0_mix(0)
            for r in range(TR):
                if r == 1:
                    degrees()
                if r:
                    dve.wait_ge(np_done, r)
                if r + 1 < TR:
                    l0_mix(r + 1)
                if r:
                    round_stats(1, r - 1)
                a, k = 2 * r * D, min(2, T - 2 * r) * D
                dve.wait_ge(np_act, r + 1)
                dve.scalar_tensor_tensor(x[:, a:a + k], e_pair[r % 2][:, 0:k], 0.5, x[:, a:a + k], ALU.mult,
                                         ALU.add).then_inc(np_done, 1)
            dve.wait_ge(np_done, TR)
            round_stats(1, TR - 1)

            dve.wait_ge(c1_mm, 1)
            link(dve.tensor_copy(c1[:, :], ps[:, 0, 0:F * 8]))
            for hd in range(H):
                dve.tensor_scalar(cb[:, hd * P:(hd + 1) * P], ones[:, :],
                                  c1[:, (hd // 2) * 8 + 2 * hd:(hd // 2) * 8 + 2 * hd + 1], None, ALU.mult)\
                   .then_inc(cb_ready, 1)
            dve.wait_ge(w_loaded, 16 * NWR)
            cv = colv[:, :].rearrange("p (f k) -> p k f", k=8)
            for k, i in enumerate((EM_B, DM_B)):
                note(dve.tensor_scalar(ncol[:, k * F * 1:(k + 1) * F * 1] if k == 0 else ncol[:, 2 * F:3 * F],
                                       cv[:, i], -1.0, None, ALU.mult))
            for k, i in enumerate((EM_B, DM_B)):
                link(dve.tensor_scalar(ncol[:, (2 * k + 1) * F:(2 * k + 2) * F], cv[:, i], -1.0, -1.0, ALU.mult,
                                       ALU.add))
            dve.sem_inc(ncol_ready, 1)
            copy_transposes(1, ht)

            def misc(*name):
                u = MISC.index(name)
                dve.wait_ge(misc_mm, u + 1)
                return 6 + u % 2

            def copy_frow(hd):
                for c in range(NC):
                    b = misc("frow", hd, c)
                    a = hd * W + c * C
                    dve.tensor_copy(frow[:, a:a + C], ps[:, b, 0:C]).then_inc(frow_ready, 1)
                    dve.wait_ge(frow_ready, NC * hd + c + 1)
                    dve.sem_inc(misc_read, 1)

            def copy_f2(k):
                pr, t0, t1 = F2_PARTS[k]
                b = misc("f2", k)
                dve.tensor_scalar(f2[:, 2 * pr * T:2 * (pr + 1) * T].rearrange("p (h t) -> p h t", h=2)[:, :, t0:t1],
                                  ps[:, b, 0:4 * (t1 - t0)].rearrange("p (t h s) -> p s h t", h=2, s=2)[:, 1],
                                  0.5, None, ALU.mult).then_inc(f2_copied, 1)
                dve.wait_ge(f2_copied, k + 1)
                dve.sem_inc(misc_read, 1)

            copy_f2(0)
            copy_frow(0)
            copy_f2(1)

            def masks(first, j0, j1):
                with dve.Fori(j0, j1) as j:
                    mask(first + j, j)

            def copy_head(hd):
                b, pr = hd % 2, hd // 2
                mine, other = b * DH, (1 - b) * DH
                banks = ps[:, b * NC:(b + 1) * NC, 0:C]
                dve.wait_ge(tile_used, BE + (hd + 1) * T)
                dve.tensor_scalar(chunks(rinv, pr)[mine:mine + DH], banks[other:other + DH], 0.25, None,
                                  ALU.max).then_inc(head_copied, 1)
                if hd < H - 1:
                    dve.tensor_copy(chunks(ga, pr)[mine:mine + DH], banks[mine:mine + DH]).then_inc(head_copied, 1)

            def invert(pr):
                for k in range(2):
                    b = misc("sums", pr, k)
                    n = min(ST, T - k * ST)
                    link(dve.reciprocal(rcol[:, 2 * k * ST:2 * (k * ST + n)].rearrange("p (t s) -> p t s", s=2),
                                        ps[:, b, 0:n * SR].rearrange("p (t r) -> p t r", r=SR)[:, :, 0:SR:DH]))
                    dve.sem_inc(misc_read, 1)
                dve.tensor_copy(rbc.rearrange("p (k d) -> p k d", d=DH),
                                rcol[:, :].unsqueeze(2).to_broadcast([P, 2 * T, DH])).then_inc(rbc_ready, 1)

            def normalise(pr, chunks_=range(NC)):
                for c in chunks_:
                    b = misc("spread", pr, c)
                    w = min(4 * P, W - c * 4 * P)
                    a = pr * NP + c * 4 * P
                    note(dve.tensor_copy(rinv[:, a:a + w], ps[:, b, 0:w]))
                    dve.tensor_tensor(ga[:, a:a + w], ga[:, a:a + w], ps[:, b, 0:w], ALU.mult)\
                       .then_inc(norm_ready, 1)
                    dve.wait_ge(norm_ready, NC * pr + c + 1)
                    dve.sem_inc(misc_read, 1)

            for hd in range(H):
                first = BE + hd * T
                masks(first, 0, 3)
                if hd < H - 1:
                    copy_frow(hd + 1)
                if hd == 0:
                    copy_f2(2)
                if hd:
                    copy_head(hd - 1)
                if hd == 2:
                    masks(first, 3, T - 1)
                    invert(0)
                    masks(first, T - 1, T)
                elif hd == 3:
                    masks(first, 3, 6)
                    normalise(0, range(2))
                    masks(first, 6, T - 1)
                    normalise(0, range(2, NC))
                    masks(first, T - 1, T)
                else:
                    masks(first, 3, T)

            def batch_stats(k, f, src, gamma, beta):
                for c in range(NC):
                    last = dve.bn_stats(bnst[:, (f * NC + c) * 6:(f * NC + c + 1) * 6], src(c, min(C, N - c * C)))
                    (link if c == NC - 1 else note)(last)
                link(dve.bn_aggr(bnag[:, f * 2:(f + 1) * 2], bnst[:, f * NC * 6:(f + 1) * NC * 6]))
                mean, var = bnag[:, 2 * f:2 * f + 1], bnag[:, 2 * f + 1:2 * f + 2]
                rs_, a, b = (bnv[:, i * F + f:i * F + f + 1] for i in range(3))
                dve.tensor_scalar(rs_, var, BN_EPS, None, ALU.add).then_inc(bn_var, 1)
                dve.wait_ge(bn_pow, F * k + f + 1)
                link(dve.tensor_tensor(a, rs_, col(gamma, f), ALU.mult))
                link(dve.tensor_tensor(b, mean, a, ALU.mult))
                dve.tensor_tensor(b, col(beta, f), b, ALU.subtract).then_inc(bn_cols, 1)

            def batch_affine(k, dst, src):
                dve.wait_ge(bn_cols, F * k + 2)
                dve.tensor_scalar(chunks(dst, 1), src, bnv[:, F + 1:F + 2], bnv[:, 2 * F + 1:2 * F + 2],
                                  ALU.mult, ALU.add).then_inc(aff_dve, 1)

            def elu(n, f, which, residual, dst, done):
                e = frow[:, 2 * f * W:(2 * f + 1) * W].rearrange("p (c n) -> p c n", c=NC)
                v = ps[:, f * NC:(f + 1) * NC, 0:C]
                dve.wait_ge(elu_exp, n + 1)
                if residual is None:
                    dve.scalar_tensor_tensor(chunks(dst, f), e, -1.0, v, ALU.add, ALU.max).then_inc(done, 1)
                    return
                link(dve.scalar_tensor_tensor(chunks(dst, f), e, ncol[:, (2 * which + 1) * F + f:(2 * which + 1) * F + f + 1],
                                              v, ALU.add, ALU.max))
                dve.scalar_tensor_tensor(dst[:, f * NP:f * NP + W], dst[:, f * NP:f * NP + W],
                                         col((EM_B, DM_B)[which], f), residual[:, f * NP:f * NP + W],
                                         ALU.add, ALU.add).then_inc(done, 1)

            def col(i, f):
                return colv[:, f * 8 + i:f * 8 + i + 1]

            def in_ga(f):
                return lambda c, n: ga[:, f * NP + c * C:f * NP + c * C + n]

            copy_head(H - 1)
            invert(1)
            dve.wait_ge(num_copied, 1)
            normalise(1)
            for f in range(F):
                dve.wait_ge(proj_mm, f + 1)
                batch_stats(0, f, lambda c, n: ps[:, f * NC + c, 0:n], E_G, E_B)
            batch_affine(0, gb, ps[:, NC:2 * NC, 0:C])
            masks(BD, 0, RING)
            dve.wait_ge(aff_dve, 1)
            dve.wait_ge(aff_act, 1)
            for f in range(F):
                elu(f, f, 0, gb, ga, mlp_sum)
                dve.wait_ge(mlp_sum, f + 1)
                batch_stats(1, f, in_ga(f), EM_G, EM_BB)
            batch_affine(1, ht, chunks(ga, 1))

            def average(q):
                dve.wait_ge(tile_used, BD + T * (q + 1))
                dve.tensor_tensor(chunks(ga, q), ps[:, q * NC:(q + 1) * NC, 0:C], chunks(rinv, q),
                                  ALU.mult).then_inc(norm_dec, 1)

            masks(BD, RING, T)
            masks(BD + T, 0, 3)
            average(0)
            masks(BD + T, 3, 7)
            elu(F, 0, 0, None, gb, dec_ready)
            masks(BD + T, 7, T)
            dve.wait_ge(tile_masked, BD + ND)
            on_diagonal(deg1, diag_added)
            average(1)
            elu(F + 1, 1, 0, None, gb, dec_ready)
            dve.wait_ge(dec_ready, F)
            for f in range(F):
                elu(2 * F + f, f, 1, gb, ga, mlp_sum)
                dve.wait_ge(mlp_sum, F + f + 1)
                batch_stats(2, f, in_ga(f), DM_G, DM_BB)
            batch_affine(2, ht, chunks(ga, 1))
            for r in range(TR):
                dve.wait_ge(tr_done, 3 * TR + r + 1)
                a, b = 2 * r * D, min(2 * r + 2, T) * D
                dve.tensor_tensor(x[:, a:b], x[:, a:b], ps[:, 6 + r % 2, 0:b - a], ALU.add).then_inc(tr_copied, 1)
                if r:
                    dve.wait_ge(tr_copied, 3 * TR + r)
                    round_stats(2, r - 1)

            dve.wait_ge(tr_copied, 4 * TR)
            round_stats(2, TR - 1)
            low_parts(1)
            copy_aggregate(agg_done, 2, ga)

            def l2_scale(r):
                dve.wait_ge(np_mm, TR + r + 1)
                for u in range(min(2, T - 2 * r)):
                    dve.scalar_tensor_tensor(e_pair[r % 2][:, u * D:(u + 1) * D], ps[:, r % 4, u * D:(u + 1) * D],
                                             dinv[:, 2 * r + u:2 * r + u + 1], rowv[:, R_L2B:R_L2B + D], ALU.mult,
                                             ALU.add).then_inc(np_mixed, 1)

            l2_scale(0)
            for r in range(TR):
                if r:
                    dve.wait_ge(np_done, TR + r)
                if r + 1 < TR:
                    l2_scale(r + 1)
                if r:
                    round_stats(3, r - 1)
                a, k = 2 * r * D, min(2, T - 2 * r) * D
                dve.wait_ge(np_mixed, T + min(2 * r + 2, T))
                dve.scalar_tensor_tensor(x[:, a:a + k], e_pair[r % 2][:, 0:k], 0.0, x[:, a:a + k], ALU.max,
                                         ALU.add).then_inc(np_done, 1)
            dve.wait_ge(np_done, 2 * TR)
            round_stats(3, TR - 1)

            copy_transposes(4, ht)
            dve.wait_ge(agg_done, 2)
            dve.wait_ge(diag_added, T)
            for half, (a, b) in enumerate(HALVES):
                for t in range(a, b):
                    on_diagonal(ndeg1, diag_removed, (t,))
                    dve.wait_ge(hn_copied, t + 1)
                    note(dve.scalar_tensor_tensor(gb[:, t * D:(t + 1) * D], h[:, t * D:(t + 1) * D], 1.0,
                                                  h[:, t * D:(t + 1) * D], ALU.mult, ALU.mult,
                                                  accum_out=n2[:, t:t + 1]))
                dve.wait_ge(dve_own, own[0])
                dve.tensor_scalar(n2[:, a:b], n2[:, a:b], NORM_EPS * NORM_EPS, None, ALU.max).then_inc(nrm_done, 1)
            for half, (a, b) in enumerate(HALVES):
                dve.wait_ge(nrm_pow, half + 1)
                for t in range(a, b):
                    dve.tensor_scalar(ga[:, t * D:(t + 1) * D], h[:, t * D:(t + 1) * D], nsum[:, t:t + 1], None,
                                      ALU.mult).then_inc(hn_done, 1)
            for r in range(TR):
                dve.wait_ge(hi_done, r + 1)
                k = min(2, T - 2 * r)
                hi = fm(h_hi)[:, :, 2 * r * P:(2 * r + k) * P]
                dve.tensor_tensor(fm(h_lo)[:, :, 2 * r * P:(2 * r + k) * P],
                                  ps[:, 6 + r % 2, 0:F * 2 * P].rearrange("p (f n) -> p f n", f=F)[:, :, 0:k * P],
                                  hi, ALU.subtract).then_inc(tr_copied, 1)
            dve.wait_ge(diag_removed, T)
            with dve.Fori(0, T) as j:
                dve.wait_ge(sim_exp, NC * j + NC)
                w = ring[:, ds(((B3 + j) % RING) * W, W)]
                dve.scalar_tensor_tensor(w, at[:, ds(j * W, W)], epsv[:, ds(j, 1)], w, ALU.add, ALU.mult)\
                   .then_inc(tile_masked, 1)
            dve.tensor_tensor(x[:, :].rearrange("p (t d) -> p t d", d=D), x[:, :].rearrange("p (t d) -> p t d", d=D),
                              rowv[:, R_L3B:R_L3B + D].unsqueeze(1).to_broadcast([P, T, D]), ALU.add)\
               .then_inc(bias_done, 1)
            dve.wait_ge(s3_mm, 1)
            link(dve.tensor_scalar(rs, ps[:, 6, 0:T], 1e-30, None, ALU.max))
            link(dve.reciprocal(rs, rs))
            copy_aggregate(tile_used, B3 + T, ga)
            dve.wait_ge(bias_done, 1)
            for t in range(T):
                dve.wait_ge(tr_done, 6 * TR + t // 2 + 1)
                a = (t % 2) * D
                last = dve.scalar_tensor_tensor(x[:, t * D:(t + 1) * D], ps[:, 6 + (t // 2) % 2, a:a + D],
                                                rs[:, t:t + 1], x[:, t * D:(t + 1) * D], ALU.mult, ALU.add)
                last.then_inc(np_done, 1)

        @block.tensor
        def _(pe):
            pe.wait_ge(consts, NCONST)

            def weight(i, f):
                return wt[:, (i * F + f) * D:(i * F + f + 1) * D]

            def to_feature_major(batch, src, ready, base, every=1):
                for r in range(TR):
                    pe.wait_ge(ready, base + min(2 * r + 2, T))
                    if r >= 2:
                        pe.wait_ge(tr_copied, batch * TR + r - 1)
                    for f in range(F):
                        for u in range(min(2, T - 2 * r)):
                            a = (2 * r + u) * D + f * P
                            last = pe.transpose(ps[:, 6 + r % 2, f * 2 * P + u * P:f * 2 * P + (u + 1) * P],
                                                src[:, a:a + P], ident[:, :])
                    last.then_inc(tr_done, 1)

            def to_node_major(batch, src):
                for r in range(TR):
                    if r >= 2:
                        if batch == 6:
                            pe.wait_ge(np_done, 2 * TR + 2 * (r - 1))
                        else:
                            pe.wait_ge(tr_copied, batch * TR + r - 1)
                    for u in range(min(2, T - 2 * r)):
                        for f in range(F):
                            a = f * NP + (2 * r + u) * P
                            last = pe.transpose(ps[:, 6 + r % 2, u * D + f * P:u * D + (f + 1) * P],
                                                src[:, a:a + P], ident[:, :])
                    last.then_inc(tr_done, 1)

            def node_product(dst, src, t, rhs, n):
                for f in range(F):
                    last = pe.matmul(dst, src[:, f * NP + t * P:f * NP + (t + 1) * P], rhs(f)[:, 0:n],
                                     start=f == 0, stop=f == F - 1)
                return last

            def aggregate(k):
                def tile(j, start, stop):
                    for f in range(F):
                        for part in (h_hi, h_lo):
                            for c in range(NC):
                                last = pe.matmul(ps[:, f * NC + c, 0:C], part[:, ds(j * D + f * P, P)],
                                                 at[:, ds(j * W + c * C, C)], start=start and part is h_hi,
                                                 stop=stop and part is h_lo)
                    return last
                pe.wait_ge(h16_done, k + 1)
                tile(0, True, False)
                with pe.Fori(1, CD) as j:
                    tile(j, False, False)
                for half, (a, b) in enumerate(((CD, HALVES[0][1]), (HALVES[1][0], T - 1))):
                    pe.wait_ge(h16_done, k + half + 1)
                    with pe.Fori(a, b) as j:
                        if k == 0:
                            pe.wait_ge(cast_act, j - CD + 1)
                            pe.wait_ge(cast_dve, CD)
                        tile(j, False, False)
                if k == 0:
                    pe.wait_ge(cast_act, T - CD)
                tile(T - 1, False, True).then_inc(agg_done, 1)

            def weighted(base, vbase):
                def tile(j, slot, start, stop):
                    pe.wait_ge(vs_ready, vbase + j + 1)
                    pe.wait_ge(tile_masked, base + j + 1)
                    for f in range(F):
                        for c in range(NC):
                            last = pe.matmul(ps[:, f * NC + c, 0:C], vs[:, slot * D + f * P:slot * D + (f + 1) * P],
                                             ring[:, ds(((base + j) % RING) * W + c * C, C)], start=start, stop=stop)
                    last.then_inc(tile_used, 1)
                return tile

            pe.wait_ge(w0_loaded, 16 * NW0)
            for d in range(F):
                for f in range(F):
                    last = pe.matmul(ps[:, 0, d * 2:d * 2 + 2], weight(W_SA_T, f)[:, d * P:(d + 1) * P],
                                     a2[:, f * 2:f * 2 + 2], start=f == 0, stop=f == F - 1)
            last.then_inc(c0_mm, 1)
            to_feature_major(0, h, h_done, 0)
            pe.wait_ge(c0_copied, 1)
            pe.wait_ge(tr_copied, TR)
            pe.wait_ge(cb_ready, F)
            for c in range(NC):
                for f in range(F):
                    last = pe.matmul(ps[:, 2 + c, 0:C], cb[:, f * P:(f + 1) * P],
                                     ht[:, f * NP + c * C:f * NP + (c + 1) * C], start=f == 0, stop=f == F - 1)
            last.then_inc(srow_mm, 1)
            for t in range(T):
                last = node_product(ps[:, 7, 3 * t:3 * t + 3], ht, t, lambda f: r3[:, f * 3:(f + 1) * 3], 3)
            last.then_inc(r3_mm, 1)
            pe.wait_ge(cast_dve, CD)
            pe.wait_ge(srow_copied, 2)
            aggregate(0)
            pe.wait_ge(agg_copied, 2)

            def sum_partitions(k, acc, column):
                for t in range(T):
                    last = pe.matmul(ps[:, 6, k * T + t:k * T + t + 1], acc[:, t * P:(t + 1) * P], column,
                                     start=True, stop=True)
                return last

            pe.wait_ge(wl0_loaded, 16 * NWL0)
            pe.wait_ge(r3_copied, 4)
            for t in range(T):
                if t >= 2:
                    pe.wait_ge(xb_added, 2 * (t - 1))
                node_product(ps[:, 6 + t % 2, 0:DG], ga, t, lambda f: wg[:, f * DG:(f + 1) * DG], DG)\
                    .then_inc(xb_mm, 1)
            tile = weighted(B0, 0)
            tile(0, 0, True, False)
            with pe.Fori(1, T - 2, 2) as j:
                tile(j, 1, False, False)
                tile(j + 1, 0, False, False)
            tile(T - 2, 1, False, False)
            pe.wait_ge(tile_summed, 2 * T)
            pe.wait_ge(xb_added, 2 * T)
            sum_partitions(2, s_acc, ones[:, 0:1])
            sum_partitions(3, d_acc, ones16[:, 0:1]).then_inc(sums_mm, 1)
            tile(T - 1, 0, False, True)

            def node_products(src, i, read_before):
                for r in range(TR):
                    if r >= 4:
                        pe.wait_ge(np_mixed, read_before + 2 * (r - 3))
                    for u in range(min(2, T - 2 * r)):
                        last = node_product(ps[:, r % 4, u * D:(u + 1) * D], src, 2 * r + u, lambda f: weight(i, f), D)
                    last.then_inc(np_mm, 1)

            pe.wait_ge(agg_copied, 4)
            node_products(gb, W_SA, 0)

            pe.wait_ge(w_loaded, 16 * NWR)
            pe.wait_ge(np_mixed, T)
            for pr in range(F):
                last = pe.matmul(ps[:, 0, pr * 8:pr * 8 + 8], wbd[:, (W_BD_T * F + pr) * P:(W_BD_T * F + pr + 1) * P],
                                 vb[:, pr * 8:(pr + 1) * 8], start=True, stop=True)
            last.then_inc(c1_mm, 1)
            pe.wait_ge(dinv_ready, 1)
            to_feature_major(1, h, h_done, T)
            pe.wait_ge(cb_ready, F + H)
            pe.wait_ge(tr_copied, 2 * TR)

            def misc(*name):
                u = MISC.index(name)
                if u >= 2:
                    pe.wait_ge(misc_read, u - 1)
                return 6 + u % 2

            def make_frow(hd):
                pr = hd // 2
                for c in range(NC):
                    b = misc("frow", hd, c)
                    pe.matmul(ps[:, b, 0:C], cb[:, hd * P:(hd + 1) * P],
                              ht[:, pr * NP + c * C:pr * NP + (c + 1) * C], start=True, stop=True)\
                      .then_inc(misc_mm, 1)

            def make_f2(k):
                pr, t0, t1 = F2_PARTS[k]
                b = misc("f2", k)
                for t in range(t0, t1):
                    last = pe.matmul(ps[:, b, 4 * (t - t0):4 * (t - t0 + 1)], ht[:, pr * NP + t * P:pr * NP + (t + 1) * P],
                                     c1[:, pr * 12:pr * 12 + 4], start=True, stop=True)
                last.then_inc(misc_mm, 1)

            make_f2(0)
            make_frow(0)
            make_f2(1)

            def gather_sums(pr):
                pe.wait_ge(head_copied, 4 * pr + 4 if pr == 0 else 2 * H - 1)
                for k in range(2):
                    b = misc("sums", pr, k)
                    for t in range(k * ST, min((k + 1) * ST, T)):
                        last = pe.transpose(ps[:, b, (t - k * ST) * SR:(t - k * ST + 1) * SR],
                                            rinv[0:SR, pr * NP + t * P:pr * NP + (t + 1) * P], ident[0:SR, 0:SR])
                    last.then_inc(misc_mm, 1)

            def spread_inverse(pr, chunks_=range(NC)):
                pe.wait_ge(rbc_ready, pr + 1)
                for c in chunks_:
                    b = misc("spread", pr, c)
                    for t in range(4 * c, min(4 * c + 4, T)):
                        last = pe.transpose(ps[:, b, (t - 4 * c) * P:(t - 4 * c + 1) * P],
                                            rbc[:, t * P:(t + 1) * P], ident[:, :])
                    last.then_inc(misc_mm, 1)

            for hd in range(H):
                b = hd % 2
                if hd >= 2:
                    pe.wait_ge(head_copied, 2 * (hd - 1))

                def enc_tile(j, par, start, stop):
                    n = hd * T + j
                    pe.wait_ge(vs_ready, T + n + 1)
                    pe.wait_ge(tile_masked, BE + n + 1)
                    for c in range(NC):
                        last = pe.matmul(ps[:, b * NC + c, 0:C], vs[:, (b * 2 + par) * P:(b * 2 + par + 1) * P],
                                         ring[:, ds(((BE + n) % RING) * W + c * C, C)], start=start, stop=stop)
                    return last.then_inc(tile_used, 1)

                s = (hd * T) % 2
                enc_tile(0, s, True, False)
                if hd < H - 1:
                    make_frow(hd + 1)
                if hd == 0:
                    make_f2(2)
                if hd == 3:
                    spread_inverse(0, range(2))
                with pe.Fori(1, 5, 2) as j:
                    enc_tile(j, 1 - s, False, False)
                    enc_tile(j + 1, s, False, False)
                if hd == 2:
                    gather_sums(0)
                if hd == 3:
                    spread_inverse(0, range(2, NC))
                with pe.Fori(5, T - 2, 2) as j:
                    enc_tile(j, 1 - s, False, False)
                    enc_tile(j + 1, s, False, False)
                enc_tile(T - 2, 1 - s, False, False)
                enc_tile(T - 1, s, False, True)

            def project(which, pr):
                for c in range(NC):
                    last = pe.matmul(ps[:, pr * NC + c, 0:C], wbd[:, (which * F + pr) * P:(which * F + pr + 1) * P],
                                     ga[:, pr * NP + c * C:pr * NP + (c + 1) * C], start=True, stop=True)
                last.then_inc(proj_mm, 1)

            def mlp_part(i, fi, fo):
                for c in range(NC):
                    last = pe.matmul(ps[:, fo * NC + c, 0:C], weight(i, fi)[:, fo * P:(fo + 1) * P],
                                     gb[:, fi * NP + c * C:fi * NP + (c + 1) * C], start=fi == 0, stop=fi == F - 1)
                return last

            pe.wait_ge(norm_ready, NC)
            pe.wait_ge(head_copied, 2 * (H - 1))
            project(W_BD, 0)
            gather_sums(1)
            spread_inverse(1)
            pe.wait_ge(norm_ready, 2 * NC)
            project(W_BD, 1)
            pe.wait_ge(aff_act, 1)
            mlp_part(MLP_E, 0, 0)
            pe.wait_ge(aff_dve, 1)
            mlp_part(MLP_E, 1, 0).then_inc(mlp_mm, 1)
            mlp_part(MLP_E, 0, 1)
            mlp_part(MLP_E, 1, 1).then_inc(mlp_mm, 1)
            pe.wait_ge(aff_act, 2)
            pe.wait_ge(aff_dve, 2)
            pe.wait_ge(misc_read, len(MISC))
            to_node_major(2, ht)

            for pr in range(2):
                def dec_tile(j, u, start, stop):
                    n, s = pr * T + j, pr * T + u
                    pe.wait_ge(vs_ready, T + NE + n + 1)
                    pe.wait_ge(loaded[s % 2], 16 * (n // 2 + 1))
                    pe.wait_ge(tile_masked, BD + n + 1)
                    for b, tile_ in ((0, back[:, s % RING * W:(s % RING + 1) * W]),
                                     (1, ring[:, (BD + s) % RING * W:((BD + s) % RING + 1) * W])):
                        for c in range(NC):
                            last = pe.matmul(ps[b * DH:(b + 1) * DH, pr * NC + c, 0:C],
                                             vs[:, s % 2 * P + b * DH:s % 2 * P + (b + 1) * DH],
                                             tile_[:, c * C:(c + 1) * C], start=start, stop=stop)
                    last.then_inc(tile_used, 1)

                dec_tile(0, 0, True, False)
                if pr == 1:
                    pe.wait_ge(norm_dec, 1)
                    project(W_BD_T, 0)
                with pe.Fori(1, 9, RING) as j:
                    for u in range(RING):
                        dec_tile(j + u, 1 + u, False, False)
                dec_tile(9, 9, False, False)
                dec_tile(10, 10, False, True)
            pe.wait_ge(dec_ready, 1)
            pe.wait_ge(norm_dec, 2)
            project(W_BD_T, 1)
            mlp_part(MLP_D, 0, 0)
            pe.wait_ge(dec_ready, F)
            mlp_part(MLP_D, 1, 0).then_inc(mlp_mm, 1)
            mlp_part(MLP_D, 0, 1)
            mlp_part(MLP_D, 1, 1).then_inc(mlp_mm, 1)
            pe.wait_ge(aff_act, 3)
            pe.wait_ge(aff_dve, 3)
            to_node_major(3, ht)

            pe.wait_ge(diag_added, T)
            aggregate(2)
            pe.wait_ge(agg_copied, 6)
            node_products(ga, W_L2, T)

            to_feature_major(4, h, h_done, 3 * T)
            pe.wait_ge(tr_copied, 5 * TR)
            for t in range(T):
                if t >= 2:
                    pe.wait_ge(hn_copied, t - 1)
                node_product(ps[:, t % 2, 0:D], ht, t, lambda f: weight(W_L3, f), D).then_inc(hn_mm, 1)
            to_feature_major(5, ga, hn_done, 0)
            pe.wait_ge(tr_copied, 6 * TR)

            def similarity(j):
                for c in range(NC):
                    if c < 2:
                        pe.wait_ge(sim_exp, NC * j + c - 1)
                    else:
                        pe.wait_ge(sim_exp, NC * j + 1)
                    pairs = [(a, b, f) for a, b in ((h_hi, h_hi), (h_hi, h_lo), (h_lo, h_hi)) for f in range(F)]
                    for k, (a, b, f) in enumerate(pairs):
                        if k == 0:
                            pe.wait_ge(tr_copied, 6 * TR)
                        last = pe.matmul(psf[:, ds((6 + (j + c) % 2) * 512, C)], a[:, ds(f * NP + j * P, P)],
                                         b[:, f * NP + c * C:f * NP + (c + 1) * C], start=k == 0,
                                         stop=k == len(pairs) - 1)
                    last.then_inc(sim_mm, 1)

            def similarity_first():
                for c in range(NC):
                    if c == 2:
                        pe.wait_ge(sim_exp, 1)
                    pairs = [(a, b, f) for a, b in ((h_hi, h_hi), (h_hi, h_lo), (h_lo, h_hi)) for f in range(F)]
                    for k, (a, b, f) in enumerate(pairs):
                        last = pe.matmul(ps[:, 6 + c % 2, 0:C], a[:, f * NP:f * NP + P],
                                         b[:, f * NP + c * C:f * NP + (c + 1) * C], start=k == 0,
                                         stop=k == len(pairs) - 1)
                    last.then_inc(sim_mm, 1)

            tile = weighted(B3, T + NE + ND)
            similarity_first()
            similarity(1)
            tile(0, 0, True, False)
            with pe.Fori(1, T - 2, 2) as j:
                similarity(j + 1)
                tile(j, 1, False, False)
                similarity(j + 2)
                tile(j + 1, 0, False, False)
            similarity(T - 1)
            tile(T - 2, 1, False, False)
            pe.wait_ge(tile_summed, 3 * T + 1)
            sum_partitions(0, s_acc, ones[:, 0:1]).then_inc(s3_mm, 1)
            tile(T - 1, 0, False, True)
            pe.wait_ge(agg_copied, 8)
            to_node_major(6, ga)


def kernel(**inputs):
    import numpy as np
    import concourse.bacc as bacc
    from concourse.bass_utils import run_bass_kernel_spmd

    a = {k: np.ascontiguousarray(v) for k, v in inputs.items()}
    n, d = a["x"].shape
    tiles = -(-n // P)
    width = -(-n // 3) * 3
    heads, dh = a["L1_gnn_W"].shape[:2]

    def zeros(*shape):
        return np.zeros(shape, np.float32)

    x = zeros(tiles * P, d)
    x[:n] = a["x"]
    adj_t = zeros(tiles * P, width)
    adj_t[:n, :n] = a["adj"].T
    bd, bdt, vb = zeros(d, P), zeros(d, P), zeros(d, 2 * heads)
    for i in range(heads):
        rows_, c = slice(i * dh, (i + 1) * dh), (i % 2) * dh
        bd[rows_, c:c + dh] = a["L1_gnn_W"][i]
        bdt[rows_, c:c + dh] = a["L1_gnn_W"][i].T
        vb[rows_, 2 * i] = a["L1_gnn_V"][i, 0, :, 0]
        vb[rows_, 2 * i + 1] = a["L1_gnn_V"][i, 1, :, 0]
    mats = [a["L0_gnn_W_sa"], a["L0_gnn_W_sa"].T, a["L1_gnn_enc_mlp_W"].T,
            a["L1_gnn_dec_mlp_W"].T, a["L2_gnn_W"], a["L3_gnn_weight"]]
    wa, wb, asa = a["L0_gnn_Wa"][0], a["L0_gnn_Wb"][0], a["L0_gnn_a_sa"][0]
    names = ["enc_bn_gamma", "enc_bn_beta", "enc_mlp_b", "enc_mlp_bn_gamma", "enc_mlp_bn_beta",
             "dec_mlp_b", "dec_mlp_bn_gamma", "dec_mlp_bn_beta"]
    arrays = {
        "in_x": x, "in_adj_t": adj_t, "in_mats": np.ascontiguousarray(np.stack(mats)),
        "in_blocks": np.ascontiguousarray(np.stack([bd, bdt])),
        "in_a2": np.ascontiguousarray(np.stack([asa[:d], asa[d:]], 1)),
        "in_wg": np.concatenate([a["L0_gnn_W_gcnb"], np.stack([wa[:d], wb[:d]], 1)], 1),
        "in_wr": np.ascontiguousarray(np.stack([wa[d:], wb[d:]], 1)),
        "in_vb": vb,
        "in_colv": np.ascontiguousarray(np.stack([a["L1_gnn_" + k] for k in names], 1)),
        "in_rows": np.concatenate([a["L0_gnn_b_gcnb"], a["L2_gnn_b"], a["L3_gnn_bias"], a["L0_gnn_ba"],
                                   a["L0_gnn_bb"]])[None],
    }
    nc = bacc.Bacc("TRN2", target_bir_lowering=False, num_devices=1)
    ap = {k: nc.dram_tensor(k, v.shape, mybir.dt.from_np(v.dtype), kind="ExternalInput").ap()
          for k, v in arrays.items()}
    out = nc.dram_tensor("out_0", (n, d), F32, kind="ExternalOutput").ap()
    gnn_stack(nc, ap["in_x"], ap["in_adj_t"], ap["in_mats"], ap["in_blocks"],
              {k: ap["in_" + k] for k in ("a2", "wg", "wr", "vb", "colv")}, ap["in_rows"], out)
    return run_bass_kernel_spmd(nc, [arrays], core_ids=[0]).results[0]["out_0"]
```

```python
from contextlib import ExitStack

import concourse.bass as bass
from concourse import mybir

F32 = mybir.dt.float32
F16 = mybir.dt.float16
ALU = mybir.AluOpType
ACT = mybir.ActivationFunctionType
AX_X = mybir.AxisListType.X
ds = bass.ds

P = 128
LN_EPS = 1e-5
BN_EPS = 1e-6
L0_EPS = 1e-5
ADJ_EPS = 1e-8
NORM_EPS = 1e-8


def gnn_stack(nc, x_in, adj_t, weights, blocks, cols, rows, out):
    N = out.shape[0]
    D = out.shape[1]
    T = -(-N // P)
    NP = T * P
    W = adj_t.shape[1]
    NC = 3
    C = W // NC
    LAST = N - (T - 1) * P
    F = D // P
    H = 4
    DH = D // H
    RING = 4
    assert F == 2 and C * NC == W and C <= 512 and W >= N
    (W_SA, W_SA_T, MLP_E, MLP_D, W_L2, W_L3) = range(6)
    (W_BD, W_BD_T) = range(2)
    (E_G, E_B, EM_B, EM_G, EM_BB, DM_B, DM_G, DM_BB) = range(8)
    R_GCNB, R_L2B, R_L3B, R_BA = 0, D, 2 * D, 3 * D
    NR = 3 * D + 2

    with ExitStack() as ctx:
        def sb(name, width, dt=F32):
            return ctx.enter_context(nc.sbuf_tensor("sb_" + name, [P, width], dt))

        def sem(name):
            return ctx.enter_context(nc.semaphore(name))

        at = sb("adj_t", T * W, F16)
        x = sb("x", T * D)
        h = sb("h", T * D)
        shared = sb("shared", T * D + 2 * NP)
        h_hi = shared[:, 0:T * D // 2].bitcast(F16)
        h_lo = shared[:, T * D // 2:T * D].bitcast(F16)
        s_acc = shared[:, T * D:T * D + NP]
        d_acc = shared[:, T * D + NP:T * D + NP + NP // 2].bitcast(F16)
        back = shared[:, 0:RING * W]
        ht = sb("ht", F * NP)
        ga = sb("ga", F * NP)
        gb = sb("gb", F * NP)
        rinv = sb("rinv", F * NP)
        frow = sb("frow", H * W)
        row_buf = frow[0:96, 3 * W:3 * W + 512]
        tt = sb("tt", 3 * W)
        ring = sb("ring", RING * W)
        vs = sb("vs", 2 * 2 * P * F)
        wt = sb("wt", 6 * F * D)
        DG = D + 2
        wg = sb("wg", F * DG)
        wbd = sb("wbd", 2 * F * P)
        colv = sb("colv", F * 8)
        rowv = sb("rowv", NR)
        smallw = sb("smallw", F * (2 + 8 + 32))
        a2 = smallw[:, 0:F * 2]
        vb = smallw[:, F * 2:F * 10]
        r3 = smallw[:, F * 10:F * 42]
        c0 = sb("c0", F * 2)
        c1 = sb("c1", F * 32)
        f2 = sb("f2", H * T)
        ident = sb("ident", P)
        ones = sb("ones", P)
        ones16 = sb("ones16", 2, F16)
        rcol = sb("rcol", 2 * T)
        rbc = gb[:, NP:NP + T * P]
        ncol = sb("ncol", 4 * F)
        stats = sb("stats", T * 6)
        lnt = sb("lnt", 6 * T)
        rstd = sb("rstd", T)
        nmr = sb("nmr", T)
        mhalf = sb("mhalf", T)
        epsv = sb("epsv", T)
        nodev = sb("nodev", 16 * T)
        bnst = sb("bnst", F * NC * 6)
        bnag = sb("bnag", F * 2)
        bnv = sb("bnv", F * 4)
        e_t = sb("e_t", 2 * D)
        cb = e_t
        e_q = sb("e_q", 2 * D)
        e_pair = (e_t, e_q)
        ps = ctx.enter_context(nc.psum_tensor("ps", [P, 8, 512], F32))

        gab, gates, attn, rs, ca, dinv, dmax, deg1, srt, sr99, n2, nsum, ndeg1 = (
            nodev[:, 0:2 * T], nodev[:, 2 * T:4 * T], nodev[:, 4 * T:6 * T], nodev[:, 6 * T:7 * T],
            nodev[:, 7 * T:8 * T], nodev[:, 8 * T:9 * T], nodev[:, 9 * T:10 * T], nodev[:, 10 * T:11 * T],
            nodev[:, 11 * T:12 * T], nodev[:, 12 * T:13 * T], nodev[:, 13 * T:14 * T], nodev[:, 14 * T:15 * T],
            nodev[:, 15 * T:16 * T])

        psf = ps[:, :, :].rearrange("p b n -> p (b n)")
        TR = -(-T // 2)
        NCONST = 11
        spill = nc.dram_tensor("spill", [2 * T * P, W], F32, kind="Internal").ap()

        def fm(a, width=NP):
            return a[:, :].rearrange("p (f n) -> p f n", f=F)

        def chunks(a, f=0, width=NP):
            return a[:, f * width:f * width + W].rearrange("p (c n) -> p c n", c=NC)

        x_ld = [sem(f"x_loaded{k}") for k in range(3)]
        adj_ld = [sem(f"adj_loaded{j}") for j in range(T)]
        w0_loaded, wl0_loaded, w_loaded = sem("w0_loaded"), sem("w_l0_loaded"), sem("w_loaded")
        cast_dve, cast_act = sem("adj_cast_by_vector"), sem("adj_cast_by_scalar")
        consts, accs_zero, ncol_ready = sem("consts_ready"), sem("accs_zero"), sem("ncol_ready")
        dve_own, pool_own = sem("dve_own"), sem("pool_own")
        stats_done, lnvar, lnpow, h_done = sem("stats_done"), sem("ln_var"), sem("ln_pow"), sem("h_done")
        h16_hi, h16_done = sem("h_high_part"), sem("h_low_part")
        tr_done, tr_copied = sem("transposed"), sem("transposes_copied")
        tile_arg, tile_tanh, tile_exp, tile_masked, tile_used, tile_summed = (
            sem("tile_arg"), sem("tile_tanh"), sem("tile_exp"), sem("tile_masked"), sem("tile_used"), sem("tile_summed"))
        vs_ready, agg_done, agg_copied = sem("values_ready"), sem("aggregated"), sem("aggregate_copied")
        rows_mm, rows_copied, cols_mm = sem("rows_mm"), sem("rows_copied"), sem("cols_mm")
        c0_mm, c0_copied, r3_copied, srow_mm, srow_copied, cb_ready = (
            sem("c0_mm"), sem("c0_copied"), sem("r3_copied"), sem("srow_mm"), sem("srow_copied"), sem("cb_ready"))
        xb_mm, xb_added, xb_scaled = sem("xb_mm"), sem("xb_added"), sem("xb_scaled")
        gate_tanh, gate_attn, dinv_ready = sem("gate_tanh"), sem("gate_attn"), sem("dinv_ready")
        np_mm, np_mixed, np_act, np_done = (
            sem("node_product"), sem("node_mixed"), sem("node_act"), sem("node_done"))
        c1_mm, frow_ready, f2_copied = sem("c1_mm"), sem("frow_ready"), sem("f2_copied")
        misc_mm, misc_read = sem("misc_mm"), sem("misc_read")
        head_copied, num_copied, rbc_ready, norm_ready, norm_dec = (
            sem("head_copied"), sem("numerators_copied"), sem("rbc_ready"), sem("normalised"), sem("norm_dec"))
        proj_mm, bn_var, bn_pow, bn_cols, aff_act, aff_dve = (
            sem("proj_mm"), sem("bn_var"), sem("bn_pow"), sem("bn_cols"), sem("aff_act"), sem("aff_dve"))
        mlp_mm, mlp_sum, elu_relu, elu_exp, dec_ready = (
            sem("mlp_mm"), sem("mlp_sum"), sem("elu_relu"), sem("elu_exp"), sem("dec_ready"))
        emb_mm, emb_act, emb_dve = sem("embedding_transposed"), sem("embedding_by_scalar"), sem("embedding_by_vector")
        saved, ring_saved, loaded = [sem("saved0"), sem("saved1")], sem("ring_saved"), [sem("loaded0"), sem("loaded1")]
        diag_added, diag_removed = sem("diagonal_added"), sem("diagonal_removed")
        hn_mm, hn_copied, nrm_done, nrm_pow, hn_done, hi_done = (
            sem("hn_mm"), sem("hn_copied"), sem("norm_done"), sem("norm_pow"), sem("hn_done"), sem("hi_done"))
        sim_mm, sim_exp, bias_done, out_stored = sem("sim_mm"), sem("sim_exp"), sem("bias_done"), sem("out_stored")

        NW0, NWL0, NWR = 4, 2, 8
        X_CUTS = (0, 4, 8, T)
        CD = 4
        landing = ([ring[:, k * W:(k + 1) * W] for k in range(RING)] + [tt[:, k * W:(k + 1) * W] for k in range(3)]
                   + [a[:, f * NP:f * NP + W] for a in (rinv, gb, ga) for f in range(F)])[:T]
        xb = shared[:, 0:T * D]
        HALVES = ((0, CD), (CD, T))
        MISC = ([("frow", hd, c) for hd in range(H) for c in range(NC)]
                + [(k, pr, c) for pr in range(2) for k, n in (("sums", 2), ("spread", NC)) for c in range(n)])
        ER = -(-T // 4)
        SR = DH + 1
        ST = 512 // SR

        N0, NE, ND, N3 = T, H * T, 2 * T, T
        B0, BE, BD, B3 = 0, N0, N0 + NE, N0 + NE + ND

        def node_block(a, f, q):
            return a[:, :].rearrange("p (t d) -> p t d", d=D)[:, 4 * q:min(4 * q + 4, T), f * P:(f + 1) * P]

        def bank_block(bank, q):
            k = min(4, T - 4 * q)
            return ps[:, bank, 0:k * P].rearrange("p (t d) -> p t d", d=P)

        def by_node(dst, bank, k):
            for c0, c1_, nu in ((0, ER - 1, 4), (ER - 1, ER, T - 4 * (ER - 1))):
                yield (dst[:, 4 * c0:4 * (c1_ - 1) + nu].rearrange("p (c u) -> p c u", u=nu),
                       ps[:, bank, 0:4 * 96].rearrange("p (u c r) -> p c u r", u=4, c=3)[:, c0:c1_, 0:nu, k])

        block = ctx.enter_context(nc.Block())

        @block.sync
        def _(sp):
            for k in range(3):
                a, b = X_CUTS[k], X_CUTS[k + 1]
                sp.dma_start(x[:, a * D:b * D].rearrange("p (t d) -> p t d", d=D),
                             x_in[a * P:b * P, :].rearrange("(t p) d -> p t d", p=P)).then_inc(x_ld[k], 16)

            def load_w(dst, src, s):
                sp.dma_start(dst.rearrange("p (f n) -> p f n", f=F),
                             src.rearrange("(f p) n -> p f n", p=P)).then_inc(s, 16)

            load_w(a2, cols["a2"], w0_loaded)
            load_w(wt[:, W_SA_T * F * D:(W_SA_T + 1) * F * D], weights[W_SA_T], w0_loaded)
            sp.dma_start(r3.rearrange("p (f n) -> p f n", f=F)[:, :, 0:2],
                         cols["wr"].rearrange("(f p) n -> p f n", p=P)).then_inc(w0_loaded, 16)
            for j in range(T):
                sp.dma_start(landing[j], adj_t[j * P:(j + 1) * P, :]).then_inc(adj_ld[j], 16)
                if j == 1:
                    sp.dma_start(rowv[:, :], rows.partition_broadcast(P)).then_inc(w0_loaded, 16)
            load_w(wg[:, :], cols["wg"], wl0_loaded)
            load_w(wt[:, W_SA * F * D:(W_SA + 1) * F * D], weights[W_SA], wl0_loaded)
            for i in (MLP_E, MLP_D, W_L2, W_L3):
                load_w(wt[:, i * F * D:(i + 1) * F * D], weights[i], w_loaded)
            for i in range(2):
                load_w(wbd[:, i * F * P:(i + 1) * F * P], blocks[i], w_loaded)
            load_w(vb, cols["vb"], w_loaded)
            load_w(colv[:, :], cols["colv"], w_loaded)
            sp.sem_inc(ring_saved, BE)
            k = 0
            for hd in range(H):
                if hd % 2:
                    with sp.Fori(0, T) as j:
                        sp.wait_ge(tile_masked, BE + hd * T + j + 1)
                        sp.sem_inc(ring_saved, 1)
                    continue
                for j in range(T):
                    slot = (BE + hd * T + j) % RING
                    sp.wait_ge(tile_masked, BE + hd * T + j + 1)
                    sp.dma_start(spill[k * P:(k + 1) * P, :], ring[:, slot * W:(slot + 1) * W])\
                      .then_inc(saved[k % 2], 16)
                    if j:
                        sp.wait_ge(saved[(k - 1) % 2], 16 * ((k - 1) // 2 + 1))
                        sp.sem_inc(ring_saved, 1)
                    k += 1
                sp.wait_ge(saved[(k - 1) % 2], 16 * ((k - 1) // 2 + 1))
                sp.sem_inc(ring_saved, 1)
            for k in range(2 * T):
                if k >= 2:
                    sp.wait_ge(loaded[k % 2], 16 * (k // 2))
                if k >= RING:
                    sp.wait_ge(tile_used, BD + k - RING + 1)
                slot = k % RING
                sp.dma_start(back[:, slot * W:(slot + 1) * W], spill[k * P:(k + 1) * P, :])\
                  .then_inc(loaded[k % 2], 16)
            for a, b in ((0, 4), (4, 8), (8, T - 1)):
                sp.wait_ge(np_done, 2 * TR + b)
                sp.dma_start(out[a * P:b * P, :].rearrange("(t p) d -> p t d", p=P),
                             x[:, a * D:b * D].rearrange("p (t d) -> p t d", d=D)).then_inc(out_stored, 16)
            sp.wait_ge(np_done, 2 * TR + T)
            sp.dma_start(out[(T - 1) * P:N, :], x[0:LAST, (T - 1) * D:T * D]).then_inc(out_stored, 16)
            sp.wait_ge(out_stored, 64)

        @block.gpsimd
        def _(pool):
            own = [0]

            def link(ins):
                own[0] += 1
                ins.then_inc(pool_own, 1)
                pool.wait_ge(pool_own, own[0])

            link(pool.memset(ident[:, :], 0.0))
            link(pool.memset(epsv[:, :], ADJ_EPS))
            pool.affine_select(out=ident[:, :], in_=ident[:, :], compare_op=ALU.not_equal, fill=1.0, base=0,
                               pattern=[[-1, P]], channel_multiplier=1).then_inc(consts, 1)
            pool.affine_select(out=epsv[:, T - 1:T], in_=epsv[:, T - 1:T], compare_op=ALU.is_ge, fill=0.0,
                               base=LAST - 1, pattern=[[0, 1]], channel_multiplier=-1).then_inc(consts, 1)
            pool.memset(ones[:, :], 1.0).then_inc(consts, 1)
            pool.memset(ones16[:, :], 1.0).then_inc(consts, 1)
            pool.memset(mhalf[:, :], -0.5).then_inc(consts, 1)
            pool.memset(r3.rearrange("p (f n) -> p f n", f=F)[:, :, 3:32], 0.0).then_inc(consts, 1)
            pool.memset(fm(c1)[:, :, 8:32], 0.0).then_inc(consts, 1)
            pool.memset(row_buf, 0.0).then_inc(consts, 1)
            for a, v in ((ga, 0.0), (gb, 0.0), (rinv, 1.0)):
                pool.memset(fm(a)[:, :, W:NP], v).then_inc(consts, 1)
            pool.wait_ge(consts, NCONST)

            def norm_power(layer):
                for k, (a, b) in enumerate(HALVES):
                    pool.wait_ge(lnvar, 2 * layer + k + 1)
                    link(pool.tensor_tensor(rstd[:, a:b], lnt[:, 4 * T + a:4 * T + b], mhalf[:, a:b], ALU.pow))
                    pool.tensor_tensor(nmr[:, a:b], lnt[:, 5 * T + a:5 * T + b], rstd[:, a:b], ALU.mult)\
                        .then_inc(lnpow, 1)

            def batch_power(k, blocks_=range(F)):
                for f in blocks_:
                    pool.wait_ge(bn_var, F * k + f + 1)
                    pool.tensor_tensor(bnv[:, f:f + 1], bnv[:, f:f + 1], mhalf[:, 0:1], ALU.pow).then_inc(bn_pow, 1)

            def node_values(j, base):
                pool.wait_ge(tile_used, base + j - 1)
                pool.tensor_copy(vs[:, ds((j % 2) * D, D)], h[:, ds(j * D, D)]).then_inc(vs_ready, 1)

            def sum_weights(j, base, before):
                pool.wait_ge(tile_masked, base + j + 1)
                pool.wait_ge(tile_summed, before + j)
                pool.tensor_tensor(s_acc[:, 0:W], s_acc[:, 0:W], ring[:, ds(((base + j) % RING) * W, W)],
                                   ALU.add).then_inc(tile_summed, 1)

            norm_power(0)
            pool.memset(s_acc[:, :], 0.0).then_inc(accs_zero, 1)
            pool.memset(d_acc[:, :], 0.0).then_inc(accs_zero, 1)
            pool.wait_ge(accs_zero, 2)

            def sum_adjacency(j):
                pool.tensor_tensor(d_acc[:, 0:W], d_acc[:, 0:W], at[:, ds(j * W, W)],
                                   ALU.add).then_inc(tile_summed, 1)
                pool.wait_ge(tile_summed, j + 1)

            with pool.Fori(0, CD) as j:
                pool.wait_ge(cast_dve, j + 1)
                sum_adjacency(j)
            with pool.Fori(CD, T) as j:
                pool.wait_ge(cast_act, j - CD + 1)
                sum_adjacency(j)
            pool.wait_ge(h_done, T)
            for j in range(2):
                pool.tensor_copy(vs[:, j * D:(j + 1) * D], h[:, j * D:(j + 1) * D]).then_inc(vs_ready, 1)
                sum_weights(j, B0, T)
            with pool.Fori(2, T) as j:
                node_values(j, B0)
                sum_weights(j, B0, T)

            norm_power(1)
            pool.wait_ge(tile_used, B0 + N0)
            link(pool.memset(vs[:, :], 1.0))
            pool.wait_ge(h_done, 2 * T)
            for hd in range(H):
                with pool.Fori(0, T) as j:
                    pool.wait_ge(tile_used, BE + hd * T + j - 1)
                    pool.tensor_copy(vs[:, ds(((hd * T + j) % 2) * P + (hd % 2) * (2 * P + DH), DH)],
                                     h[:, ds(j * D + hd * DH, DH)]).then_inc(vs_ready, 1)
            batch_power(0)
            def pair_values(pr, j):
                pool.tensor_copy(vs[:, ds(((pr * T + j) % 2) * P, P)],
                                 h[:, ds(j * D + pr * P, P)]).then_inc(vs_ready, 1)

            batch_power(1, (0,))
            pool.wait_ge(emb_act, ER)
            pool.wait_ge(tile_used, BE + NE)
            for j in range(2):
                pair_values(0, j)
            batch_power(1, (1,))
            for pr in range(2):
                if pr == 1:
                    pool.wait_ge(emb_dve, ER)
                with pool.Fori(2 * (1 - pr), T) as j:
                    pool.wait_ge(tile_used, BD + pr * T + j - 1)
                    pair_values(pr, j)
            batch_power(2)
            norm_power(2)
            pool.wait_ge(tile_used, BD + ND)
            pool.memset(s_acc[:, :], 0.0).then_inc(tile_summed, 1)
            norm_power(3)
            for k, (a, b) in enumerate(HALVES):
                pool.wait_ge(nrm_done, k + 1)
                pool.tensor_tensor(nsum[:, a:b], n2[:, a:b], mhalf[:, a:b], ALU.pow).then_inc(nrm_pow, 1)
            pool.wait_ge(hn_copied, T)
            pool.wait_ge(tile_used, B3)
            with pool.Fori(0, T - 1) as j:
                node_values(j, B3)
                sum_weights(j, B3, 2 * T + 1)
            node_values(T - 1, B3)

        @block.scalar
        def _(act):
            act.preload_act_table(ACT.Exp)
            act.wait_ge(consts, NCONST)

            def norm_apply(layer, halves=(0, 1), split=False):
                for k in halves:
                    a, b = HALVES[k]
                    act.wait_ge(lnpow, 2 * layer + k + 1)
                    for t in range(a, b):
                        act.activation(h[:, t * D:(t + 1) * D], x[:, t * D:(t + 1) * D], ACT.Relu,
                                       bias=nmr[:, t:t + 1], scale=rstd[:, t:t + 1]).then_inc(h_done, 1)
                    if split:
                        act.wait_ge(h_done, T * layer + b)
                        act.activation(h_hi[:, a * D:b * D], h[:, a * D:b * D], ACT.Copy).then_inc(h16_hi, 1)

            def copy_aggregate(done, count, dst):
                act.wait_ge(done, count)
                act.activation(chunks(dst), ps[:, 0:NC, 0:C], ACT.Copy).then_inc(agg_copied, 1)

            norm_apply(0, split=True)
            for j in range(CD, T):
                if j == CD + 3:
                    act.wait_ge(srow_mm, 1)
                    act.activation(chunks(frow, 0, W), ps[:, 2:2 + NC, 0:C], ACT.Copy).then_inc(srow_copied, 1)
                act.wait_ge(adj_ld[j], 16)
                act.activation(at[:, j * W:(j + 1) * W], landing[j], ACT.Copy).then_inc(cast_act, 1)
            act.wait_ge(r3_copied, 8)

            def score_exp(j):
                act.wait_ge(tile_arg, j + 1)
                act.wait_ge(r3_copied, 8)
                act.activation(ring[:, ds((j % RING) * W, W)], tt[:, ds((j % 2) * W, W)], ACT.Exp,
                               bias=srt[:, ds(j, 1)], scale=-1.0).then_inc(tile_exp, 1)

            act.wait_ge(cast_dve, CD)
            with act.Fori(0, RING) as j:
                score_exp(j)
            copy_aggregate(agg_done, 1, ga)
            act.wait_ge(xb_added, 2 * T)
            act.activation(gates, gates, ACT.Tanh, scale=0.5).then_inc(gate_tanh, 1)
            with act.Fori(0, T) as t:
                act.wait_ge(gate_attn, 1)
                act.activation(xb[:, ds(t * D, D)], xb[:, ds(t * D, D)], ACT.Copy,
                               scale=attn[:, ds(t + T, 1)]).then_inc(xb_scaled, 1)
            with act.Fori(RING, T) as j:
                act.wait_ge(tile_used, j - RING + 1)
                act.wait_ge(tile_summed, T + j - RING + 1)
                score_exp(j)
            copy_aggregate(tile_used, B0 + T, gb)
            for r in range(TR):
                act.wait_ge(np_mixed, min(2 * r + 2, T))
                e = e_pair[r % 2][:, 0:min(2, T - 2 * r) * D]
                act.activation(e, e, ACT.Tanh, scale=0.5).then_inc(np_act, 1)
            norm_apply(1)


            def tanh(base, m, head_of, node_of):
                act.activation(tt[:, ds((m % 3) * W, W)], frow[:, ds(head_of(m) * W, W)], ACT.Tanh,
                               bias=f2[:, ds(head_of(m) * T + node_of(m), 1)], scale=0.5).then_inc(tile_tanh, 1)

            def exp(base, m):
                act.wait_ge(tile_tanh, base - BE + m + 1)
                act.wait_ge(tile_used, base + m - RING + 1)
                act.wait_ge(ring_saved, BE + NE if base == BD else base + m - RING + 1)
                act.wait_ge(f2_copied, 2 * H)
                act.activation(ring[:, ds(((base + m) % RING) * W, W)], tt[:, ds((m % 3) * W, W)], ACT.Exp,
                               scale=0.5).then_inc(tile_exp, 1)

            def tiles(base, a, b, head_of, node_of):
                with act.Fori(a, b) as m:
                    act.wait_ge(tile_exp, base + m - 1)
                    if base == BE:
                        act.wait_ge(frow_ready, NC * ((m + 1) // T) + NC)
                    act.wait_ge(f2_copied, 2 * H)
                    tanh(base, m + 1, head_of, node_of)
                    exp(base, m)

            def batch_affine(k, dst, src):
                act.wait_ge(bn_cols, F * k + 1)
                act.activation(chunks(dst), src, ACT.Identity, bias=bnv[:, 2 * F:2 * F + 1],
                               scale=bnv[:, F:F + 1]).then_inc(aff_act, 1)

            def elu_exp_part(n, f, nbias, ready, count):
                e = frow[:, 2 * f * W:(2 * f + 1) * W]
                act.wait_ge(ready, count)
                act.activation(e.rearrange("p (c n) -> p c n", c=NC), ps[:, f * NC:(f + 1) * NC, 0:C], ACT.Relu,
                               bias=nbias, scale=-1.0).then_inc(elu_relu, 1)
                act.wait_ge(elu_relu, n + 1)
                act.activation(e, e, ACT.Exp, scale=-1.0).then_inc(elu_exp, 1)

            by_head = (lambda m: m // T, lambda m: m % T)
            for c in range(NC):
                act.wait_ge(misc_mm, c + 1)
                act.activation(frow[:, c * C:(c + 1) * C], ps[:, 6 + c % 2, 0:C], ACT.Copy).then_inc(frow_ready, 1)
                act.wait_ge(frow_ready, c + 1)
                act.sem_inc(misc_read, 1)
            act.wait_ge(f2_copied, 2 * H)
            tanh(BE, 0, *by_head)
            exp(BE, 0)
            tanh(BE, 1, *by_head)
            tiles(BE, 1, NE - 1, *by_head)
            exp(BE, NE - 1)
            batch_affine(0, gb, ps[:, 0:NC, 0:C])
            act.wait_ge(tile_used, BE + NE)
            act.activation(chunks(ga, 1)[DH:P], ps[DH:P, NC:2 * NC, 0:C], ACT.Copy).then_inc(num_copied, 1)
            odd_heads = (lambda m: 2 * (m // T) + 1, lambda m: m % T)
            tanh(BD, 0, *odd_heads)
            tiles(BD, 0, RING, *odd_heads)
            act.wait_ge(ncol_ready, 1)
            for f in range(F):
                elu_exp_part(f, f, ncol[:, f:f + 1], mlp_mm, f + 1)
            batch_affine(1, ht, chunks(ga))
            for q in range(ER):
                act.wait_ge(emb_mm, q + 1)
                act.activation(node_block(h, 0, q), bank_block(6 + q % 2, q), ACT.Copy).then_inc(emb_act, 1)
            SPLIT = T + 6
            tiles(BD, RING, SPLIT, *odd_heads)
            elu_exp_part(F, 0, 0.0, proj_mm, F + 1)
            tiles(BD, SPLIT, ND - 1, *odd_heads)
            exp(BD, ND - 1)
            elu_exp_part(F + 1, 1, 0.0, proj_mm, F + 2)
            for f in range(F):
                elu_exp_part(2 * F + f, f, ncol[:, 2 * F + f:2 * F + f + 1], mlp_mm, F + f + 1)
            batch_affine(2, ht, chunks(ga))

            norm_apply(2, split=True)
            copy_aggregate(agg_done, 2, ga)
            norm_apply(3)
            act.wait_ge(tr_copied, 4 * TR)
            for t in range(T):
                act.wait_ge(hn_mm, t + 1)
                act.activation(h[:, t * D:(t + 1) * D], ps[:, t % 4, 0:D], ACT.Copy).then_inc(hn_copied, 1)
            for r in range(TR):
                act.wait_ge(tr_done, 4 * TR + r + 1)
                k = min(2, T - 2 * r)
                act.activation(fm(h_hi)[:, :, 2 * r * P:(2 * r + k) * P],
                               ps[:, 6 + r % 2, 0:F * 2 * P].rearrange("p (f n) -> p f n", f=F)[:, :, 0:k * P],
                               ACT.Copy).then_inc(hi_done, 1)
            with act.Fori(0, T) as j:
                act.wait_ge(tile_used, B3 + j - RING + 1)
                act.wait_ge(tile_summed, 2 * T + 1 + j - RING + 1)
                for c in range(NC):
                    act.wait_ge(sim_mm, NC * j + c + 1)
                    act.wait_ge(hi_done, TR)
                    act.activation(ring[:, ds(((B3 + j) % RING) * W + c * C, C)],
                                   psf[:, ds((6 + (j + c) % 2) * 512, C)], ACT.Exp).then_inc(sim_exp, 1)
            copy_aggregate(tile_used, B3 + T, ga)

        @block.vector
        def _(dve):
            own = [0]

            def link(ins):
                own[0] += 1
                ins.then_inc(dve_own, 1)
                dve.wait_ge(dve_own, own[0])

            def note(ins):
                own[0] += 1
                ins.then_inc(dve_own, 1)

            def row_stats(t):
                dve.bn_stats(stats[:, ds(t * 6, 6)], x[:, ds(t * D, D)]).then_inc(stats_done, 1)

            def norm_half(layer, half):
                a, b = HALVES[half]
                dve.wait_ge(stats_done, T * layer + b)
                s = stats[:, :].rearrange("p (t k) -> p k t", k=6)[:, :, a:b]
                total, diff, m2, d2, var, nmean = (lnt[:, k * T + a:k * T + b] for k in range(6))
                note(dve.tensor_tensor(total, s[:, 1], s[:, 4], ALU.add))
                note(dve.tensor_tensor(diff, s[:, 1], s[:, 4], ALU.subtract))
                link(dve.tensor_tensor(m2, s[:, 2], s[:, 5], ALU.add))
                note(dve.tensor_tensor(d2, diff, diff, ALU.mult))
                note(dve.tensor_scalar(nmean, total, -0.5, None, ALU.mult))
                link(dve.tensor_scalar(m2, m2, 1.0 / D, LN_EPS, ALU.mult, ALU.add))
                dve.scalar_tensor_tensor(var, d2, 0.25, m2, ALU.mult, ALU.add).then_inc(lnvar, 1)

            def round_stats(layer, r):
                for t in range(2 * r, min(2 * r + 2, T)):
                    row_stats(t)
                    for half, (a, b) in enumerate(HALVES):
                        if t == b - 1:
                            norm_half(layer, half)

            def copy_transposes(batch, dst):
                for r in range(TR):
                    dve.wait_ge(tr_done, batch * TR + r + 1)
                    k = min(2, T - 2 * r) * P
                    dve.tensor_copy(fm(dst)[:, :, 2 * r * P:2 * r * P + k],
                                    ps[:, 6 + r % 2, 0:F * 2 * P].rearrange("p (f n) -> p f n", f=F)[:, :, 0:k])\
                       .then_inc(tr_copied, 1)

            def copy_aggregate(done, count, dst):
                dve.wait_ge(done, count)
                dve.tensor_copy(chunks(dst, 1), ps[:, NC:2 * NC, 0:C]).then_inc(agg_copied, 1)

            def copy_rows(n, bank):
                dve.wait_ge(rows_mm, n)
                for a, b, w in ((0, 32 * (ER - 1), 512), (32 * (ER - 1), 96, NP - 512 * (ER - 1))):
                    dve.tensor_copy(row_buf[a:b, 0:w], ps[a:b, bank, 0:w]).then_inc(rows_copied, 1)

            def on_diagonal(values, done):
                for j in range(T):
                    d = at[:, j * W + j * P:j * W + min((j + 1) * P, W)]
                    dve.scalar_tensor_tensor(d, ident[:, 0:d.shape[1]], values[:, j:j + 1], d, ALU.mult,
                                             ALU.add).then_inc(done, 1)

            for k in range(3):
                dve.wait_ge(x_ld[k], 16)
                for t in range(X_CUTS[k], X_CUTS[k + 1]):
                    row_stats(t)
                if k != 1:
                    norm_half(0, k // 2)

            def cast(j):
                dve.wait_ge(adj_ld[j], 16)
                dve.tensor_copy(at[:, j * W:(j + 1) * W], landing[j]).then_inc(cast_dve, 1)

            def low_parts(layer):
                for k, (a, b) in enumerate(HALVES):
                    dve.wait_ge(h16_hi, 2 * layer + k + 1)
                    dve.tensor_tensor(h_lo[:, a * D:b * D], h[:, a * D:b * D], h_hi[:, a * D:b * D],
                                      ALU.subtract).then_inc(h16_done, 1)

            cast(0)
            dve.wait_ge(c0_mm, 1)
            link(dve.tensor_copy(c0[:, :], ps[:, 0, 0:F * 2]))
            r3v = r3.rearrange("p (f n) -> p f n", f=F)
            c0v = c0[:, :].rearrange("p (f n) -> p f n", f=F)
            dve.wait_ge(w0_loaded, 16 * NW0)
            dve.tensor_copy(r3v[:, :, 2:3], c0v[:, :, 1:2]).then_inc(c0_copied, 1)
            dve.wait_ge(consts, NCONST)
            for f in range(F):
                dve.tensor_scalar(cb[:, f * P:(f + 1) * P], ones[:, :], c0[:, f * 2:f * 2 + 1], None, ALU.mult)\
                   .then_inc(cb_ready, 1)
            cast(1)
            copy_transposes(0, ht)
            cast(2)
            low_parts(0)
            cast(3)
            copy_rows(1, 7)
            dve.wait_ge(srow_mm, 1)
            dve.wait_ge(srow_copied, 1)
            dve.tensor_scalar(frow[:, W:2 * W], frow[:, 0:W], 0.01, None, ALU.mult)\
               .then_inc(srow_copied, 1)
            dve.wait_ge(cols_mm, 1)
            for k, dst, scale in ((2, srt, -0.01), (2, sr99, 0.99)):
                for d, v in by_node(dst, 6, k):
                    dve.tensor_scalar(d, v, scale, None, ALU.mult).then_inc(r3_copied, 1)
            for k in range(2):
                for d, v in by_node(gab[:, k * T:(k + 1) * T], 6, k):
                    dve.tensor_scalar(d, v, rowv[:, R_BA + k:R_BA + k + 1], None, ALU.add).then_inc(r3_copied, 1)
            dve.wait_ge(srow_copied, 2)
            dve.wait_ge(r3_copied, 8)

            def score_arg(j):
                dve.scalar_tensor_tensor(tt[:, ds((j % 2) * W, W)], frow[:, 0:W], sr99[:, ds(j, 1)],
                                         frow[:, W:2 * W], ALU.add, ALU.max).then_inc(tile_arg, 1)

            def mask(n, j):
                dve.wait_ge(tile_exp, n + 1)
                w = ring[:, ds((n % RING) * W, W)]
                dve.tensor_tensor(w, w, at[:, ds(j * W, W)], ALU.mult).then_inc(tile_masked, 1)

            dve.wait_ge(cast_act, min(3, T - CD))
            score_arg(0)
            with dve.Fori(1, RING + 1) as j:
                score_arg(j)
                mask(j - 1, j - 1)
            copy_aggregate(agg_done, 1, ga)
            for t in range(T):
                dve.wait_ge(xb_mm, t + 1)
                dve.tensor_tensor(xb[:, t * D:(t + 1) * D], ps[:, 6 + t % 2, 0:D], rowv[:, R_GCNB:R_GCNB + D],
                                  ALU.add).then_inc(xb_added, 1)
                dve.tensor_tensor(gates.rearrange("p (k t) -> p t k", k=2)[:, t], ps[:, 6 + t % 2, D:DG],
                                  gab.rearrange("p (k t) -> p t k", k=2)[:, t], ALU.add).then_inc(xb_added, 1)
            dve.wait_ge(gate_tanh, 1)
            dve.tensor_scalar(attn, gates, 0.5, 0.5, ALU.mult, ALU.add).then_inc(gate_attn, 1)
            with dve.Fori(RING + 1, T) as j:
                score_arg(j)
                mask(j - 1, j - 1)
            mask(T - 1, T - 1)
            link(dve.tensor_scalar(x[:, :], x[:, :], 0.5, None, ALU.add))
            copy_rows(2, 6)
            copy_aggregate(tile_used, B0 + T, gb)
            dve.wait_ge(cols_mm, 2)
            for d, v in by_node(rs, 7, 0):
                link(dve.tensor_scalar(d, v, L0_EPS, None, ALU.add))
            link(dve.reciprocal(rs, rs))
            link(dve.tensor_tensor(ca, attn[:, 0:T], rs, ALU.mult))
            dve.wait_ge(xb_scaled, T)

            def l0_mix(r):
                dve.wait_ge(np_mm, r + 1)
                for u in range(min(2, T - 2 * r)):
                    t = 2 * r + u
                    dve.scalar_tensor_tensor(e_pair[r % 2][:, u * D:(u + 1) * D], ps[:, r % 4, u * D:(u + 1) * D],
                                             ca[:, t:t + 1], xb[:, t * D:(t + 1) * D], ALU.mult, ALU.add)\
                       .then_inc(np_mixed, 1)

            def degrees():
                link(dve.tensor_scalar(dmax, ps[:, 7, 384:384 + T], 1.0, None, ALU.max))
                link(dve.reciprocal(dinv, dmax))
                note(dve.tensor_scalar(deg1, dmax, 1.0, None, ALU.add))
                link(dve.tensor_scalar(ndeg1, dmax, -1.0, -1.0, ALU.mult, ALU.add))
                dve.sem_inc(dinv_ready, 1)

            l0_mix(0)
            for r in range(TR):
                if r == 1:
                    degrees()
                if r:
                    dve.wait_ge(np_done, r)
                if r + 1 < TR:
                    l0_mix(r + 1)
                if r:
                    round_stats(1, r - 1)
                a, k = 2 * r * D, min(2, T - 2 * r) * D
                dve.wait_ge(np_act, r + 1)
                dve.scalar_tensor_tensor(x[:, a:a + k], e_pair[r % 2][:, 0:k], 0.5, x[:, a:a + k], ALU.mult,
                                         ALU.add).then_inc(np_done, 1)
            dve.wait_ge(np_done, TR)
            round_stats(1, TR - 1)

            dve.wait_ge(c1_mm, 1)
            link(dve.tensor_copy(fm(c1)[:, :, 0:8], ps[:, 0, 0:F * 8].rearrange("p (f n) -> p f n", f=F)))
            for hd in range(H):
                dve.tensor_scalar(cb[:, hd * P:(hd + 1) * P], ones[:, :],
                                  c1[:, (hd // 2) * 32 + 2 * hd:(hd // 2) * 32 + 2 * hd + 1], None, ALU.mult)\
                   .then_inc(cb_ready, 1)
            dve.wait_ge(w_loaded, 16 * NWR)
            cv = colv[:, :].rearrange("p (f k) -> p k f", k=8)
            for k, i in enumerate((EM_B, DM_B)):
                a = 2 * k * F
                note(dve.tensor_scalar(ncol[:, a:a + F], cv[:, i], -1.0, None, ALU.mult))
                link(dve.tensor_scalar(ncol[:, a + F:a + 2 * F], cv[:, i], -1.0, -1.0, ALU.mult, ALU.add))
            dve.sem_inc(ncol_ready, 1)
            copy_transposes(1, ht)

            def misc(*name):
                u = MISC.index(name)
                dve.wait_ge(misc_mm, u + 1)
                return 6 + u % 2

            def copy_frow(hd):
                for c in range(NC):
                    b = misc("frow", hd, c)
                    a = hd * W + c * C
                    dve.tensor_copy(frow[:, a:a + C], ps[:, b, 0:C]).then_inc(frow_ready, 1)
                    dve.wait_ge(frow_ready, NC * hd + c + 1)
                    dve.sem_inc(misc_read, 1)

            copy_rows(3, 1)
            dve.wait_ge(cols_mm, 3)
            for hd in range(H):
                for d, v in by_node(f2[:, hd * T:(hd + 1) * T], 2, 2 * hd + 1):
                    dve.tensor_scalar(d, v, 0.5, None, ALU.mult).then_inc(f2_copied, 1)

            def masks(first, j0, j1):
                with dve.Fori(j0, j1) as j:
                    mask(first + j, j)

            def copy_head(hd):
                b, pr = hd % 2, hd // 2
                mine, other = b * DH, (1 - b) * DH
                banks = ps[:, b * NC:(b + 1) * NC, 0:C]
                dve.wait_ge(tile_used, BE + (hd + 1) * T)
                dve.tensor_scalar(chunks(rinv, pr)[mine:mine + DH], banks[other:other + DH], 0.25, None,
                                  ALU.max).then_inc(head_copied, 1)
                if hd < H - 1:
                    dve.tensor_copy(chunks(ga, pr)[mine:mine + DH], banks[mine:mine + DH]).then_inc(head_copied, 1)

            def invert(pr):
                for k in range(2):
                    b = misc("sums", pr, k)
                    n = min(ST, T - k * ST)
                    link(dve.reciprocal(rcol[:, 2 * k * ST:2 * (k * ST + n)].rearrange("p (t s) -> p t s", s=2),
                                        ps[:, b, 0:n * SR].rearrange("p (t r) -> p t r", r=SR)[:, :, 0:SR:DH]))
                    dve.sem_inc(misc_read, 1)
                dve.tensor_copy(rbc.rearrange("p (k d) -> p k d", d=DH),
                                rcol[:, :].unsqueeze(2).to_broadcast([P, 2 * T, DH])).then_inc(rbc_ready, 1)

            def normalise(pr, steps):
                for step, c in steps:
                    b = misc("spread", pr, c)
                    w = min(4 * P, W - c * 4 * P)
                    a = pr * NP + c * 4 * P
                    if step == "scale":
                        dve.tensor_tensor(ga[:, a:a + w], ga[:, a:a + w], ps[:, b, 0:w], ALU.mult)\
                           .then_inc(norm_ready, 1)
                    else:
                        link(dve.tensor_copy(rinv[:, a:a + w], ps[:, b, 0:w]))
                        dve.sem_inc(misc_read, 1)

            for hd in range(H):
                first = BE + hd * T
                masks(first, 0, 3)
                if hd < H - 1:
                    copy_frow(hd + 1)
                if hd:
                    copy_head(hd - 1)
                if hd == 2:
                    masks(first, 3, T - 1)
                    invert(0)
                    masks(first, T - 1, T)
                elif hd == 3:
                    masks(first, 3, 6)
                    normalise(0, (("scale", 0), ("keep", 0), ("scale", 1), ("keep", 1)))
                    masks(first, 6, T - 1)
                    normalise(0, (("scale", 2), ("keep", 2)))
                    masks(first, T - 1, T)
                else:
                    masks(first, 3, T)

            def batch_stats(k, f, src, gamma, beta):
                for c in range(NC):
                    last = dve.bn_stats(bnst[:, (f * NC + c) * 6:(f * NC + c + 1) * 6], src(c, min(C, N - c * C)))
                    (link if c == NC - 1 else note)(last)
                link(dve.bn_aggr(bnag[:, f * 2:(f + 1) * 2], bnst[:, f * NC * 6:(f + 1) * NC * 6]))
                mean, var = bnag[:, 2 * f:2 * f + 1], bnag[:, 2 * f + 1:2 * f + 2]
                rs_, a, b = (bnv[:, i * F + f:i * F + f + 1] for i in range(3))
                dve.tensor_scalar(rs_, var, BN_EPS, None, ALU.add).then_inc(bn_var, 1)
                dve.wait_ge(bn_pow, F * k + f + 1)
                link(dve.tensor_tensor(a, rs_, col(gamma, f), ALU.mult))
                link(dve.tensor_tensor(b, mean, a, ALU.mult))
                dve.tensor_tensor(b, col(beta, f), b, ALU.subtract).then_inc(bn_cols, 1)

            def batch_affine(k, dst, src):
                dve.wait_ge(bn_cols, F * k + 2)
                dve.tensor_scalar(chunks(dst, 1), src, bnv[:, F + 1:F + 2], bnv[:, 2 * F + 1:2 * F + 2],
                                  ALU.mult, ALU.add).then_inc(aff_dve, 1)

            def elu(n, f, which, residual, dst, done):
                e = frow[:, 2 * f * W:(2 * f + 1) * W].rearrange("p (c n) -> p c n", c=NC)
                v = ps[:, f * NC:(f + 1) * NC, 0:C]
                dve.wait_ge(elu_exp, n + 1)
                if residual is None:
                    dve.scalar_tensor_tensor(chunks(dst, f), e, -1.0, v, ALU.add, ALU.max).then_inc(done, 1)
                    return
                link(dve.scalar_tensor_tensor(chunks(dst, f), e, ncol[:, (2 * which + 1) * F + f:(2 * which + 1) * F + f + 1],
                                              v, ALU.add, ALU.max))
                dve.scalar_tensor_tensor(dst[:, f * NP:f * NP + W], dst[:, f * NP:f * NP + W],
                                         col((EM_B, DM_B)[which], f), residual[:, f * NP:f * NP + W],
                                         ALU.add, ALU.add).then_inc(done, 1)

            def col(i, f):
                return colv[:, f * 8 + i:f * 8 + i + 1]

            def in_ga(f):
                return lambda c, n: ga[:, f * NP + c * C:f * NP + c * C + n]

            def projected_stats(f):
                dve.wait_ge(proj_mm, f + 1)
                batch_stats(0, f, lambda c, n: ps[:, f * NC + c, 0:n], E_G, E_B)

            projected_stats(0)
            copy_head(H - 1)
            invert(1)
            dve.wait_ge(num_copied, 1)
            normalise(1, (("scale", 0), ("keep", 0), ("scale", 1), ("scale", 2), ("keep", 1), ("keep", 2)))
            projected_stats(1)
            batch_affine(0, gb, ps[:, NC:2 * NC, 0:C])
            masks(BD, 0, 3)
            dve.wait_ge(aff_dve, 1)
            dve.wait_ge(aff_act, 1)
            for f in range(F):
                elu(f, f, 0, gb, ga, mlp_sum)
                dve.wait_ge(mlp_sum, f + 1)
                batch_stats(1, f, in_ga(f), EM_G, EM_BB)
            batch_affine(1, ht, chunks(ga, 1))

            def average(q):
                dve.wait_ge(tile_used, BD + T * (q + 1))
                dve.tensor_tensor(chunks(ga, q), ps[:, q * NC:(q + 1) * NC, 0:C], chunks(rinv, q),
                                  ALU.mult).then_inc(norm_dec, 1)

            masks(BD, 3, T)
            for q in range(ER):
                dve.wait_ge(emb_mm, ER + q + 1)
                dve.tensor_copy(node_block(h, 1, q), bank_block(6 + (ER + q) % 2, q)).then_inc(emb_dve, 1)
            masks(BD + T, 0, 3)
            average(0)
            masks(BD + T, 3, 7)
            elu(F, 0, 0, None, gb, dec_ready)
            masks(BD + T, 7, T)
            dve.wait_ge(tile_masked, BD + ND)
            on_diagonal(deg1, diag_added)
            average(1)
            elu(F + 1, 1, 0, None, gb, dec_ready)
            dve.wait_ge(dec_ready, F)
            for f in range(F):
                elu(2 * F + f, f, 1, gb, ga, mlp_sum)
                dve.wait_ge(mlp_sum, F + f + 1)
                batch_stats(2, f, in_ga(f), DM_G, DM_BB)
            batch_affine(2, ht, chunks(ga, 1))
            for r in range(TR):
                dve.wait_ge(tr_done, 2 * TR + r + 1)
                a, b = 2 * r * D, min(2 * r + 2, T) * D
                dve.tensor_tensor(x[:, a:b], x[:, a:b], ps[:, 6 + r % 2, 0:b - a], ALU.add).then_inc(tr_copied, 1)
                if r:
                    dve.wait_ge(tr_copied, 2 * TR + r)
                    round_stats(2, r - 1)

            dve.wait_ge(tr_copied, 3 * TR)
            round_stats(2, TR - 1)
            low_parts(1)
            copy_aggregate(agg_done, 2, ga)

            def l2_scale(r):
                dve.wait_ge(np_mm, TR + r + 1)
                for u in range(min(2, T - 2 * r)):
                    dve.scalar_tensor_tensor(e_pair[r % 2][:, u * D:(u + 1) * D], ps[:, r % 4, u * D:(u + 1) * D],
                                             dinv[:, 2 * r + u:2 * r + u + 1], rowv[:, R_L2B:R_L2B + D], ALU.mult,
                                             ALU.add).then_inc(np_mixed, 1)

            l2_scale(0)
            for r in range(TR):
                if r:
                    dve.wait_ge(np_done, TR + r)
                if r + 1 < TR:
                    l2_scale(r + 1)
                if r:
                    round_stats(3, r - 1)
                a, k = 2 * r * D, min(2, T - 2 * r) * D
                dve.wait_ge(np_mixed, T + min(2 * r + 2, T))
                dve.scalar_tensor_tensor(x[:, a:a + k], e_pair[r % 2][:, 0:k], 0.0, x[:, a:a + k], ALU.max,
                                         ALU.add).then_inc(np_done, 1)
            dve.wait_ge(np_done, 2 * TR)
            round_stats(3, TR - 1)

            copy_transposes(3, ht)
            def square_norms(a, b):
                for t in range(a, b):
                    dve.wait_ge(hn_copied, t + 1)
                    note(dve.scalar_tensor_tensor(gb[:, t * D:(t + 1) * D], h[:, t * D:(t + 1) * D], 1.0,
                                                  h[:, t * D:(t + 1) * D], ALU.mult, ALU.mult,
                                                  accum_out=n2[:, t:t + 1]))

            def norm_floor(half):
                a, b = HALVES[half]
                dve.wait_ge(dve_own, own[0])
                dve.tensor_scalar(n2[:, a:b], n2[:, a:b], NORM_EPS * NORM_EPS, None, ALU.max).then_inc(nrm_done, 1)

            def unit_rows(half):
                dve.wait_ge(nrm_pow, half + 1)
                for t in range(*HALVES[half]):
                    dve.tensor_scalar(ga[:, t * D:(t + 1) * D], h[:, t * D:(t + 1) * D], nsum[:, t:t + 1], None,
                                      ALU.mult).then_inc(hn_done, 1)

            square_norms(*HALVES[0])
            norm_floor(0)
            square_norms(HALVES[1][0], HALVES[1][0] + 3)
            unit_rows(0)
            square_norms(HALVES[1][0] + 3, T)
            norm_floor(1)
            for r in range(TR):
                if r == 2:
                    unit_rows(1)
                dve.wait_ge(hi_done, r + 1)
                k = min(2, T - 2 * r)
                hi = fm(h_hi)[:, :, 2 * r * P:(2 * r + k) * P]
                dve.tensor_tensor(fm(h_lo)[:, :, 2 * r * P:(2 * r + k) * P],
                                  ps[:, 6 + r % 2, 0:F * 2 * P].rearrange("p (f n) -> p f n", f=F)[:, :, 0:k * P],
                                  hi, ALU.subtract).then_inc(tr_copied, 1)
            dve.wait_ge(agg_done, 2)
            dve.wait_ge(diag_added, T)
            on_diagonal(ndeg1, diag_removed)
            dve.wait_ge(diag_removed, T)
            with dve.Fori(0, T) as j:
                dve.wait_ge(sim_exp, NC * j + NC)
                w = ring[:, ds(((B3 + j) % RING) * W, W)]
                dve.scalar_tensor_tensor(w, at[:, ds(j * W, W)], epsv[:, ds(j, 1)], w, ALU.add, ALU.mult)\
                   .then_inc(tile_masked, 1)
            dve.tensor_tensor(x[:, :].rearrange("p (t d) -> p t d", d=D), x[:, :].rearrange("p (t d) -> p t d", d=D),
                              rowv[:, R_L3B:R_L3B + D].unsqueeze(1).to_broadcast([P, T, D]), ALU.add)\
               .then_inc(bias_done, 1)
            copy_rows(4, 6)
            dve.wait_ge(cols_mm, 4)
            for d, v in by_node(rs, 7, 0):
                link(dve.tensor_scalar(d, v, 1e-30, None, ALU.max))
            link(dve.reciprocal(rs, rs))
            copy_aggregate(tile_used, B3 + T, ga)
            dve.wait_ge(bias_done, 1)
            for t in range(T):
                dve.wait_ge(tr_done, 5 * TR + t // 2 + 1)
                a = (t % 2) * D
                last = dve.scalar_tensor_tensor(x[:, t * D:(t + 1) * D], ps[:, 6 + (t // 2) % 2, a:a + D],
                                                rs[:, t:t + 1], x[:, t * D:(t + 1) * D], ALU.mult, ALU.add)
                last.then_inc(np_done, 1)

        @block.tensor
        def _(pe):
            pe.wait_ge(consts, NCONST)

            def weight(i, f):
                return wt[:, (i * F + f) * D:(i * F + f + 1) * D]

            def to_feature_major(batch, src, ready, base):
                for r in range(TR):
                    if batch and r:
                        keep_clock(3 if r == 2 else 1, 5)
                    pe.wait_ge(ready, base + min(2 * r + 2, T))
                    if r >= 2:
                        pe.wait_ge(tr_copied, batch * TR + r - 1)
                    for f in range(F):
                        for u in range(min(2, T - 2 * r)):
                            a = (2 * r + u) * D + f * P
                            last = pe.transpose(ps[:, 6 + r % 2, f * 2 * P + u * P:f * 2 * P + (u + 1) * P],
                                                src[:, a:a + P], ident[:, :])
                    last.then_inc(tr_done, 1)

            def to_node_major(batch, src):
                for r in range(TR):
                    if r >= 2:
                        if batch == 5:
                            pe.wait_ge(np_done, 2 * TR + 2 * (r - 1))
                        else:
                            pe.wait_ge(tr_copied, batch * TR + r - 1)
                    for u in range(min(2, T - 2 * r)):
                        for f in range(F):
                            a = f * NP + (2 * r + u) * P
                            last = pe.transpose(ps[:, 6 + r % 2, u * D + f * P:u * D + (f + 1) * P],
                                                src[:, a:a + P], ident[:, :])
                    last.then_inc(tr_done, 1)

            def node_product(dst, src, t, rhs, n):
                for f in range(F):
                    last = pe.matmul(dst, src[:, f * NP + t * P:f * NP + (t + 1) * P], rhs(f)[:, 0:n],
                                     start=f == 0, stop=f == F - 1)
                return last

            def keep_clock(n, bank):
                with pe.Fori(0, n):
                    for _ in range(2):
                        pe.matmul(ps[:, bank, 384:512], ident[:, :], ident[:, :], start=True, stop=True)

            def node_rows(bank, src, values, first=True, more=False, width=NP):
                for f, v in enumerate(values):
                    for c in range(ER):
                        w = min(512, width - 512 * c)
                        last = pe.matmul(ps[32 * c:32 * c + 32, bank, 0:w], v,
                                         src[:, f * width + 512 * c:f * width + 512 * c + w],
                                         start=first and f == 0, stop=not more and f == len(values) - 1)
                if not more:
                    last.then_inc(rows_mm, 1)

            def node_columns(n, bank):
                pe.wait_ge(rows_copied, 2 * n)
                for u in range(4):
                    k = 32 * len(range(u, T, 4))
                    last = pe.transpose(ps[:, bank, u * 96:u * 96 + k], row_buf[0:k, u * P:(u + 1) * P],
                                        ident[0:k, 0:k])
                last.then_inc(cols_mm, 1)

            def aggregate(k):
                def tile(j, start, stop):
                    for f in range(F):
                        for part in (h_hi, h_lo):
                            for c in range(NC):
                                last = pe.matmul(ps[:, f * NC + c, 0:C], part[:, ds(j * D + f * P, P)],
                                                 at[:, ds(j * W + c * C, C)], start=start and part is h_hi,
                                                 stop=stop and part is h_lo)
                    return last
                pe.wait_ge(h16_done, k + 1)
                tile(0, True, False)
                with pe.Fori(1, CD) as j:
                    tile(j, False, False)
                pe.wait_ge(h16_done, k + 2)
                with pe.Fori(CD, T - 1) as j:
                    if k == 0:
                        pe.wait_ge(cast_act, j - CD + 1)
                        pe.wait_ge(cast_dve, CD)
                    tile(j, False, False)
                if k == 0:
                    pe.wait_ge(cast_act, T - CD)
                tile(T - 1, False, True).then_inc(agg_done, 1)

            def weighted(base, vbase):
                def tile(j, slot, start, stop):
                    pe.wait_ge(vs_ready, vbase + j + 1)
                    pe.wait_ge(tile_masked, base + j + 1)
                    for f in range(F):
                        for c in range(NC):
                            last = pe.matmul(ps[:, f * NC + c, 0:C], vs[:, slot * D + f * P:slot * D + (f + 1) * P],
                                             ring[:, ds(((base + j) % RING) * W + c * C, C)], start=start, stop=stop)
                    last.then_inc(tile_used, 1)
                return tile

            pe.wait_ge(w0_loaded, 16 * NW0)
            for d in range(F):
                for f in range(F):
                    last = pe.matmul(ps[:, 0, d * 2:d * 2 + 2], weight(W_SA_T, f)[:, d * P:(d + 1) * P],
                                     a2[:, f * 2:f * 2 + 2], start=f == 0, stop=f == F - 1)
            last.then_inc(c0_mm, 1)
            to_feature_major(0, h, h_done, 0)
            pe.wait_ge(c0_copied, 1)
            pe.wait_ge(tr_copied, TR)
            node_rows(7, ht, [r3[:, f * 32:(f + 1) * 32] for f in range(F)])
            pe.wait_ge(cb_ready, F)
            for c in range(NC):
                for f in range(F):
                    last = pe.matmul(ps[:, 2 + c, 0:C], cb[:, f * P:(f + 1) * P],
                                     ht[:, f * NP + c * C:f * NP + (c + 1) * C], start=f == 0, stop=f == F - 1)
            last.then_inc(srow_mm, 1)
            node_columns(1, 6)
            pe.wait_ge(cast_dve, CD)
            pe.wait_ge(srow_copied, 1)
            aggregate(0)
            pe.wait_ge(agg_copied, 2)

            pe.wait_ge(wl0_loaded, 16 * NWL0)
            pe.wait_ge(r3_copied, 8)
            for t in range(T):
                if t >= 2:
                    pe.wait_ge(xb_added, 2 * (t - 1))
                node_product(ps[:, 6 + t % 2, 0:DG], ga, t, lambda f: wg[:, f * DG:(f + 1) * DG], DG)\
                    .then_inc(xb_mm, 1)
            tile = weighted(B0, 0)
            tile(0, 0, True, False)
            with pe.Fori(1, T - 2, 2) as j:
                tile(j, 1, False, False)
                tile(j + 1, 0, False, False)
            tile(T - 2, 1, False, False)
            pe.wait_ge(tile_summed, 2 * T)
            pe.wait_ge(xb_added, 2 * T)
            node_rows(6, s_acc, [ones[:, 0:32]])
            for t in range(T):
                pe.matmul(ps[:, 7, 384 + t:385 + t], d_acc[:, t * P:(t + 1) * P], ones16[:, 0:1], start=True, stop=True)
            tile(T - 1, 0, False, True)
            node_columns(2, 7)

            def node_products(src, i, read_before):
                for r in range(TR):
                    if r >= 4:
                        pe.wait_ge(np_mixed, read_before + 2 * (r - 3))
                    for u in range(min(2, T - 2 * r)):
                        last = node_product(ps[:, r % 4, u * D:(u + 1) * D], src, 2 * r + u, lambda f: weight(i, f), D)
                    last.then_inc(np_mm, 1)

            pe.wait_ge(agg_copied, 4)
            node_products(gb, W_SA, 0)
            keep_clock(8, 5)

            pe.wait_ge(w_loaded, 16 * NWR)
            pe.wait_ge(np_mixed, T)
            for pr in range(F):
                last = pe.matmul(ps[:, 0, pr * 8:pr * 8 + 8], wbd[:, (W_BD_T * F + pr) * P:(W_BD_T * F + pr + 1) * P],
                                 vb[:, pr * 8:(pr + 1) * 8], start=True, stop=True)
            last.then_inc(c1_mm, 1)
            pe.wait_ge(dinv_ready, 1)
            to_feature_major(1, h, h_done, T)
            pe.wait_ge(cb_ready, F + H)
            pe.wait_ge(tr_copied, 2 * TR)

            def misc(*name):
                u = MISC.index(name)
                if u >= 2:
                    pe.wait_ge(misc_read, u - 1)
                return 6 + u % 2

            def make_frow(hd):
                pr = hd // 2
                for c in range(NC):
                    b = misc("frow", hd, c)
                    pe.matmul(ps[:, b, 0:C], cb[:, hd * P:(hd + 1) * P],
                              ht[:, pr * NP + c * C:pr * NP + (c + 1) * C], start=True, stop=True)\
                      .then_inc(misc_mm, 1)

            node_rows(1, ht, [c1[:, f * 32:(f + 1) * 32] for f in range(F)])
            make_frow(0)
            node_columns(3, 2)

            def gather_sums(pr):
                pe.wait_ge(head_copied, 4 * pr + 4 if pr == 0 else 2 * H - 1)
                for k in range(2):
                    b = misc("sums", pr, k)
                    for t in range(k * ST, min((k + 1) * ST, T)):
                        last = pe.transpose(ps[:, b, (t - k * ST) * SR:(t - k * ST + 1) * SR],
                                            rinv[0:SR, pr * NP + t * P:pr * NP + (t + 1) * P], ident[0:SR, 0:SR])
                    last.then_inc(misc_mm, 1)

            def spread_inverse(pr, chunks_=range(NC)):
                pe.wait_ge(rbc_ready, pr + 1)
                for c in chunks_:
                    b = misc("spread", pr, c)
                    for t in range(4 * c, min(4 * c + 4, T)):
                        last = pe.transpose(ps[:, b, (t - 4 * c) * P:(t - 4 * c + 1) * P],
                                            rbc[:, t * P:(t + 1) * P], ident[:, :])
                    last.then_inc(misc_mm, 1)

            def project(which, pr):
                for c in range(NC):
                    last = pe.matmul(ps[:, pr * NC + c, 0:C], wbd[:, (which * F + pr) * P:(which * F + pr + 1) * P],
                                     ga[:, pr * NP + c * C:pr * NP + (c + 1) * C], start=True, stop=True)
                last.then_inc(proj_mm, 1)

            pe.wait_ge(f2_copied, 2 * H)
            for hd in range(H):
                b = hd % 2
                if hd >= 2:
                    pe.wait_ge(head_copied, 2 * (hd - 1))

                def enc_tile(j, par, start, stop):
                    n = hd * T + j
                    pe.wait_ge(vs_ready, T + n + 1)
                    pe.wait_ge(tile_masked, BE + n + 1)
                    for c in range(NC):
                        last = pe.matmul(ps[:, b * NC + c, 0:C], vs[:, (b * 2 + par) * P:(b * 2 + par + 1) * P],
                                         ring[:, ds(((BE + n) % RING) * W + c * C, C)], start=start, stop=stop)
                    return last.then_inc(tile_used, 1)

                s = (hd * T) % 2
                enc_tile(0, s, True, False)
                if hd < H - 1:
                    make_frow(hd + 1)
                if hd == 3:
                    spread_inverse(0, range(2))
                with pe.Fori(1, 5, 2) as j:
                    enc_tile(j, 1 - s, False, False)
                    enc_tile(j + 1, s, False, False)
                if hd == 2:
                    gather_sums(0)
                if hd == 3:
                    spread_inverse(0, range(2, NC))
                with pe.Fori(5, T - 2, 2) as j:
                    enc_tile(j, 1 - s, False, False)
                    enc_tile(j + 1, s, False, False)
                if hd == H - 1:
                    pe.wait_ge(norm_ready, NC)
                    pe.wait_ge(head_copied, 2 * (H - 1))
                    project(W_BD, 0)
                enc_tile(T - 2, 1 - s, False, False)
                enc_tile(T - 1, s, False, True)

            def mlp_part(i, fi, fo):
                for c in range(NC):
                    last = pe.matmul(ps[:, fo * NC + c, 0:C], weight(i, fi)[:, fo * P:(fo + 1) * P],
                                     gb[:, fi * NP + c * C:fi * NP + (c + 1) * C], start=fi == 0, stop=fi == F - 1)
                return last

            keep_clock(3, 7)
            gather_sums(1)
            pe.wait_ge(aff_act, 1)
            keep_clock(3, 0)
            spread_inverse(1, range(2))
            keep_clock(2, 0)
            spread_inverse(1, range(2, NC))
            keep_clock(2, 0)
            pe.wait_ge(norm_ready, 2 * NC)
            project(W_BD, 1)
            mlp_part(MLP_E, 0, 0)
            pe.wait_ge(misc_read, len(MISC))
            keep_clock(4, 7)
            pe.wait_ge(aff_dve, 1)
            mlp_part(MLP_E, 1, 0).then_inc(mlp_mm, 1)
            mlp_part(MLP_E, 0, 1)
            mlp_part(MLP_E, 1, 1).then_inc(mlp_mm, 1)
            def embedding_to_node_major(f):
                for q in range(ER):
                    n = f * ER + q
                    if n >= 2:
                        pe.wait_ge(emb_act, min(n - 1, ER))
                        if n > ER + 1:
                            pe.wait_ge(emb_dve, n - 1 - ER)
                    for t in range(4 * q, min(4 * q + 4, T)):
                        last = pe.transpose(ps[:, 6 + n % 2, (t - 4 * q) * P:(t - 4 * q + 1) * P],
                                            ht[:, f * NP + t * P:f * NP + (t + 1) * P], ident[:, :])
                    last.then_inc(emb_mm, 1)

            keep_clock(12, 7)
            pe.wait_ge(aff_act, 2)
            embedding_to_node_major(0)

            for pr in range(2):
                def dec_tile(j, u, start, stop):
                    n, s = pr * T + j, pr * T + u
                    pe.wait_ge(vs_ready, T + NE + n + 1)
                    pe.wait_ge(loaded[s % 2], 16 * (n // 2 + 1))
                    pe.wait_ge(tile_masked, BD + n + 1)
                    for b, tile_ in ((0, back[:, s % RING * W:(s % RING + 1) * W]),
                                     (1, ring[:, (BD + s) % RING * W:((BD + s) % RING + 1) * W])):
                        for c in range(NC):
                            last = pe.matmul(ps[b * DH:(b + 1) * DH, pr * NC + c, 0:C],
                                             vs[:, s % 2 * P + b * DH:s % 2 * P + (b + 1) * DH],
                                             tile_[:, c * C:(c + 1) * C], start=start, stop=stop)
                    last.then_inc(tile_used, 1)

                dec_tile(0, 0, True, False)
                if pr == 1:
                    pe.wait_ge(norm_dec, 1)
                    project(W_BD_T, 0)
                with pe.Fori(1, 9, RING) as j:
                    for u in range(RING):
                        dec_tile(j + u, 1 + u, False, False)
                if pr == 0:
                    pe.wait_ge(aff_dve, 2)
                    embedding_to_node_major(1)
                else:
                    pe.wait_ge(dec_ready, 1)
                    mlp_part(MLP_D, 0, 0)
                dec_tile(9, 9, False, False)
                dec_tile(10, 10, False, True)
            pe.wait_ge(norm_dec, 2)
            project(W_BD_T, 1)
            pe.wait_ge(emb_dve, ER)
            keep_clock(6, 7)
            pe.wait_ge(dec_ready, F)
            mlp_part(MLP_D, 1, 0).then_inc(mlp_mm, 1)
            mlp_part(MLP_D, 0, 1)
            mlp_part(MLP_D, 1, 1).then_inc(mlp_mm, 1)
            keep_clock(20, 7)
            pe.wait_ge(aff_act, 3)
            pe.wait_ge(aff_dve, 3)
            to_node_major(2, ht)

            pe.wait_ge(tr_copied, 3 * TR)
            keep_clock(8, 7)
            pe.wait_ge(diag_added, T)
            aggregate(2)
            pe.wait_ge(agg_copied, 6)
            node_products(ga, W_L2, T)
            keep_clock(10, 7)

            to_feature_major(3, h, h_done, 3 * T)
            pe.wait_ge(tr_copied, 4 * TR)
            for t in range(T):
                if t >= 4:
                    pe.wait_ge(hn_copied, t - 3)
                node_product(ps[:, t % 4, 0:D], ht, t, lambda f: weight(W_L3, f), D).then_inc(hn_mm, 1)
            to_feature_major(4, ga, hn_done, 0)
            pe.wait_ge(tr_copied, 5 * TR)

            def similarity(j):
                for c in range(NC):
                    if c < 2:
                        pe.wait_ge(sim_exp, NC * j + c - 1)
                    else:
                        pe.wait_ge(sim_exp, NC * j + 1)
                    pairs = [(a, b, f) for a, b in ((h_hi, h_hi), (h_hi, h_lo), (h_lo, h_hi)) for f in range(F)]
                    for k, (a, b, f) in enumerate(pairs):
                        if k == 0:
                            pe.wait_ge(tr_copied, 5 * TR)
                        last = pe.matmul(psf[:, ds((6 + (j + c) % 2) * 512, C)], a[:, ds(f * NP + j * P, P)],
                                         b[:, f * NP + c * C:f * NP + (c + 1) * C], start=k == 0,
                                         stop=k == len(pairs) - 1)
                    last.then_inc(sim_mm, 1)

            def similarity_first():
                for c in range(NC):
                    if c == 2:
                        pe.wait_ge(sim_exp, 1)
                    pairs = [(a, b, f) for a, b in ((h_hi, h_hi), (h_hi, h_lo), (h_lo, h_hi)) for f in range(F)]
                    for k, (a, b, f) in enumerate(pairs):
                        last = pe.matmul(ps[:, 6 + c % 2, 0:C], a[:, f * NP:f * NP + P],
                                         b[:, f * NP + c * C:f * NP + (c + 1) * C], start=k == 0,
                                         stop=k == len(pairs) - 1)
                    last.then_inc(sim_mm, 1)

            tile = weighted(B3, T + NE + ND)
            similarity_first()
            similarity(1)
            tile(0, 0, True, False)
            with pe.Fori(1, T - 2, 2) as j:
                similarity(j + 1)
                tile(j, 1, False, False)
                similarity(j + 2)
                tile(j + 1, 0, False, False)
            similarity(T - 1)
            tile(T - 2, 1, False, False)
            pe.wait_ge(tile_summed, 3 * T)
            pe.wait_ge(sim_exp, NC * T)
            node_rows(6, s_acc, [ones[:, 0:32]], more=True)
            pe.wait_ge(tile_masked, B3 + T)
            a = (B3 + T - 1) % RING * W
            node_rows(6, ring[:, a:a + W], [ones[:, 0:32]], first=False, width=W)
            tile(T - 1, 0, False, True)
            node_columns(4, 7)
            keep_clock(5, 6)
            pe.wait_ge(agg_copied, 8)
            to_node_major(5, ga)


def kernel(**inputs):
    import numpy as np
    import concourse.bacc as bacc
    from concourse.bass_utils import run_bass_kernel_spmd

    a = {k: np.ascontiguousarray(v) for k, v in inputs.items()}
    n, d = a["x"].shape
    tiles = -(-n // P)
    width = -(-n // 3) * 3
    heads, dh = a["L1_gnn_W"].shape[:2]

    def zeros(*shape):
        return np.zeros(shape, np.float32)

    x = zeros(tiles * P, d)
    x[:n] = a["x"]
    adj_t = zeros(tiles * P, width)
    adj_t[:n, :n] = a["adj"].T
    bd, bdt, vb = zeros(d, P), zeros(d, P), zeros(d, 2 * heads)
    for i in range(heads):
        rows_, c = slice(i * dh, (i + 1) * dh), (i % 2) * dh
        bd[rows_, c:c + dh] = a["L1_gnn_W"][i]
        bdt[rows_, c:c + dh] = a["L1_gnn_W"][i].T
        vb[rows_, 2 * i] = a["L1_gnn_V"][i, 0, :, 0]
        vb[rows_, 2 * i + 1] = a["L1_gnn_V"][i, 1, :, 0]
    mats = [a["L0_gnn_W_sa"], a["L0_gnn_W_sa"].T, a["L1_gnn_enc_mlp_W"].T,
            a["L1_gnn_dec_mlp_W"].T, a["L2_gnn_W"], a["L3_gnn_weight"]]
    wa, wb, asa = a["L0_gnn_Wa"][0], a["L0_gnn_Wb"][0], a["L0_gnn_a_sa"][0]
    names = ["enc_bn_gamma", "enc_bn_beta", "enc_mlp_b", "enc_mlp_bn_gamma", "enc_mlp_bn_beta",
             "dec_mlp_b", "dec_mlp_bn_gamma", "dec_mlp_bn_beta"]
    arrays = {
        "in_x": x, "in_adj_t": adj_t, "in_mats": np.ascontiguousarray(np.stack(mats)),
        "in_blocks": np.ascontiguousarray(np.stack([bd, bdt])),
        "in_a2": np.ascontiguousarray(np.stack([asa[:d], asa[d:]], 1)),
        "in_wg": np.concatenate([a["L0_gnn_W_gcnb"], np.stack([wa[:d], wb[:d]], 1)], 1),
        "in_wr": np.ascontiguousarray(np.stack([wa[d:], wb[d:]], 1)),
        "in_vb": vb,
        "in_colv": np.ascontiguousarray(np.stack([a["L1_gnn_" + k] for k in names], 1)),
        "in_rows": np.concatenate([a["L0_gnn_b_gcnb"], a["L2_gnn_b"], a["L3_gnn_bias"], a["L0_gnn_ba"],
                                   a["L0_gnn_bb"]])[None],
    }
    nc = bacc.Bacc("TRN2", target_bir_lowering=False, num_devices=1)
    ap = {k: nc.dram_tensor(k, v.shape, mybir.dt.from_np(v.dtype), kind="ExternalInput").ap()
          for k, v in arrays.items()}
    out = nc.dram_tensor("out_0", (n, d), F32, kind="ExternalOutput").ap()
    gnn_stack(nc, ap["in_x"], ap["in_adj_t"], ap["in_mats"], ap["in_blocks"],
              {k: ap["in_" + k] for k in ("a2", "wg", "wr", "vb", "colv")}, ap["in_rows"], out)
    return run_bass_kernel_spmd(nc, [arrays], core_ids=[0]).results[0]["out_0"]
```
